# Optimizing a Trainium2 kernel written in Bass

```python
import numpy as np
import jax
import jax.numpy as jnp

def _softmax(x, axis=-1):
    return jax.nn.softmax(x, axis=axis)

def _gelu(x):
    return jax.nn.gelu(x, approximate=True)

def _silu(x):
    return jax.nn.silu(x)

def _sigmoid(x):
    return jax.nn.sigmoid(x)

def _layernorm(x, axis=-1, eps=1e-05):
    m = jnp.mean(x, axis=axis, keepdims=True)
    v = jnp.var(x, axis=axis, keepdims=True)
    return (x - m) / jnp.sqrt(v + eps)

def _scatter_add(tgt, idx, src, axis=0):
    return tgt.at[idx].add(src)

def _segment_sum(src, seg, n):
    return jax.ops.segment_sum(src, seg, n)
kernel_name = 'mk_seq_postln_d2_jaxref_r8_345579'

def setup_inputs(seed: int=0):
    np.random.seed(seed)
    _w = jnp.asarray

    def _L0_attn_setup():
        import jax, jax.numpy as jnp
        import numpy as np
        D_MODEL = 128
        N_HEADS = 16
        HEAD_DIM = D_MODEL // N_HEADS
        D_LATENT = 32
        LAMBDA_DECAY = 0.01
        TIME_STEP = 0.01
        CLAMP = 10000.0

        def _reference_tuple_inner(x, Wq, Wk, Wv, Wo, W_down_kv, W_up_k, W_up_v):
            B, S, _ = x.shape
            q = x @ Wq
            k = x @ Wk
            v = x @ Wv
            latent_kv = (k + v) @ W_down_kv
            k_rec = latent_kv @ W_up_k
            v_rec = latent_kv @ W_up_v

            def heads(t):
                return t.reshape(B, S, N_HEADS, HEAD_DIM).transpose(0, 2, 1, 3)
            qh, kh, vh = (heads(q), heads(k_rec), heads(v_rec))
            scale = 1.0 / (jnp.sqrt(jnp.float32(D_MODEL)) + 1e-08)
            scores = jnp.einsum('bhqd,bhkd->bhqk', qh, kh) * scale
            scores = jnp.clip(jnp.nan_to_num(scores, nan=-1000000000.0), -CLAMP, CLAMP)
            idx = jnp.arange(S, dtype=jnp.float32)
            decay = jnp.exp(-LAMBDA_DECAY * TIME_STEP * jnp.abs(idx[:, None] - idx[None, :]))
            scores = scores * decay[None, None, :, :]
            scores = jnp.clip(jnp.nan_to_num(scores, nan=-1000000000.0), -CLAMP, CLAMP)
            attn = jax.nn.softmax(scores, axis=-1)
            out = jnp.einsum('bhqk,bhkd->bhqd', attn, vh)
            out = out.transpose(0, 2, 1, 3).reshape(B, S, D_MODEL)
            return (out @ Wo, latent_kv)
        key = jax.random.key(seed)
        ks = jax.random.split(key, 8)
        B, S = (2, 256)

        def w(k, i, o):
            return jax.random.normal(k, (i, o), dtype=jnp.float32) * 0.02
        return {'x': jax.random.normal(ks[0], (B, S, D_MODEL), dtype=jnp.float32), 'Wq': w(ks[1], D_MODEL, D_MODEL), 'Wk': w(ks[2], D_MODEL, D_MODEL), 'Wv': w(ks[3], D_MODEL, D_MODEL), 'Wo': w(ks[4], D_MODEL, D_MODEL), 'W_down_kv': w(ks[5], D_MODEL, D_LATENT), 'W_up_k': w(ks[6], D_LATENT, D_MODEL), 'W_up_v': w(ks[7], D_LATENT, D_MODEL)}
    _L0_attn_in = _L0_attn_setup()

    def _L0_ffn_setup():
        import jax, jax.numpy as jnp
        import numpy as np
        NUM_EXPERTS = 8
        CAPACITY_FACTOR = 1.0
        key = jax.random.key(seed)
        k1, k2, k3, k4 = jax.random.split(key, 4)
        B, S, D, E, F = (8, 256, 128, NUM_EXPERTS, 512)
        x = jax.random.normal(k1, (B, S, D), dtype=jnp.float32)
        router_w = jax.random.normal(k2, (D, E), dtype=jnp.float32) * D ** (-0.5)
        w1 = jax.random.normal(k3, (E, D, F), dtype=jnp.float32) * D ** (-0.5)
        w2 = jax.random.normal(k4, (E, F, D), dtype=jnp.float32) * F ** (-0.5)
        return {'x': x, 'router_w': router_w, 'w1': w1, 'w2': w2}
    _L0_ffn_in = _L0_ffn_setup()

    def _L1_attn_setup():
        import jax, jax.numpy as jnp
        import numpy as np
        B, T, D = (2, 512, 128)
        H, DK, DV = (8, 128, 128)
        INTER = 512
        CHUNK = 128
        EPS = 1e-05

        def rmsnorm(x, w, eps=EPS):
            return x * jax.lax.rsqrt(jnp.mean(x * x, axis=-1, keepdims=True) + eps) * w

        def linear_attention(x, Wq, Wk, Wv, Wo, out_norm_w):
            b, t, d = x.shape
            n = t // CHUNK
            q = (x @ Wq).reshape(b, t, H, DK).transpose(0, 2, 1, 3)
            k = (x @ Wk).reshape(b, t, H, DK).transpose(0, 2, 1, 3)
            v = (x @ Wv).reshape(b, t, H, DV).transpose(0, 2, 1, 3)
            qc = q.reshape(b, H, n, CHUNK, DK).transpose(2, 0, 1, 3, 4)
            kc = k.reshape(b, H, n, CHUNK, DK).transpose(2, 0, 1, 3, 4)
            vc = v.reshape(b, H, n, CHUNK, DV).transpose(2, 0, 1, 3, 4)
            causal = jnp.tril(jnp.ones((CHUNK, CHUNK), dtype=bool))

            def step(S, qkv):
                qb, kb, vb = qkv
                attn = jnp.einsum('bhid,bhjd->bhij', qb, kb)
                attn = jnp.where(causal, attn, 0.0)
                o = jnp.einsum('bhij,bhjv->bhiv', attn, vb) + jnp.einsum('bhid,bhdv->bhiv', qb, S)
                S = S + jnp.einsum('bhid,bhiv->bhdv', kb, vb)
                return (S, o)
            S0 = jnp.zeros((b, H, DK, DV), x.dtype)
            _, o = jax.lax.scan(step, S0, (qc, kc, vc))
            o = o.transpose(1, 2, 0, 3, 4).reshape(b, H, t, DV)
            o = rmsnorm(o, out_norm_w)
            o = o.transpose(0, 2, 1, 3).reshape(b, t, H * DV)
            return o @ Wo
        key = jax.random.key(seed)
        ks = jax.random.split(key, 9)
        s = 0.02
        return {'hidden_states': jax.random.normal(ks[0], (B, T, D), jnp.float32), 'attn_norm_w': jnp.ones((D,), jnp.float32), 'Wq': jax.random.normal(ks[1], (D, H * DK), jnp.float32) * s, 'Wk': jax.random.normal(ks[2], (D, H * DK), jnp.float32) * s, 'Wv': jax.random.normal(ks[3], (D, H * DV), jnp.float32) * s, 'Wo': jax.random.normal(ks[4], (H * DV, D), jnp.float32) * s, 'attn_out_norm_w': jnp.ones((DV,), jnp.float32), 'mlp_norm_w': jnp.ones((D,), jnp.float32), 'Wgate': jax.random.normal(ks[5], (D, INTER), jnp.float32) * s, 'Wup': jax.random.normal(ks[6], (D, INTER), jnp.float32) * s, 'Wdown': jax.random.normal(ks[7], (INTER, D), jnp.float32) * s}
    _L1_attn_in = _L1_attn_setup()

    def _L1_ffn_setup():
        import jax, jax.numpy as jnp
        import numpy as np
        E = 8
        K = 2
        CF = 1.25
        key = jax.random.key(seed)
        kx, kr, kg, ku, kd = jax.random.split(key, 5)
        D, F = (128, 512)
        x = jax.random.normal(kx, (4, 256, D), dtype=jnp.float32)
        router_w = 0.02 * jax.random.normal(kr, (E, D), dtype=jnp.float32)
        wg = jax.random.normal(kg, (E, D, F), dtype=jnp.float32) / np.sqrt(D)
        wu = jax.random.normal(ku, (E, D, F), dtype=jnp.float32) / np.sqrt(D)
        wd = jax.random.normal(kd, (E, F, D), dtype=jnp.float32) / np.sqrt(F)
        return {'x': x, 'router_w': router_w, 'wg': wg, 'wu': wu, 'wd': wd}
    _L1_ffn_in = _L1_ffn_setup()
    _d = {'L0_attn_x': _L0_attn_in['x'], 'L0_attn_Wq': _L0_attn_in['Wq'], 'L0_attn_Wk': _L0_attn_in['Wk'], 'L0_attn_Wv': _L0_attn_in['Wv'], 'L0_attn_Wo': _L0_attn_in['Wo'], 'L0_attn_W_down_kv': _L0_attn_in['W_down_kv'], 'L0_attn_W_up_k': _L0_attn_in['W_up_k'], 'L0_attn_W_up_v': _L0_attn_in['W_up_v'], 'L0_ffn_router_w': _L0_ffn_in['router_w'], 'L0_ffn_w1': _L0_ffn_in['w1'], 'L0_ffn_w2': _L0_ffn_in['w2'], 'L1_attn_attn_norm_w': _L1_attn_in['attn_norm_w'], 'L1_attn_Wq': _L1_attn_in['Wq'], 'L1_attn_Wk': _L1_attn_in['Wk'], 'L1_attn_Wv': _L1_attn_in['Wv'], 'L1_attn_Wo': _L1_attn_in['Wo'], 'L1_attn_attn_out_norm_w': _L1_attn_in['attn_out_norm_w'], 'L1_attn_mlp_norm_w': _L1_attn_in['mlp_norm_w'], 'L1_attn_Wgate': _L1_attn_in['Wgate'], 'L1_attn_Wup': _L1_attn_in['Wup'], 'L1_attn_Wdown': _L1_attn_in['Wdown'], 'L1_ffn_router_w': _L1_ffn_in['router_w'], 'L1_ffn_wg': _L1_ffn_in['wg'], 'L1_ffn_wu': _L1_ffn_in['wu'], 'L1_ffn_wd': _L1_ffn_in['wd']}
    _x0 = _d['L0_attn_x']
    _d['L0_attn_x'] = jax.random.normal(jax.random.fold_in(jax.random.key(seed), 1), (2, 1024, 128), dtype=_x0.dtype)
    del _x0
    return _d

def reference(L0_attn_x, L0_attn_Wq, L0_attn_Wk, L0_attn_Wv, L0_attn_Wo, L0_attn_W_down_kv, L0_attn_W_up_k, L0_attn_W_up_v, L0_ffn_router_w, L0_ffn_w1, L0_ffn_w2, L1_attn_attn_norm_w, L1_attn_Wq, L1_attn_Wk, L1_attn_Wv, L1_attn_Wo, L1_attn_attn_out_norm_w, L1_attn_mlp_norm_w, L1_attn_Wgate, L1_attn_Wup, L1_attn_Wdown, L1_ffn_router_w, L1_ffn_wg, L1_ffn_wu, L1_ffn_wd):

    def _L0_attn_ref(x, Wq, Wk, Wv, Wo, W_down_kv, W_up_k, W_up_v):
        import jax, jax.numpy as jnp
        import numpy as np
        D_MODEL = 128
        N_HEADS = 16
        HEAD_DIM = D_MODEL // N_HEADS
        D_LATENT = 32
        LAMBDA_DECAY = 0.01
        TIME_STEP = 0.01
        CLAMP = 10000.0

        def _reference_tuple_inner(x, Wq, Wk, Wv, Wo, W_down_kv, W_up_k, W_up_v):
            B, S, _ = x.shape
            q = x @ Wq
            k = x @ Wk
            v = x @ Wv
            latent_kv = (k + v) @ W_down_kv
            k_rec = latent_kv @ W_up_k
            v_rec = latent_kv @ W_up_v

            def heads(t):
                return t.reshape(B, S, N_HEADS, HEAD_DIM).transpose(0, 2, 1, 3)
            qh, kh, vh = (heads(q), heads(k_rec), heads(v_rec))
            scale = 1.0 / (jnp.sqrt(jnp.float32(D_MODEL)) + 1e-08)
            scores = jnp.einsum('bhqd,bhkd->bhqk', qh, kh) * scale
            scores = jnp.clip(jnp.nan_to_num(scores, nan=-1000000000.0), -CLAMP, CLAMP)
            idx = jnp.arange(S, dtype=jnp.float32)
            decay = jnp.exp(-LAMBDA_DECAY * TIME_STEP * jnp.abs(idx[:, None] - idx[None, :]))
            scores = scores * decay[None, None, :, :]
            scores = jnp.clip(jnp.nan_to_num(scores, nan=-1000000000.0), -CLAMP, CLAMP)
            attn = jax.nn.softmax(scores, axis=-1)
            out = jnp.einsum('bhqk,bhkd->bhqd', attn, vh)
            out = out.transpose(0, 2, 1, 3).reshape(B, S, D_MODEL)
            return (out @ Wo, latent_kv)
        return _reference_tuple_inner(x, Wq, Wk, Wv, Wo, W_down_kv, W_up_k, W_up_v)[0]

    def _L0_ffn_ref(x, router_w, w1, w2):
        import jax, jax.numpy as jnp
        import numpy as np
        NUM_EXPERTS = 8
        CAPACITY_FACTOR = 1.0
        B, S, D = x.shape
        E = router_w.shape[1]
        T = B * S
        C = int(CAPACITY_FACTOR * T / E)
        x_flat = x.reshape(T, D)
        logits = x_flat @ router_w
        probs = jax.nn.softmax(logits, axis=-1)
        expert_idx = jnp.argmax(probs, axis=-1)
        gate = jnp.take_along_axis(probs, expert_idx[:, None], axis=1)[:, 0]
        onehot = jax.nn.one_hot(expert_idx, E, dtype=jnp.float32)
        pos_all = jnp.cumsum(onehot, axis=0) - 1.0
        pos = jnp.take_along_axis(pos_all, expert_idx[:, None], axis=1)[:, 0]
        pos = pos.astype(jnp.int32)
        keep = (pos < C).astype(x_flat.dtype)
        pos_c = jnp.clip(pos, 0, C - 1)
        expert_in = jnp.zeros((E, C, D), dtype=x_flat.dtype)
        expert_in = expert_in.at[expert_idx, pos_c].add(x_flat * keep[:, None])
        hidden = jax.nn.gelu(jnp.einsum('ecd,edf->ecf', expert_in, w1))
        expert_out = jnp.einsum('ecf,efd->ecd', hidden, w2)
        y = expert_out[expert_idx, pos_c] * (gate * keep)[:, None]
        return y.reshape(B, S, D)

    def _L1_attn_ref(hidden_states, attn_norm_w, Wq, Wk, Wv, Wo, attn_out_norm_w, mlp_norm_w, Wgate, Wup, Wdown):
        import jax, jax.numpy as jnp
        import numpy as np
        B, T, D = (2, 512, 128)
        H, DK, DV = (8, 128, 128)
        INTER = 512
        CHUNK = 128
        EPS = 1e-05

        def rmsnorm(x, w, eps=EPS):
            return x * jax.lax.rsqrt(jnp.mean(x * x, axis=-1, keepdims=True) + eps) * w

        def linear_attention(x, Wq, Wk, Wv, Wo, out_norm_w):
            b, t, d = x.shape
            n = t // CHUNK
            q = (x @ Wq).reshape(b, t, H, DK).transpose(0, 2, 1, 3)
            k = (x @ Wk).reshape(b, t, H, DK).transpose(0, 2, 1, 3)
            v = (x @ Wv).reshape(b, t, H, DV).transpose(0, 2, 1, 3)
            qc = q.reshape(b, H, n, CHUNK, DK).transpose(2, 0, 1, 3, 4)
            kc = k.reshape(b, H, n, CHUNK, DK).transpose(2, 0, 1, 3, 4)
            vc = v.reshape(b, H, n, CHUNK, DV).transpose(2, 0, 1, 3, 4)
            causal = jnp.tril(jnp.ones((CHUNK, CHUNK), dtype=bool))

            def step(S, qkv):
                qb, kb, vb = qkv
                attn = jnp.einsum('bhid,bhjd->bhij', qb, kb)
                attn = jnp.where(causal, attn, 0.0)
                o = jnp.einsum('bhij,bhjv->bhiv', attn, vb) + jnp.einsum('bhid,bhdv->bhiv', qb, S)
                S = S + jnp.einsum('bhid,bhiv->bhdv', kb, vb)
                return (S, o)
            S0 = jnp.zeros((b, H, DK, DV), x.dtype)
            _, o = jax.lax.scan(step, S0, (qc, kc, vc))
            o = o.transpose(1, 2, 0, 3, 4).reshape(b, H, t, DV)
            o = rmsnorm(o, out_norm_w)
            o = o.transpose(0, 2, 1, 3).reshape(b, t, H * DV)
            return o @ Wo
        x = hidden_states
        h = rmsnorm(x, attn_norm_w)
        x = x + linear_attention(h, Wq, Wk, Wv, Wo, attn_out_norm_w)
        h = rmsnorm(x, mlp_norm_w)
        x = x + jax.nn.silu(h @ Wgate) * (h @ Wup) @ Wdown
        return x

    def _L1_ffn_ref(x, router_w, wg, wu, wd):
        import jax, jax.numpy as jnp
        import numpy as np
        E = 8
        K = 2
        CF = 1.25
        B, L, D = x.shape
        xf = x.reshape(-1, D)
        N = xf.shape[0]
        capacity = max(1, int(CF * N / E))
        logits = xf @ router_w.T
        probs = jax.nn.softmax(logits, axis=-1)
        topw, topi = jax.lax.top_k(probs, K)
        topw = topw / (topw.sum(-1, keepdims=True) + 1e-06)
        fe = topi.reshape(-1)
        fw = topw.reshape(-1)
        ft = jnp.repeat(jnp.arange(N), K)
        order = jnp.lexsort((-fw, fe))
        se, sw, st = (fe[order], fw[order], ft[order])
        counts = jax.ops.segment_sum(jnp.ones_like(se), se, num_segments=E)
        starts = jnp.cumsum(counts) - counts
        rank = jnp.arange(N * K) - starts[se]
        keep = rank < capacity
        pos = jnp.where(keep, rank, capacity)
        disp = jnp.zeros((E, capacity + 1, D), x.dtype).at[se, pos].set(xf[st])
        disp = disp[:, :capacity]
        g = jnp.einsum('ecd,edf->ecf', disp, wg)
        u = jnp.einsum('ecd,edf->ecf', disp, wu)
        eo = jnp.einsum('ecf,efd->ecd', jax.nn.silu(g) * u, wd)
        gathered = eo[se, jnp.minimum(pos, capacity - 1)]
        contrib = gathered * (sw * keep.astype(x.dtype))[:, None]
        out = jnp.zeros_like(xf).at[st].add(contrib)
        return out.reshape(B, L, D)
    x = L0_attn_x
    x = _layernorm(x + _L0_attn_ref(x, L0_attn_Wq, L0_attn_Wk, L0_attn_Wv, L0_attn_Wo, L0_attn_W_down_kv, L0_attn_W_up_k, L0_attn_W_up_v), axis=-1)
    x = _layernorm(x + _L0_ffn_ref(x, L0_ffn_router_w, L0_ffn_w1, L0_ffn_w2), axis=-1)
    x = _layernorm(x + _L1_attn_ref(x, L1_attn_attn_norm_w, L1_attn_Wq, L1_attn_Wk, L1_attn_Wv, L1_attn_Wo, L1_attn_attn_out_norm_w, L1_attn_mlp_norm_w, L1_attn_Wgate, L1_attn_Wup, L1_attn_Wdown), axis=-1)
    x = _layernorm(x + _L1_ffn_ref(x, L1_ffn_router_w, L1_ffn_wg, L1_ffn_wu, L1_ffn_wd), axis=-1)
    return x

_drawn_inputs = setup_inputs


def setup_inputs(seed=0):
    import zlib

    import numpy as np

    out = dict(_drawn_inputs(seed))
    spreads = {'L1_attn_attn_norm_w': (1.0, 0.2),
     'L1_attn_attn_out_norm_w': (1.0, 0.2),
     'L1_attn_mlp_norm_w': (1.0, 0.6)}
    factors = {'L0_attn_Wq': 8.0,
     'L0_attn_Wk': 8.0,
     'L0_attn_Wv': 8.0,
     'L0_attn_Wo': 8.0,
     'L0_attn_W_down_kv': 8.0,
     'L0_attn_W_up_k': 8.0,
     'L0_attn_W_up_v': 8.0}
    for name, (base, spread) in spreads.items():
        noise = np.random.default_rng([zlib.crc32(name.encode()), seed]).standard_normal(out[name].shape)
        drawn = base * np.exp(spread * noise) if base else spread * noise
        out[name] = jnp.asarray(drawn.astype(out[name].dtype))
    for name, factor in factors.items():
        out[name] = (out[name] * factor).astype(out[name].dtype)
    return out
```

```python
from contextlib import ExitStack

import numpy as np

import concourse.bass as bass
from concourse import mybir

ALU = mybir.AluOpType
ACT = mybir.ActivationFunctionType
AX = mybir.AxisListType.X
F32 = mybir.dt.float32
BF16 = mybir.dt.bfloat16
I32 = mybir.dt.int32

P = 128
B, S, D = 2, 1024, 128
T = B * S
NT = T // P
SB = S // P
EPS = 1e-5

H0, HD = 16, 8
GH = 4
NG = B * H0 // GH
LAT = 32
SCALE0 = 1.0 / (np.sqrt(np.float32(D)) + np.float32(1e-8))
CLAMP = 10000.0
DECAY = 0.01 * 0.01
NPART = 3
KR = NPART * NPART * HD
KX = KR + NPART


def host_constants():
    i = np.arange(S, dtype=np.float32)
    p = np.arange(P)
    c = np.float32(-DECAY)
    ramp = np.stack([np.exp(c * i), np.exp(-c * i)]).astype(np.float32)
    u = np.arange(2 * S - P)[None, :] - (S - P) - p[:, None]
    bound = (np.float32(CLAMP) * np.exp(-c * u.astype(np.float32))).astype(np.float32)
    rest = np.where(u > 0, np.exp(2 * c * u.astype(np.float32)), 1.0).astype(np.float32)
    ident = np.eye(P, dtype=np.float32)
    before = (p[:, None] < p[None, :]).astype(np.float32)
    return {
        "c_ramp": np.ascontiguousarray(np.broadcast_to(ramp[None], (P, 2, S))),
        "c_bound": bound, "c_rest": rest, "c_ident": ident, "c_before": before,
        "c_causal": (p[:, None] <= p[None, :]).astype(np.float32),
        "c_order": np.ascontiguousarray(np.broadcast_to(np.arange(E, 0, -1, dtype=np.float32), (P, E))),
        "c_number": np.ascontiguousarray(np.broadcast_to(np.arange(E, dtype=np.float32), (P, E))),
    }


def attention_setup(nc, mem, dram, io):
    with ExitStack() as ctx:
        sb, ps, sem = tools(nc, ctx)
        wq, wk, wv = (sb(n, [P, D]) for n in ("wq", "wk", "wv"))
        wd, wu = sb("wd", [P, LAT]), sb("wu", [LAT, 2, D])
        wkv, wkv_t, l_t, w_rec = sb("wkv", [P, D]), sb("wkv_t", [P, D]), sb("l_t", [LAT, P]), sb("w_rec", [P, 2, D])
        ramp = sb("ramp", [P, 2, S])
        raw = sb("raw", [P, 2, T])
        full = sb("full", [P, 2, T])
        rest1, rest2 = sb("rest1", [P, 2, T]), None
        parts = sb("parts", [P, 2, NPART, T], BF16)
        bank = [ps(f"setup{i}", [P, 512]) for i in range(8)]
        loaded_x, loaded_w = sem("loaded_x"), sem("loaded_w")
        transposed, copied, folded, fold_copied = sem("transposed"), sem("copied"), sem("folded"), sem("fold_copied")
        kv_summed, projected, taken = sem("kv_summed"), sem("projected"), sem("taken")
        scaled, part0, left1, part1, part2, stored = (sem(n) for n in ("scaled", "part0", "left1", "part1", "part2", "stored"))
        x_tok, x_t, ident, v_src = mem["x_tok"], mem["x_t"], mem["ident"], mem["v_src"]
        squared, summed, judged, ones_in = sem("squared"), sem("summed"), sem("judged"), sem("ones_in")
        ones, limits = sb("ones", [P, 1]), sb("limits", [1, 8])
        block = ctx.enter_context(nc.Block())

        @block.sync
        def _(sp):
            sp.dma_start(ident[:, :], io["c_ident"]).then_inc(loaded_x, 16)
            sp.dma_start(x_tok[:, :, :], io["L0_attn_x"].rearrange("b (t p) d -> p (b t) d", p=P)).then_inc(loaded_x, 16)
            for dst, name in ((wq, "Wq"), (wk, "Wk"), (wv, "Wv"), (wd, "W_down_kv")):
                sp.dma_start(dst[:, :], io["L0_attn_" + name]).then_inc(loaded_w, 16)
            sp.dma_start(wu[:, 0, :], io["L0_attn_W_up_k"]).then_inc(loaded_w, 16)
            sp.dma_start(wu[:, 1, :], io["L0_attn_W_up_v"]).then_inc(loaded_w, 16)
            sp.dma_start(ramp[:, :, :], io["c_ramp"]).then_inc(loaded_w, 16)
            sp.dma_start(mem["rest"][:, :], io["c_rest"]).then_inc(loaded_w, 16)
            for n in range(4):
                sp.wait_ge(part2, n + 1)
                for g in range(NG // B):
                    for b in range(B):
                        for k in range(NPART):
                            sp.dma_start(dram["parts"][n % 2, n // 2, b * (NG // B) + g, :, k, :, :],
                                         parts[32 * g:32 * g + 32, n % 2, k, b * S:(b + 1) * S]).then_inc(stored, 16)
            sp.wait_ge(stored, 4 * NG * NPART * 16)
            sp.wait_ge(loaded_w, 8 * 16)

        @block.tensor
        def _(pe):
            pe.wait_ge(loaded_x, 32)
            for t in range(NT):
                last = pe.transpose(bank[t // 4][:, t % 4 * P:t % 4 * P + P], x_tok[:, t, :], ident[:, :])
                if t % 4 == 3:
                    last.then_inc(transposed, 1)
            pe.wait_ge(kv_summed, 1)
            pe.transpose(bank[4][:, 0:P], wkv[:, :], ident[:, :]).then_inc(folded, 1)
            pe.wait_ge(fold_copied, 1)
            pe.matmul(bank[5][0:LAT, 0:P], wd[:, :], wkv_t[:, :], start=True, stop=True).then_inc(folded, 1)
            pe.wait_ge(fold_copied, 2)
            pe.matmul(bank[6][:, 0:2 * D], l_t[:, :], wu[:, :, :], start=True, stop=True).then_inc(folded, 1)
            for n in range(2):
                if n == 1:
                    pe.wait_ge(fold_copied, 3)
                for c in range(4):
                    if n == 0:
                        pe.wait_ge(copied, 4)
                    w = wq[:, :] if n == 0 else w_rec[:, 0, :]
                    pe.matmul(bank[4 * n + c][:, :], w, x_t[:, c * 512:(c + 1) * 512],
                              start=True, stop=True).then_inc(projected, 1)
            for t in range(NT):
                if t % 4 == 0:
                    pe.wait_ge(taken, t // 4 + 1)
                last = pe.matmul(bank[t // 4][:, t % 4 * P:t % 4 * P + P], x_t[:, t * P:(t + 1) * P],
                                 w_rec[:, 1, :], start=True, stop=True)
                if t % 4 == 3:
                    last.then_inc(projected, 1)
            pe.wait_ge(ones_in, 1)
            pe.wait_ge(taken, 9)
            for n in range(2):
                pe.wait_ge(squared, n + 1)
                for c in range(4):
                    last = pe.matmul(bank[4 * n + c][0:1, :], ones[:, :], full[:, n, c * 512:(c + 1) * 512], start=True, stop=True)
                last.then_inc(summed, 1)

        @block.scalar
        def _(act):
            for c in range(4):
                act.wait_ge(transposed, c + 1)
                act.copy(x_t[:, c * 512:(c + 1) * 512], bank[c][:, :]).then_inc(copied, 1)
            for n in range(2):
                for c in range(4):
                    act.wait_ge(projected, 4 * n + c + 1)
                    act.activation(raw[:, n, c * 512:(c + 1) * 512], bank[4 * n + c][:, :], ACT.Copy,
                                   scale=float(SCALE0) if n == 0 else 1.0).then_inc(taken, 1)
            for t in range(NT):
                if t % 4 == 0:
                    act.wait_ge(projected, 8 + t // 4 + 1)
                last = act.copy(
                    v_src[:, t // SB * (NG // B):(t // SB + 1) * (NG // B), t % SB, :],
                    bank[t // 4][:, t % 4 * P:t % 4 * P + P].rearrange("p (g r) -> p g r", r=GH * HD))
            last.then_inc(taken, 1)
            for n in range(2):
                act.wait_ge(taken, 4 * (n + 1))
                act.activation(full[:, n, :], raw[:, n, :], ACT.Square).then_inc(squared, 1)
            for n in range(4):
                act.wait_ge(scaled, 2 * n + 2)
                if n >= 2:
                    act.wait_ge(stored, (n - 1) * NG * NPART * 16)
                act.copy(parts[:, n % 2, 0, :], full[:, n % 2, :]).then_inc(part0, 1)
                act.wait_ge(left1, n + 1)
                act.copy(parts[:, n % 2, 1, :], rest1[:, n % 2, :]).then_inc(part1, 1)

        @block.vector
        def _(dve):
            dve.memset(ones[:, :], 1.0).then_inc(ones_in, 1)
            dve.wait_ge(loaded_w, 8 * 16)
            dve.tensor_tensor(wkv[:, :], wk[:, :], wv[:, :], ALU.add).then_inc(kv_summed, 1)
            dve.wait_ge(folded, 1)
            dve.tensor_copy(wkv_t[:, :], bank[4][:, 0:P]).then_inc(fold_copied, 1)
            dve.wait_ge(folded, 2)
            dve.tensor_copy(l_t[:, :], bank[5][0:LAT, 0:P]).then_inc(fold_copied, 1)
            dve.wait_ge(folded, 3)
            dve.tensor_copy(w_rec[:, :, :], bank[6][:, 0:2 * D].rearrange("p (a b) -> p a b", a=2)).then_inc(fold_copied, 1)

            def judge():
                for n in range(2):
                    dve.wait_ge(summed, n + 1)
                    for c in range(4):
                        dve.tensor_reduce(limits[:, c:c + 1], bank[4 * n + c][0:1, :], AX, ALU.max).then_inc(judged, 1)
                    dve.wait_ge(judged, 10 * n + 4)
                    dve.tensor_reduce(limits[:, 4 + n:5 + n], limits[:, 0:4], AX, ALU.max).then_inc(judged, 1)
                    for c in range(4):
                        if c == 0:
                            dve.wait_ge(judged, 10 * n + 5)
                        dve.tensor_reduce(limits[:, c:c + 1], bank[4 * n + c][0:1, :], AX, ALU.add).then_inc(judged, 1)
                    dve.wait_ge(judged, 10 * n + 9)
                    dve.tensor_reduce(limits[:, 6 + n:7 + n], limits[:, 0:4], AX, ALU.add).then_inc(judged, 1)
                    dve.wait_ge(judged, 10 * n + 10)
                dve.tensor_tensor(limits[:, 0:1], limits[:, 4:5], limits[:, 5:6], ALU.mult).then_inc(judged, 1)
                dve.tensor_tensor(limits[:, 1:2], limits[:, 6:7], limits[:, 7:8], ALU.mult).then_inc(judged, 1)
                dve.wait_ge(judged, 22)
                dve.tensor_scalar(limits[:, 2:3], limits[:, 0:1], 0.9 * CLAMP * CLAMP, None, ALU.is_lt).then_inc(judged, 1)
                dve.tensor_scalar(limits[:, 3:4], limits[:, 1:2], 1e30, None, ALU.is_lt).then_inc(judged, 1)
                dve.wait_ge(judged, 24)
                dve.tensor_tensor(limits[:, 4:5], limits[:, 2:3], limits[:, 3:4], ALU.mult).then_inc(judged, 1)
                dve.wait_ge(judged, 25)
                dve.tensor_scalar(mem["clamps"][:, :], limits[:, 4:5], -1.0, 1.0, ALU.mult, ALU.add).then_inc(judged, 1)

            def first_left(n):
                dve.wait_ge(taken, 4 * (n % 2 + 1))
                dve.wait_ge(summed, n % 2 + 1)
                if n >= 2:
                    dve.wait_ge(part0, n - 1)
                    dve.wait_ge(left1, n - 1)
                for b in range(B):
                    dve.tensor_tensor(full[:, n % 2, b * S:(b + 1) * S], raw[:, n % 2, b * S:(b + 1) * S],
                                      ramp[:, (n // 2 + n) % 2, :], ALU.mult).then_inc(scaled, 1)
                dve.wait_ge(part0, n + 1)
                if n >= 2:
                    dve.wait_ge(part1, n - 1)
                    dve.wait_ge(part2, n - 1)
                dve.tensor_tensor(rest1[:, n % 2, :], full[:, n % 2, :], parts[:, n % 2, 0, :],
                                  ALU.subtract).then_inc(left1, 1)

            def second_left(n):
                dve.wait_ge(part1, n + 1)
                dve.tensor_tensor(parts[:, n % 2, 2, :], rest1[:, n % 2, :], parts[:, n % 2, 1, :],
                                  ALU.subtract).then_inc(part2, 1)

            for n in range(4):
                first_left(n)
                if n:
                    second_left(n - 1)
            second_left(3)
            judge()


def tools(nc, ctx, last=False):
    stage = nc.next_id()
    taken = []

    def zero():
        for s in taken:
            nc.sync.sem_clear(s)

    if not last:
        ctx.callback(zero)

    def sb(name, shape, dt=F32):
        return ctx.enter_context(nc.sbuf_tensor(f"{name}_{stage}", shape, dt))

    def ps(name, shape, dt=F32):
        return ctx.enter_context(nc.psum_tensor(f"{name}_{stage}", shape, dt))

    def sem(name):
        taken.append(ctx.enter_context(nc.semaphore(f"{name}_{stage}")))
        return taken[-1]

    return sb, ps, sem


LOWEST = -3.0e38


class Group:

    def __init__(self, k, turn=0):
        self.k, self.turn = k, turn
        self.third = k % 3
        self.n = k + 3 * turn
        self.round = k // 3 + turn


def attention_scores(nc, mem, dram):
    with ExitStack() as ctx:
        sb, ps, sem = tools(nc, ctx)
        NU = SB * GH + SB // 2
        HALF = S // 2
        NA = SB * GH * 2
        stack = [sb(f"stack{i}", [P, 2, 2, GH, S], BF16) for i in range(3)]
        v_aug = [sb(f"v_aug{i}", [P, SB, GH, 32]) for i in range(3)]
        prob = [sb(f"prob{i}", [P, GH, S]) for i in range(2)]
        prob_late = [sb(f"prob_late{i}", [P, 2, GH, P]) for i in range(2)]
        junk = sb("junk", [P, 2, HALF], BF16)
        top = sb("top", [P, 2, GH, SB, 2])
        neg = sb("neg", [P, GH, SB])
        neg_left = sb("neg_left", [P, GH, SB])
        neg_parts = sb("neg_parts", [P, GH, NPART, SB], BF16)
        ident_b = sb("ident_b", [P, P], BF16)
        neg_rows = sb("neg_rows", [GH * NPART * SB, P], BF16)
        o_t = sb("o_t", [P, S])
        recip = sb("recip", [P, SB, GH])
        score = [ps(f"score{i}", [P, S]) for i in range(2)]
        out_ps = ps("out_ps", [P, S])
        row = ps("row", [P, 2, HALF])
        rest, ident, v_src, o_src = mem["rest"], mem["ident"], mem["v_src"], mem["o_src"]

        rows_set, values_set, ident_cast = sem("rows_set"), sem("values_set"), sem("ident_cast")
        dve_passed, pool_passed = sem("dve_passed"), sem("pool_passed")
        stacks_in = [sem(f"stacks_in{i}") for i in range(3)]
        v_staged = sem("v_staged")
        row_ready, row_done = sem("row_ready"), sem("row_done")
        neg_chain, neg_turned, neg_copied = sem("neg_chain"), sem("neg_turned"), sem("neg_copied")
        neg_in = [sem(f"neg_in{i}") for i in range(3)]
        scored, exped, masked, mask_late = sem("scored"), sem("exped"), sem("masked"), sem("mask_late")
        weighted, o_copied, o_turned, o_inv, o_done = sem("weighted"), sem("o_copied"), sem("o_turned"), sem("o_inv"), sem("o_done")
        block = ctx.enter_context(nc.Block())

        units = []
        for pair in range(SB // 2):
            units += [("tile", 2 * pair + k, h) for k in range(2) for h in range(GH)]
            units += [("late", pair, 0)]
        unit_at = {u: n for n, u in enumerate(units)}

        def first(g):
            return isinstance(g.n, int) and g.n == 0

        def run_groups(eng, body):
            body(None, Group(0), None)
            body(Group(0), Group(1), None)
            with eng.Fori(0, (NG - 2) // 3) as turn:
                for k in (1, 2, 3):
                    body(Group(k, turn), Group(k + 1, turn), Group(k - 1, turn))
            body(Group(NG - 1), None, Group(NG - 2))

        LOADS, NEGS = 2 * GH * (NPART + 1), 2 * GH

        product_order = []
        for n, (kind, tile, h) in enumerate(units):
            if kind == "tile" and h == GH - 1 and tile:
                product_order.append(("tile", tile - 1))
            if kind == "tile" and h == 1 and tile % 2 == 0 and tile:
                product_order.append(("late", tile // 2 - 1))
        product_order += [("tile", SB - 1), ("late", SB // 2 - 1)]
        NW = len(product_order)

        def used_tile(g, tile):
            if tile >= 2:
                return g.n * NW + product_order.index(("tile", tile - 2)) + 1
            return (g.n - 1) * NW + product_order.index(("tile", SB - 2 + tile)) + 1

        def used_late(g, pair):
            if pair >= 2:
                return g.n * NW + product_order.index(("late", pair - 2)) + 1
            return (g.n - 1) * NW + product_order.index(("late", SB // 2 - 2 + pair)) + 1

        @block.sync
        def _(sp):
            with sp.If(sp.value_load(mem["clamps"][0:1, 0:1], min_val=0, max_val=1) == 0):
                def load(g):
                    to = stack[g.third]
                    for half in range(2):
                        for h in range(GH):
                            for a in range(NPART):
                                rows = slice(a * NPART * HD, (a + 1) * NPART * HD)
                                sp.dma_start(to[rows, half, 0, h, :],
                                             dram["parts"][0, half, g.n, h, a, :, :].unsqueeze(0).to_broadcast([NPART, HD, S])
                                             ).then_inc(stacks_in[g.third], 16)
                            key = dram["parts"][1, half, g.n, h, :, :, :].rearrange("k r t -> (k r) t")
                            sp.dma_start(to[0:KR, half, 1, h, :],
                                         key.unsqueeze(0).to_broadcast([NPART, NPART * HD, S])).then_inc(stacks_in[g.third], 16)

                def store_neg(g):
                    sp.wait_ge(neg_copied, g.n + 1)
                    for h in range(GH):
                        for half in range(2):
                            sp.dma_start(stack[g.third][KR:KR + NPART, half, 0, h, :].rearrange("k (t c) -> k t c", c=P),
                                         neg_rows[h * NPART * SB:(h + 1) * NPART * SB, :]
                                         ).then_inc(neg_in[g.third], 16)

                sp.wait_ge(rows_set, 3)
                load(Group(0))
                load(Group(1))
                store_neg(Group(0))
                load(Group(2))
                store_neg(Group(1))

                def body(g, ahead):
                    sp.wait_ge(scored, g.n * NU)
                    load(ahead)
                    store_neg(Group(g.k + 1, g.turn))

                with sp.Fori(0, (NG - 2) // 3 - 1) as turn:
                    for k in (1, 2, 3):
                        body(Group(k, turn), Group(k + 2, turn))
                body(Group(NG - 4), Group(NG - 2))
                body(Group(NG - 3), Group(NG - 1))
                store_neg(Group(NG - 1))
                for i in range(3):
                    sp.wait_ge(neg_in[i], (NG - 1 - i + 3) // 3 * NEGS * 16)

        @block.tensor
        def _(pe):
            with pe.If(pe.value_load(mem["clamps"][0:1, 0:1], min_val=0, max_val=1) == 0):
                def row_unit(g, n):
                    tile, h, part = n // (2 * GH), n // 2 % GH, n % 2
                    if n == 0:
                        pe.wait_ge(stacks_in[g.third], (g.round + 1) * LOADS * 16)
                        if not first(g):
                            pe.wait_ge(neg_copied, g.n)
                    if not (first(g) and n < 2):
                        pe.wait_ge(row_done, g.n * NA + n - 1)
                    pe.matmul(row[:, n % 2, :], stack[g.third][0:KR, 0, 0, h, tile * P:(tile + 1) * P],
                              stack[g.third][0:KR, 0, 1, h, part * HALF:(part + 1) * HALF],
                              start=True, stop=True).then_inc(row_ready, 1)

                def turn_neg(g):
                    pe.wait_ge(neg_chain, 6 * (g.n + 1))
                    pe.transpose(row[0:GH * NPART * SB, 0, 0:P // 2].bitcast(BF16),
                                 neg_parts[:, :, :, :], ident_b[:, :]).then_inc(neg_turned, 1)

                def column_unit(g, n):
                    kind, tile, h = units[n]
                    if n == 0:
                        pe.wait_ge(neg_in[g.third], (g.round + 1) * NEGS * 16)
                    if not (first(g) and n < 2):
                        pe.wait_ge(exped, g.n * NU + n - 1)
                    out = score[n % 2]
                    if kind == "tile":
                        at = tile * P
                        pieces = [(1, a, min(b, at)) for a, b in ((0, HALF), (HALF, S)) if a < at]
                        pieces += [(0, max(a, at), b) for a, b in ((0, HALF), (HALF, S)) if b > at]
                        for half, a, b in pieces:
                            last = pe.matmul(out[:, a:b], stack[g.third][0:KX, half, 1, h, at:at + P],
                                             stack[g.third][0:KX, half, 0, h, a:b], start=True, stop=True)
                    else:
                        for k in range(2):
                            at = (2 * tile + k) * P
                            for hh in range(GH):
                                c = (k * GH + hh) * P
                                last = pe.matmul(out[:, c:c + P], stack[g.third][0:KX, 1, 1, hh, at:at + P],
                                                 stack[g.third][0:KX, 1, 0, hh, at:at + P], start=True, stop=True)
                    last.then_inc(scored, 1)

                def weigh(g, tile):
                    if tile == 0:
                        pe.wait_ge(v_staged, g.n + 1)
                        if not first(g):
                            pe.wait_ge(o_done, g.n)
                    pe.wait_ge(masked, g.n * SB + tile + 1)
                    for part in range(2):
                        for h in range(GH):
                            last = pe.matmul(out_ps[32 * h:32 * h + 32, part * HALF:(part + 1) * HALF],
                                             v_aug[g.third][:, tile, h, :], prob[tile % 2][:, h, part * HALF:(part + 1) * HALF],
                                             start=(tile == 0), stop=False, skip_group_check=True)
                    last.then_inc(weighted, 1)

                def weigh_late(g, pair):
                    pe.wait_ge(mask_late, g.n * (SB // 2) + pair + 1)
                    for k in range(2):
                        tile = 2 * pair + k
                        for h in range(GH):
                            last = pe.matmul(out_ps[32 * h:32 * h + 32, tile * P:(tile + 1) * P],
                                             v_aug[g.third][:, tile, h, :], prob_late[pair % 2][:, k, h, :],
                                             start=False, stop=(pair == SB // 2 - 1), skip_group_check=True)
                    last.then_inc(weighted, 1)

                def turn_out(g):
                    pe.wait_ge(o_copied, g.n + 1)
                    for t in range(SB):
                        last = pe.transpose(out_ps[:, t * P:(t + 1) * P], o_t[:, t * P:(t + 1) * P], ident[:, :])
                    last.then_inc(o_turned, 1)

                def body(g, nxt, before):
                    if g is None:
                        for n in range(NA):
                            row_unit(nxt, n)
                        turn_neg(nxt)
                        return
                    rows = list(range(NA)) if nxt is not None else []
                    for n, (kind, tile, h) in enumerate(units):
                        column_unit(g, n)
                        if kind == "tile":
                            for r in rows[:2]:
                                row_unit(nxt, r)
                            rows = rows[2:]
                        if n == 3 and not first(g):
                            turn_out(before)
                        if kind == "tile" and h == GH - 1 and tile:
                            weigh(g, tile - 1)
                        if kind == "tile" and h == 1 and tile % 2 == 0 and tile:
                            weigh_late(g, tile // 2 - 1)
                    if nxt is not None:
                        turn_neg(nxt)
                    weigh(g, SB - 1)
                    weigh_late(g, SB // 2 - 1)

                pe.wait_ge(ident_cast, 1)
                pe.wait_ge(values_set, 6)
                run_groups(pe, body)
                turn_out(Group(NG - 1))

        @block.scalar
        def _(act):
            with act.If(act.value_load(mem["clamps"][0:1, 0:1], min_val=0, max_val=1) == 0):
                def finish(g):
                    act.wait_ge(weighted, (g.n + 1) * (SB + SB // 2))
                    if not first(g):
                        act.wait_ge(o_turned, g.n)
                    act.copy(o_t[:, :], out_ps[:, :]).then_inc(o_copied, 1)

                def body(g, nxt, before):
                    if g is None:
                        return
                    for n, (kind, tile, h) in enumerate(units):
                        if n == 3 and not first(g):
                            finish(before)
                        act.wait_ge(scored, g.n * NU + n + 1)
                        if kind == "tile":
                            if h == 0 and not (first(g) and tile < 2):
                                act.wait_ge(weighted, used_tile(g, tile))
                            act.activation(prob[tile % 2][:, h, :], score[n % 2][:, :], ACT.Exp).then_inc(exped, 1)
                        else:
                            if not (first(g) and tile < 2):
                                act.wait_ge(weighted, used_late(g, tile))
                            act.activation(prob_late[tile % 2][:, :, :, :],
                                           score[n % 2][:, :].rearrange("p (k h c) -> p k h c", k=2, h=GH),
                                           ACT.Exp).then_inc(exped, 1)

                run_groups(act, body)
                finish(Group(NG - 1))

        @block.gpsimd
        def _(pool):
            with pool.If(pool.value_load(mem["clamps"][0:1, 0:1], min_val=0, max_val=1) == 0):
                def stage(g):
                    if not (isinstance(g.n, int) and g.n < 2):
                        pool.wait_ge(weighted, (g.n - 1) * NW)
                    pool.tensor_copy(v_aug[g.third][:, :, :, 0:HD],
                                     v_src[:, g.n, :, :].rearrange("p t (h r) -> p t h r", r=HD)).then_inc(v_staged, 1)

                def body(g, nxt, before):
                    if g is None:
                        stage(nxt)
                        return
                    if nxt is not None:
                        stage(nxt)
                    for n, (kind, tile, h) in enumerate(units):
                        if kind == "tile" and h == GH - 1:
                            at = tile * P
                            pool.wait_ge(exped, g.n * NU + n + 1)
                            pool.sem_inc(pool_passed, 1)
                            pool.affine_select(out=prob[tile % 2][:, :, at:at + P], in_=prob[tile % 2][:, :, at:at + P],
                                               compare_op=ALU.is_ge, fill=0.0, base=0, pattern=[[0, GH], [1, P]],
                                               channel_multiplier=-1).then_inc(masked, 1)
                        if kind == "late":
                            pool.wait_ge(exped, g.n * NU + n + 1)
                            pool.sem_inc(pool_passed, 1)
                            pool.affine_select(out=prob_late[tile % 2][:, :, :, :], in_=prob_late[tile % 2][:, :, :, :],
                                               compare_op=ALU.is_gt, fill=0.0, base=0, pattern=[[0, 2 * GH], [-1, P]],
                                               channel_multiplier=1).then_inc(mask_late, 1)

                for v in v_aug:
                    pool.memset(v[:, :, :, HD + 1:32], 0.0).then_inc(values_set, 1)
                    pool.memset(v[:, :, :, HD:HD + 1], 1.0).then_inc(values_set, 1)
                pool.tensor_copy(ident_b[:, :], ident[:, :]).then_inc(ident_cast, 1)
                run_groups(pool, body)

        @block.vector
        def _(dve):
            with dve.If(dve.value_load(mem["clamps"][0:1, 0:1], min_val=0, max_val=1) == 0):
                def row_unit(g, n):
                    tile, h, part = n // (2 * GH), n // 2 % GH, n % 2
                    dve.wait_ge(row_ready, g.n * NA + n + 1)
                    if not (first(g) and n < 2):
                        dve.wait_ge(row_done, g.n * NA + n - 1)
                    at = S - P - tile * P + part * HALF
                    dve.sem_inc(dve_passed, 1)
                    dve.tensor_tensor_reduce(junk[:, n % 2, :], row[:, n % 2, :], rest[:, at:at + HALF], 1.0, LOWEST,
                                             ALU.mult, ALU.max, top[:, 0, h, tile, part:part + 1]).then_inc(row_done, 1)

                def negate(g):
                    base = g.n * 6
                    dve.wait_ge(row_done, (g.n + 1) * NA)
                    dve.tensor_reduce(top[:, 1, :, :, 0], top[:, 0, :, :, :], AX, ALU.max).then_inc(neg_chain, 1)
                    dve.wait_ge(neg_chain, base + 1)
                    dve.tensor_scalar(neg[:, :, :], top[:, 1, :, :, 0], -1.0, None, ALU.mult).then_inc(neg_chain, 1)
                    dve.wait_ge(neg_chain, base + 2)
                    if not first(g):
                        dve.wait_ge(neg_turned, g.n)
                    dve.tensor_copy(neg_parts[:, :, 0, :], neg[:, :, :]).then_inc(neg_chain, 1)
                    dve.wait_ge(neg_chain, base + 3)
                    dve.tensor_tensor(neg_left[:, :, :], neg[:, :, :], neg_parts[:, :, 0, :], ALU.subtract).then_inc(neg_chain, 1)
                    dve.wait_ge(neg_chain, base + 4)
                    dve.tensor_copy(neg_parts[:, :, 1, :], neg_left[:, :, :]).then_inc(neg_chain, 1)
                    dve.wait_ge(neg_chain, base + 5)
                    dve.tensor_tensor(neg_parts[:, :, 2, :], neg_left[:, :, :], neg_parts[:, :, 1, :], ALU.subtract).then_inc(neg_chain, 1)
                    dve.wait_ge(neg_turned, g.n + 1)
                    if not first(g):
                        prev = Group(g.k - 1, g.turn)
                        dve.wait_ge(neg_in[prev.third], (prev.round + 1) * NEGS * 16)
                    dve.tensor_copy(neg_rows[:, :], row[0:GH * NPART * SB, 0, 0:P // 2].bitcast(BF16)).then_inc(neg_copied, 1)

                def finish(g):
                    dve.wait_ge(o_turned, g.n + 1)
                    out = out_ps[:, :].rearrange("p (t h r) -> p t h r", t=SB, h=GH)
                    if not first(g):
                        dve.wait_ge(o_done, g.n)
                    dve.reciprocal(recip[:, :, :], out[:, :, :, HD]).then_inc(o_inv, 1)
                    dve.wait_ge(o_inv, g.n + 1)
                    dve.tensor_tensor(o_src[:, g.n, :, :].rearrange("p t (h r) -> p t h r", r=HD), out[:, :, :, 0:HD],
                                      recip[:, :, :].unsqueeze(3).to_broadcast([P, SB, GH, HD]), ALU.mult).then_inc(o_done, 1)

                def body(g, nxt, before):
                    if nxt is not None:
                        for n in range(NA):
                            row_unit(nxt, n)
                            if n == 11 and g is not None and not first(g):
                                finish(before)
                        negate(nxt)
                    else:
                        finish(before)

                for keys in stack:
                    dve.memset(keys[64:P, :, 1, :, :], 1.0).then_inc(rows_set, 1)
                run_groups(dve, body)
                finish(Group(NG - 1))


def attention_general(nc, mem, dram, io):
    with ExitStack() as ctx:
        sb, ps, sem = tools(nc, ctx)
        queries, keys = sb("queries", [P, S], BF16), sb("keys", [P, S], BF16)
        bound, low, rest = sb("bound", [P, 2 * S - P]), sb("low", [P, 2 * S - P]), mem["rest"]
        raw, clean, number = sb("raw", [P, S]), sb("clean", [P, S]), sb("number", [P, S], I32)
        prob, prob_t = sb("prob", [P, S]), sb("prob_t", [P, S])
        top, neg, denom, inv = (sb(n, [P, 1]) for n in ("top", "neg", "denom", "inv"))
        score, turned_ps, out_ps = ps("score", [P, S]), ps("turned", [P, S]), ps("out", [P, HD])
        loaded, tables, set_up, scored, steps, maxed, exped, turned, t_copied, weighted, done = (
            sem(n) for n in ("loaded", "tables", "set_up", "scored", "steps", "maxed", "exped", "turned", "t_copied",
                             "weighted", "done"))
        ident, v_src, o_src = mem["ident"], mem["v_src"], mem["o_src"]
        passed = sem("passed")
        block = ctx.enter_context(nc.Block())
        STEPS = 9

        def general(eng):
            return eng.If(eng.value_load(mem["clamps"][0:1, 0:1], min_val=0, max_val=1) == 1)

        def head_tiles(eng, body):
            with eng.Fori(0, NG) as g:
                with eng.Fori(0, GH) as h:
                    with eng.Fori(0, SB) as shift:
                        body(g, h, shift, g * (GH * SB) + h * SB + shift)

        def hold(eng, semaphore, value):
            eng.wait_ge(semaphore, value)
            eng.sem_inc(passed, 1)

        parts = dram["parts"]
        v_heads = v_src[:, :, :, :].rearrange("p g t (h r) -> p g h t r", r=HD)
        o_heads = o_src[:, :, :, :].rearrange("p g t (h r) -> p g h t r", r=HD)

        @block.sync
        def _(sp):
            with general(sp):
                sp.dma_start(bound[:, :], io["c_bound"]).then_inc(tables, 16)
                sp.wait_ge(tables, 16)
                with sp.Fori(0, NG) as g:
                  with sp.Fori(0, GH) as h:
                    hold(sp, done, g * (GH * SB) + h * SB + 1)
                    for a in range(NPART):
                        sp.dma_start(queries[a * NPART * HD:(a + 1) * NPART * HD, :],
                                     parts[0, 0, g, h, a, :, :].unsqueeze(0).to_broadcast([NPART, HD, S])).then_inc(loaded, 16)
                    sp.dma_start(keys[0:KR, :], parts[1, 0, g, h, :, :, :].rearrange("k r t -> (k r) t")
                                 .unsqueeze(0).to_broadcast([NPART, NPART * HD, S])).then_inc(loaded, 16)

        @block.tensor
        def _(pe):
            def body(g, h, shift, n):
                hold(pe, loaded, g * (GH * 16 * (NPART + 1)) + h * (16 * (NPART + 1)) + 16 * (NPART + 1))
                hold(pe, done, n + 1)
                for c in range(2):
                    last = pe.matmul(score[:, c * 512:(c + 1) * 512],
                                     queries[0:KR, bass.ds((SB - 1) * P - shift * P, P)],
                                     keys[0:KR, c * 512:(c + 1) * 512], start=True, stop=True)
                last.then_inc(scored, 1)
                hold(pe, exped, n + 1)
                for t in range(SB):
                    last = pe.transpose(turned_ps[:, t * P:(t + 1) * P], prob[:, t * P:(t + 1) * P], ident[:, :])
                last.then_inc(turned, 1)
                hold(pe, t_copied, n + 1)
                for t in range(SB):
                    last = pe.matmul(out_ps[:, :], prob_t[:, t * P:(t + 1) * P], v_heads[:, g, h, t, :],
                                     start=(t == 0), stop=(t == SB - 1))
                last.then_inc(weighted, 1)

            with general(pe):
                pe.wait_ge(tables, 16)
                head_tiles(pe, body)

        @block.scalar
        def _(act):
            def body(g, h, shift, n):
                hold(act, maxed, n + 1)
                act.activation(prob[:, :], clean[:, :], ACT.Exp, bias=neg[:, 0:1], accum_out=denom[:, 0:1]).then_inc(exped, 1)

            with general(act):
                head_tiles(act, body)

        @block.vector
        def _(dve):
            def body(g, h, shift, n):
                base = n * STEPS

                def step(k, ins):
                    ins.then_inc(steps, 1)
                    hold(dve, steps, base + k)

                hold(dve, scored, n + 1)
                dve.tensor_copy(raw[:, :], score[:, :]).then_inc(steps, 1)

                def at(table):
                    return table[:, bass.ds(shift * P, S)]

                dve.tensor_copy(clean[:, :], at(low)).then_inc(steps, 1)
                hold(dve, steps, base + 2)
                step(3, dve.tensor_tensor(number[:, :], raw[:, :], raw[:, :], ALU.is_equal))
                step(4, dve.copy_predicated(clean[:, :], number[:, :], raw[:, :]))
                step(5, dve.tensor_tensor(clean[:, :], clean[:, :], at(bound), ALU.min))
                step(6, dve.tensor_tensor(clean[:, :], clean[:, :], at(low), ALU.max))
                step(7, dve.tensor_tensor(clean[:, :], clean[:, :], at(rest), ALU.mult))
                step(8, dve.tensor_reduce(top[:, :], clean[:, :], AX, ALU.max))
                dve.tensor_scalar(neg[:, :], top[:, :], -1.0, None, ALU.mult).then_inc(maxed, 1)
                hold(dve, exped, n + 1)
                step(9, dve.reciprocal(inv[:, :], denom[:, :]))
                hold(dve, turned, n + 1)
                dve.tensor_copy(prob_t[:, :], turned_ps[:, :]).then_inc(t_copied, 1)
                hold(dve, weighted, n + 1)
                dve.tensor_scalar(o_heads[:, g, h, (SB - 1) - shift, :], out_ps[:, :], inv[:, 0:1], None, ALU.mult).then_inc(done, 1)

            with general(dve):
                dve.wait_ge(tables, 16)
                dve.tensor_scalar(low[:, :], bound[:, :], -1.0, None, ALU.mult).then_inc(set_up, 1)
                dve.wait_ge(set_up, 1)
                dve.sem_inc(done, 1)
                head_tiles(dve, body)


class Steps:

    def __init__(self, eng, semaphore):
        self.eng, self.semaphore, self.done = eng, semaphore, 0

    def __call__(self, *instructions):
        for ins in instructions:
            ins.then_inc(self.semaphore, 1)
        self.done += len(instructions)
        self.eng.wait_ge(self.semaphore, self.done)


def attention_output(nc, mem, io):
    with ExitStack() as ctx:
        sb, ps, sem = tools(nc, ctx)
        wo, a_t = sb("wo", [P, D]), sb("a_t", [P, 2, 512])
        o_tok, ordered = sb("o_tok", [P, NT, D]), sem("ordered")
        turned_ps = [ps(f"turned_ps{i}", [P, 512]) for i in range(2)]
        out_ps = [ps(f"attn_ps{i}", [P, 512]) for i in range(2)]
        loaded, turned, copied, projected, added = (sem(n) for n in ("wo_in", "turned", "copied", "projected", "added"))
        ident, o_src, x, y = mem["ident"], mem["o_src"], mem["x_tok"], mem["y"]
        block = ctx.enter_context(nc.Block())

        @block.sync
        def _(sp):
            sp.dma_start(wo[:, :], io["L0_attn_Wo"]).then_inc(loaded, 16)
            sp.wait_ge(loaded, 16)

        @block.tensor
        def _(pe):
            pe.wait_ge(loaded, 16)
            for c in range(NT // 4 + 1):
                if c < NT // 4:
                    pe.wait_ge(ordered, c + 1)
                    if c >= 2:
                        pe.wait_ge(copied, c - 1)
                    for k in range(4):
                        last = pe.transpose(turned_ps[c % 2][:, k * P:(k + 1) * P], o_tok[:, 4 * c + k, :], ident[:, :])
                    last.then_inc(turned, 1)
                if c:
                    n = c - 1
                    pe.wait_ge(copied, n + 1)
                    if n >= 2:
                        pe.wait_ge(added, n - 1)
                    for k in range(4):
                        last = pe.matmul(out_ps[n % 2][:, k * P:(k + 1) * P], a_t[:, n % 2, k * P:(k + 1) * P],
                                         wo[:, :], start=True, stop=True)
                    last.then_inc(projected, 1)

        @block.scalar
        def _(act):
            for c in range(NT // 4):
                act.wait_ge(turned, c + 1)
                if c >= 2:
                    act.wait_ge(projected, c - 1)
                act.copy(a_t[:, c % 2, :], turned_ps[c % 2][:, :]).then_inc(copied, 1)

        @block.vector
        def _(dve):
            for c in range(NT // 4):
                b, t = 4 * c // SB, 4 * c % SB
                dve.tensor_copy(o_tok[:, 4 * c:4 * c + 4, :].rearrange("p t (g r) -> p g t r", r=GH * HD),
                                o_src[:, b * (NG // B):(b + 1) * (NG // B), t:t + 4, :]).then_inc(ordered, 1)
            for c in range(NT // 4):
                dve.wait_ge(projected, c + 1)
                dve.tensor_tensor(y[:, 4 * c:4 * c + 4, :], x[:, 4 * c:4 * c + 4, :],
                                  out_ps[c % 2][:, :].rearrange("p (t d) -> p t d", d=D), ALU.add).then_inc(added, 1)


def layer_norm(nc, mem, out=None):
    with ExitStack() as ctx:
        sb, ps, sem = tools(nc, ctx)
        stats, mv = sb("stats", [P, NT, 6]), sb("mv", [P, NT, 2])
        var, std, inv = sb("var", [P, NT]), sb("std", [P, NT]), sb("inv", [P, NT])
        bank = [ps(f"norm_ps{i}", [P, 512]) for i in range(4)]
        steps, var_in, std_in, normed = sem("ln_steps"), sem("var_in"), sem("std_in"), sem("normed")
        turned, copied, stored = sem("ln_turned"), sem("ln_copied"), sem("ln_stored")
        x, x_t, y, ident = mem["x_tok"], mem["x_t"], mem["y"], mem["ident"]
        block = ctx.enter_context(nc.Block())

        @block.vector
        def _(dve):
            step = Steps(dve, steps)
            step(*[dve.bn_stats(stats[:, t, :], y[:, t, :]) for t in range(NT)])
            step(*[dve.bn_aggr(mv[:, t, :], stats[:, t, :]) for t in range(NT)])
            dve.tensor_scalar(var[:, :], mv[:, :, 1], EPS, None, ALU.add).then_inc(var_in, 1)
            dve.wait_ge(std_in, 1)
            step(dve.reciprocal(inv[:, :], std[:, :]))
            for t in range(NT):
                dve.tensor_scalar(x[:, t, :], y[:, t, :], mv[:, t, 0:1], inv[:, t:t + 1],
                                  ALU.subtract, ALU.mult).then_inc(normed, 1)

        @block.scalar
        def _(act):
            act.wait_ge(var_in, 1)
            act.activation(std[:, :], var[:, :], ACT.Sqrt).then_inc(std_in, 1)
            if out is None:
                for c in range(NT // 4):
                    act.wait_ge(turned, c + 1)
                    act.copy(x_t[:, c * 512:(c + 1) * 512], bank[c][:, :]).then_inc(copied, 1)

        if out is None:
            @block.tensor
            def _(pe):
                for t in range(NT):
                    pe.wait_ge(normed, t + 1)
                    last = pe.transpose(bank[t // 4][:, t % 4 * P:t % 4 * P + P], x[:, t, :], ident[:, :])
                    if t % 4 == 3:
                        last.then_inc(turned, 1)
        else:
            @block.sync
            def _(sp):
                for c in range(4):
                    sp.wait_ge(normed, NT // 4 * (c + 1))
                    sp.dma_start(out.rearrange("b (t p) d -> p (b t) d", p=P)[:, 4 * c:4 * c + 4, :],
                                 x[:, 4 * c:4 * c + 4, :]).then_inc(stored, 16)
                sp.wait_ge(stored, 64)


E = 8
C0 = T // E
C1 = int(1.25 * T / E)
F0 = F1 = 512


def route(nc, mem, io, layer):
    K = 1 + layer
    cap = (C0, C1)[layer]
    rows = E * cap
    table, far = mem[f"slots{layer}"], float(4 * T)
    with ExitStack() as ctx:
        sb, ps, sem = tools(nc, ctx)

        def cube(name, dt=F32):
            return sb(name, [P, NT, E], dt)

        router = sb("router", [P, E])
        router_e = sb("router_e", [E, D])
        before, ones = sb("before", [P, P], BF16), sb("ones", [P, P], BF16)
        before_f = sb("before_f", [P, P])
        order, number = sb("order", [P, E]), sb("number", [P, E])
        logit, e_x, same, ranked, left = cube("logit"), cube("e_x"), cube("same"), cube("ranked"), cube("left")
        pick = [cube(f"pick{k}") for k in range(K)]
        picked_b = cube("picked_b", BF16)
        total, total2, place, prod = cube("total"), cube("total2"), cube("place"), cube("prod")
        kept = cube("kept")
        mx, mx2, denom, inv, prob1, prob2, tie = (sb(n, [P, NT]) for n in ("mx", "mx2", "denom", "inv", "prob1", "prob2", "tie"))
        slot, own, is_kept, at, out_at = (sb(n, [P, NT]) for n in ("slot", "own", "is_kept", "at", "out_at"))
        out_index = [sb(f"out_index{k}", [P, NT], I32) for k in range(K)]
        in_index, gate = mem["in_index"], mem["gate"]
        zeros = sb("zeros", [P, 512])
        weight, above = cube("weight"), cube("above", BF16)
        found, cand, more = sb("found", [P, E], I32), sb("cand", [P, E], I32), sb("more", [P, E], I32)
        count, room, fit = sb("count", [P, E], BF16), sb("room", [P, E]), cube("fit")
        logit_ps = ps("logit_ps", [P, NT, E])
        turn_ps = ps("turn_ps", [P, 512])
        place_ps, total_ps, count_ps = ps("place_ps", [P, NT, E]), ps("total_ps", [P, NT, E]), ps("count_ps", [P, 512])
        loaded, zeroed, set_up, routed, steps, exp_in, exped = (
            sem(n) for n in ("rt_loaded", "rt_zeroed", "rt_set", "rt_routed", "rt_steps", "rt_exp_in", "rt_exped"))
        cum_in, cum_out, count_in, count_out, index_in = (
            sem(n) for n in ("cum_in", "cum_out", "count_in", "count_out", "index_in"))
        sent = mem[f"sent{layer}"]
        turned = sem("rt_turned")
        x, x_t, ident = mem["x_tok"], mem["x_t"], mem["ident"]
        block = ctx.enter_context(nc.Block())

        @block.sync
        def _(sp):
            sp.dma_start(before_f[:, :], io["c_before"]).then_inc(loaded, 16)
            sp.dma_start(order[:, :], io["c_order"]).then_inc(loaded, 16)
            sp.dma_start(number[:, :], io["c_number"]).then_inc(loaded, 16)
            if layer == 0:
                sp.dma_start(router[:, :], io["L0_ffn_router_w"]).then_inc(loaded, 16)
            else:
                sp.dma_start(router_e[:, :], io["L1_ffn_router_w"]).then_inc(loaded, 16)
            sp.wait_ge(set_up, 1)
            for r in range(0, rows, 4 * P):
                sp.dma_start(table[r:r + 4 * P, :].rearrange("(p k) d -> p (k d)", k=4), zeros[:, :]).then_inc(zeroed, 16)
            sp.wait_ge(zeroed, 16 * (rows // (4 * P)))

        @block.tensor
        def _(pe):
            pe.wait_ge(loaded, 64)
            if layer == 1:
                pe.transpose(turn_ps[:, 0:E], router_e[:, :], ident[0:E, 0:E]).then_inc(turned, 1)
                pe.wait_ge(steps, 1)
            for t in range(NT):
                last = pe.matmul(logit_ps[:, t, :], x_t[:, t * P:(t + 1) * P], router[:, :], start=True, stop=True)
            last.then_inc(routed, 1)

            def cumulate(n):
                pe.wait_ge(cum_in, n + 1)
                pe.matmul(place_ps[:, :, :], before[:, :], picked_b[:, :, :], start=True, stop=True)
                pe.matmul(total_ps[:, :, :], ones[:, :], picked_b[:, :, :], start=True, stop=True).then_inc(cum_out, 1)

            if layer == 1:
                for n in range(BITS + 1):
                    pe.wait_ge(count_in, n + 1)
                    pe.matmul(count_ps[:, 0:E], ones[:, :], count[:, :], start=True, stop=True).then_inc(count_out, 1)
            for n in range(1 + layer):
                cumulate(n)

        @block.scalar
        def _(act):
            act.wait_ge(exp_in, 1)
            act.activation(e_x[:, :, :], left[:, :, :], ACT.Exp).then_inc(exped, 1)

        def wide(a):
            return a.unsqueeze(2).to_broadcast([P, NT, E])

        def tiles(a):
            return a.unsqueeze(1).to_broadcast([P, NT, E])

        @block.vector
        def _(dve):
            step = Steps(dve, steps)
            dve.wait_ge(loaded, 64)
            if layer == 1:
                dve.wait_ge(turned, 1)
                step(dve.tensor_copy(router[:, :], turn_ps[:, 0:E]))
            dve.memset(zeros[:, :], 0.0).then_inc(set_up, 1)
            step(dve.memset(ones[:, :], 1.0), dve.tensor_copy(before[:, :], before_f[:, :]))
            dve.wait_ge(routed, 1)
            step(dve.tensor_copy(logit[:, :, :], logit_ps[:, :, :]))
            step(dve.tensor_reduce(mx[:, :], logit[:, :, :], AX, ALU.max))
            dve.tensor_tensor(left[:, :, :], logit[:, :, :], wide(mx[:, :]), ALU.subtract).then_inc(exp_in, 1)
            dve.wait_ge(exped, 1)
            step(dve.tensor_reduce(denom[:, :], e_x[:, :, :], AX, ALU.add), dve.tensor_reduce(mx[:, :], e_x[:, :, :], AX, ALU.max))
            step(dve.reciprocal(inv[:, :], denom[:, :]))
            step(dve.tensor_tensor(prob1[:, :], mx[:, :], inv[:, :], ALU.mult))

            def first_of(values, top, to):
                step(dve.tensor_tensor(same[:, :, :], values, wide(top), ALU.is_equal))
                step(dve.tensor_tensor(ranked[:, :, :], same[:, :, :], tiles(order[:, :]), ALU.mult))
                step(dve.tensor_reduce(tie[:, :], ranked[:, :, :], AX, ALU.max))
                step(dve.tensor_tensor(to[:, :, :], ranked[:, :, :], wide(tie[:, :]), ALU.is_equal))

            first_of(e_x[:, :, :], mx[:, :], pick[0])
            if layer == 1:
                step(dve.scalar_tensor_tensor(left[:, :, :], pick[0][:, :, :], -2.0, e_x[:, :, :], ALU.mult, ALU.add))
                step(dve.tensor_reduce(mx2[:, :], left[:, :, :], AX, ALU.max))
                first_of(left[:, :, :], mx2[:, :], pick[1])
                step(dve.tensor_tensor(prob2[:, :], mx2[:, :], inv[:, :], ALU.mult))
                step(dve.tensor_tensor(denom[:, :], prob1[:, :], prob2[:, :], ALU.add))
                step(dve.tensor_scalar(denom[:, :], denom[:, :], 1e-6, None, ALU.add))
                step(dve.reciprocal(inv[:, :], denom[:, :]))
                step(dve.tensor_tensor(prob1[:, :], prob1[:, :], inv[:, :], ALU.mult),
                     dve.tensor_tensor(prob2[:, :], prob2[:, :], inv[:, :], ALU.mult))
                step(dve.tensor_tensor(prod[:, :, :], pick[0][:, :, :], wide(prob1[:, :]), ALU.mult),
                     dve.tensor_tensor(left[:, :, :], pick[1][:, :, :], wide(prob2[:, :]), ALU.mult),
                     dve.tensor_tensor(same[:, :, :], pick[0][:, :, :], pick[1][:, :, :], ALU.add))
                step(dve.tensor_tensor(weight[:, :, :], prod[:, :, :], left[:, :, :], ALU.add))
                step(dve.scalar_tensor_tensor(weight[:, :, :], same[:, :, :], -1.0, weight[:, :, :], ALU.add, ALU.add))
                step(dve.memset(found[:, :], 0))
                for n in range(BITS):
                    step(dve.tensor_scalar(cand[:, :], found[:, :], 1 << (BITS - 1 - n), None, ALU.bitwise_or))
                    step(dve.tensor_tensor(above[:, :, :], weight[:, :, :], tiles(cand[:, :].bitcast(F32)), ALU.is_ge))
                    with nc.allow_low_precision(reason="counts up to NT are exact"):
                        dve.tensor_reduce(count[:, :], above[:, :, :].rearrange("p t e -> p e t"), AX, ALU.add).then_inc(count_in, 1)
                    dve.wait_ge(count_out, n + 1)
                    step(dve.tensor_scalar(more[:, :], count_ps[:, 0:E], float(cap), None, ALU.is_ge))
                    step(dve.copy_predicated(found[:, :], more[:, :], cand[:, :]))
                bound = found[:, :].bitcast(F32)
                step(dve.tensor_tensor(above[:, :, :], weight[:, :, :], tiles(bound), ALU.is_gt),
                     dve.tensor_tensor(picked_b[:, :, :], weight[:, :, :], tiles(bound), ALU.is_equal))
                with nc.allow_low_precision(reason="counts up to NT are exact"):
                    dve.tensor_reduce(count[:, :], above[:, :, :].rearrange("p t e -> p e t"), AX, ALU.add).then_inc(count_in, 1)
                dve.wait_ge(count_out, BITS + 1)
                step(dve.tensor_scalar(room[:, :], count_ps[:, 0:E], -1.0, float(cap), ALU.mult, ALU.add))
            else:
                step(dve.tensor_copy(picked_b[:, :, :], pick[0][:, :, :]))

            def earlier(n):
                dve.sem_inc(cum_in, 1)
                dve.wait_ge(cum_out, n + 1)
                step(dve.memset(total[:, 0, :], 0.0), dve.tensor_copy(total[:, 1:NT, :], total_ps[:, 0:NT - 1, :]))
                a, b, d = total, total2, 1
                while d < NT:
                    step(dve.tensor_tensor(b[:, d:NT, :], a[:, d:NT, :], a[:, 0:NT - d, :], ALU.add),
                         dve.tensor_copy(b[:, 0:d, :], a[:, 0:d, :]))
                    a, b, d = b, a, 2 * d
                step(dve.tensor_tensor(place[:, :, :], a[:, :, :], place_ps[:, :, :], ALU.add))

            earlier(0)
            if layer == 1:
                step(dve.tensor_tensor(fit[:, :, :], place[:, :, :], tiles(room[:, :]), ALU.is_lt))
                step(dve.tensor_tensor(fit[:, :, :], fit[:, :, :], picked_b[:, :, :], ALU.mult))
                step(dve.tensor_tensor(kept[:, :, :], fit[:, :, :], above[:, :, :], ALU.add))
                step(dve.tensor_copy(picked_b[:, :, :], kept[:, :, :]))
                earlier(1)
            for k in range(K):
                step(dve.tensor_tensor(prod[:, :, :], pick[k][:, :, :], place[:, :, :], ALU.mult))
                step(dve.tensor_reduce(slot[:, :], prod[:, :, :], AX, ALU.add))
                step(dve.tensor_tensor(prod[:, :, :], pick[k][:, :, :], tiles(number[:, :]), ALU.mult))
                step(dve.tensor_reduce(own[:, :], prod[:, :, :], AX, ALU.add))
                if layer == 0:
                    step(dve.tensor_scalar(is_kept[:, :], slot[:, :], float(cap), None, ALU.is_lt))
                else:
                    step(dve.tensor_tensor(prod[:, :, :], pick[k][:, :, :], kept[:, :, :], ALU.mult))
                    step(dve.tensor_reduce(is_kept[:, :], prod[:, :, :], AX, ALU.add))
                step(dve.tensor_scalar(slot[:, :], slot[:, :], float(cap - 1), None, ALU.min))
                step(dve.scalar_tensor_tensor(at[:, :], own[:, :], float(cap), slot[:, :], ALU.mult, ALU.add))
                step(dve.tensor_scalar(out_at[:, :], is_kept[:, :], -far, far, ALU.mult, ALU.add))
                step(dve.tensor_tensor(out_at[:, :], out_at[:, :], at[:, :], ALU.add))
                step(dve.tensor_copy(out_index[k][:, :], out_at[:, :]),
                     dve.tensor_copy(in_index[:, k, :], at[:, :]),
                     dve.tensor_tensor(gate[:, k, :], (prob1, prob2)[k][:, :], is_kept[:, :], ALU.mult))
                dve.sem_inc(index_in, 1)

        @block.gpsimd
        def _(pool):
            pool.wait_ge(zeroed, 16 * (rows // (4 * P)))
            for k in range(K):
                pool.wait_ge(index_in, k + 1)
                for t in range(NT):
                    pool.indirect_dma_start(table[:, :], bass.IndirectOffsetOnAxis(out_index[k][:, t:t + 1], 0),
                                            x[:, t, :], None, bounds_check=rows - 1, oob_is_err=False).then_inc(sent, 16)
            pool.wait_ge(sent, 16 * NT * K)


BITS = 30


def experts(nc, mem, io, layer):
    cap = (C0, C1)[layer]
    F, FC = F0, F0 // P
    NX = -(-cap // P)
    names = (("w1", "w2"), ("wg", "wu", "wd"))[layer]
    ups = len(names) - 1
    sizes = [min(P, cap - k * P) for k in range(NX)]
    with ExitStack() as ctx:
        sb, ps, sem = tools(nc, ctx)
        w_up = [sb(f"w_up{i}", [P, ups, F]) for i in range(2)]
        w_down = [sb(f"w_down{i}", [P, FC, D]) for i in range(2)]
        rows_in = [sb(f"rows_in{i}", [P, NX, D]) for i in range(2)]
        rows_t = [sb(f"rows_t{i}", [P, cap]) for i in range(2)]
        hidden = [sb(f"hidden{i}", [P, FC, cap]) for i in range(2)]
        acted = sb("acted", [P, 2, cap])
        rows_out = [sb(f"rows_out{i}", [P, NX, D]) for i in range(2)]
        turn_ps = ps("xturn_ps", [P, 512])
        up_ps = [[ps(f"up_ps{i}{j}", [P, 512]) for j in range(ups)] for i in range(2)]
        down_ps = [ps(f"down_ps{i}", [P, 512]) for i in range(2)]
        w_in = [sem(f"w_in{i}") for i in range(2)]
        r_in = [sem(f"r_in{i}") for i in range(2)]
        turned, t_copied, upped, h_in, downed, out_in = (sem(n) for n in ("xturned", "t_copied", "upped", "h_in", "downed", "out_in"))
        acted_in = sem("acted_in")
        stored = [sem(f"r_out{i}") for i in range(2)]
        ident = mem["ident"]
        table, results = mem[f"slots{layer}"], mem[f"results{layer}"]
        block = ctx.enter_context(nc.Block())
        NL = ups + 1

        @block.sync
        def _(sp):
            def store(e):
                sp.wait_ge(out_in, (e + 1) * NX)
                for k, n in enumerate(sizes):
                    sp.dma_start(results[e * cap + k * P:e * cap + k * P + n, :], rows_out[e % 2][0:n, k, :]).then_inc(stored[e % 2], 16)

            for e in range(E):
                if e >= 2:
                    sp.wait_ge(downed, e - 1)
                for j in range(ups):
                    sp.dma_start(w_up[e % 2][:, j, :], io[f"L{layer}_ffn_{names[j]}"][e]).then_inc(w_in[e % 2], 16)
                sp.dma_start(w_down[e % 2][:, :, :],
                             io[f"L{layer}_ffn_{names[-1]}"][e].rearrange("(c p) d -> p c d", p=P)).then_inc(w_in[e % 2], 16)
                for k, n in enumerate(sizes):
                    sp.dma_start(rows_in[e % 2][0:n, k, :], table[e * cap + k * P:e * cap + k * P + n, :]).then_inc(r_in[e % 2], 16)
                if e >= 2:
                    store(e - 2)
            store(E - 2)
            store(E - 1)
            for i in range(2):
                sp.wait_ge(stored[i], E // 2 * NX * 16)

        @block.tensor
        def _(pe):
            for e in range(E):
                pe.wait_ge(r_in[e % 2], (e // 2 + 1) * NX * 16)
                if e:
                    pe.wait_ge(t_copied, e)
                for k, n in enumerate(sizes):
                    last = pe.transpose(turn_ps[:, k * P:k * P + n], rows_in[e % 2][0:n, k, :], ident[0:n, 0:n])
                last.then_inc(turned, 1)
                pe.wait_ge(w_in[e % 2], (e // 2 + 1) * NL * 16)
                pe.wait_ge(t_copied, e + 1)
                for c in range(FC):
                    n = e * FC + c
                    if n >= 2:
                        pe.wait_ge(h_in, n - 1)
                    for j in range(ups):
                        last = pe.matmul(up_ps[n % 2][j][:, 0:cap], w_up[e % 2][:, j, c * P:(c + 1) * P],
                                         rows_t[e % 2][:, :], start=True, stop=True)
                    last.then_inc(upped, 1)
                pe.wait_ge(h_in, (e + 1) * FC)
                if e >= 2:
                    pe.wait_ge(out_in, (e - 1) * NX)
                for k, n in enumerate(sizes):
                    for c in range(FC):
                        last = pe.matmul(down_ps[e % 2][0:n, k * P:(k + 1) * P], hidden[e % 2][:, c, k * P:k * P + n],
                                         w_down[e % 2][:, c, :], start=(c == 0), stop=(c == FC - 1))
                last.then_inc(downed, 1)

        @block.scalar
        def _(act):
            for n in range(E * FC):
                e, c = n // FC, n % FC
                act.wait_ge(upped, n + 1)
                if c == 0 and e >= 2:
                    act.wait_ge(downed, e - 1)
                if layer == 0:
                    act.activation(hidden[e % 2][:, c, :], up_ps[n % 2][0][:, 0:cap], ACT.Gelu_apprx_tanh).then_inc(h_in, 1)
                else:
                    if n >= 2:
                        act.wait_ge(h_in, n - 1)
                    act.activation(acted[:, n % 2, :], up_ps[n % 2][0][:, 0:cap], ACT.Silu).then_inc(acted_in, 1)

        @block.vector
        def _(dve):
            for e in range(E):
                dve.wait_ge(turned, e + 1)
                if e >= 2:
                    dve.wait_ge(upped, (e - 1) * FC)
                dve.tensor_copy(rows_t[e % 2][:, :], turn_ps[:, 0:cap]).then_inc(t_copied, 1)
                if layer == 1:
                    for c in range(FC):
                        n = e * FC + c
                        dve.wait_ge(acted_in, n + 1)
                        if c == 0 and e >= 2:
                            dve.wait_ge(downed, e - 1)
                        dve.tensor_tensor(hidden[e % 2][:, c, :], acted[:, n % 2, :], up_ps[n % 2][1][:, 0:cap],
                                          ALU.mult).then_inc(h_in, 1)
                dve.wait_ge(downed, e + 1)
                if e >= 2:
                    dve.wait_ge(stored[e % 2], (e // 2) * NX * 16)
                for k, n in enumerate(sizes):
                    dve.tensor_copy(rows_out[e % 2][0:n, k, :], down_ps[e % 2][0:n, k * P:(k + 1) * P]).then_inc(out_in, 1)


def combine(nc, mem, layer):
    K = 1 + layer
    with ExitStack() as ctx:
        sb, ps, sem = tools(nc, ctx)
        got = [sb(f"got{k}", [P, NT, D]) for k in range(K)]
        gathered = mem[f"gathered{layer}"]
        summed = sem("summed")
        x, y, in_index, gate = mem["x_tok"], mem["y"], mem["in_index"], mem["gate"]
        block = ctx.enter_context(nc.Block())

        @block.gpsimd
        def _(pool):
            for t in range(NT):
                for k in range(K):
                    pool.indirect_dma_start(got[k][:, t, :], None, mem[f"results{layer}"][:, :],
                                            bass.IndirectOffsetOnAxis(in_index[:, k, t:t + 1], 0)).then_inc(gathered[t // 4], 16)

        @block.vector
        def _(dve):
            for t in range(NT):
                if t % 4 == 0:
                    dve.wait_ge(gathered[t // 4], 4 * K * 16)
                for k in range(K):
                    if k:
                        dve.wait_ge(summed, K * t + k)
                    dve.scalar_tensor_tensor(y[:, t, :], got[k][:, t, :], gate[:, k, t:t + 1],
                                             (x, y)[k][:, t, :], ALU.mult, ALU.add).then_inc(summed, 1)


H1 = 8
NC1 = S // P


def rms_scale(dve, act_ready, step, x, square, mean, eps, var_in, std_in, std, inv):
    step(dve.tensor_tensor(square[:, :, :], x[:, :, :], x[:, :, :], ALU.mult))
    step(dve.tensor_reduce(mean[:, :], square[:, :, :], AX, ALU.add))
    dve.tensor_scalar(mean[:, :], mean[:, :], 1.0 / D, eps, ALU.mult, ALU.add).then_inc(var_in, 1)
    dve.wait_ge(std_in, act_ready)
    step(dve.reciprocal(inv[:, :], std[:, :]))


def rms_norm(nc, mem, io, weight, source):
    with ExitStack() as ctx:
        sb, ps, sem = tools(nc, ctx)
        w_row = sb("w_row", [P, D])
        square = sb("square", [P, NT, D])
        mean, std, inv = sb("mean", [P, NT]), sb("std", [P, NT]), sb("inv", [P, NT])
        bank = [ps(f"rms_ps{i}", [P, 512]) for i in range(4)]
        loaded, steps, var_in, std_in, normed, turned, copied = (
            sem(n) for n in ("rms_loaded", "rms_steps", "rms_var", "rms_std", "rms_normed", "rms_turned", "rms_copied"))
        x, h_tok, h_t, ident = mem[source], mem["h_tok"], mem["h_t"], mem["ident"]
        block = ctx.enter_context(nc.Block())

        @block.sync
        def _(sp):
            sp.dma_start(w_row[:, :], io[weight].rearrange("(a d) -> a d", a=1).to_broadcast([P, D])).then_inc(loaded, 16)
            sp.wait_ge(loaded, 16)

        @block.vector
        def _(dve):
            step = Steps(dve, steps)
            rms_scale(dve, 1, step, x, square, mean, EPS, var_in, std_in, std, inv)
            dve.wait_ge(loaded, 16)
            for t in range(NT):
                dve.scalar_tensor_tensor(h_tok[:, t, :], x[:, t, :], inv[:, t:t + 1], w_row[:, :],
                                         ALU.mult, ALU.mult).then_inc(normed, 1)

        @block.scalar
        def _(act):
            act.wait_ge(var_in, 1)
            act.activation(std[:, :], mean[:, :], ACT.Sqrt).then_inc(std_in, 1)
            for c in range(NT // 4):
                act.wait_ge(turned, c + 1)
                act.copy(h_t[:, c * 512:(c + 1) * 512], bank[c][:, :]).then_inc(copied, 1)

        @block.tensor
        def _(pe):
            for t in range(NT):
                pe.wait_ge(normed, t + 1)
                last = pe.transpose(bank[t // 4][:, t % 4 * P:t % 4 * P + P], h_tok[:, t, :], ident[:, :])
                if t % 4 == 3:
                    last.then_inc(turned, 1)


def linear_weights(nc, mem, io):
    with ExitStack() as ctx:
        sb, ps, sem = tools(nc, ctx)
        w = [sb(f"w{n}", [P, H1, P]) for n in "qkv"]
        wo, turned_w = sb("wo1", [P, H1, D]), sb("turned_w", [P, 2, 3, P])
        norm_w = sb("norm_w", [P, 1])
        turn_ps = [ps(f"wturn_ps{i}", [P, 3, P]) for i in range(2)]
        fold_ps = [ps(f"fold_ps{i}", [P, 2, D]) for i in range(2)]
        loaded, scaled, turned, t_copied, folded, f_copied = (
            sem(n) for n in ("lw_loaded", "lw_scaled", "lw_turned", "lw_tcopied", "lw_folded", "lw_fcopied"))
        ident, a_w, vm_w = mem["ident"], mem["a_w"], mem["vm_w"]
        block = ctx.enter_context(nc.Block())

        @block.sync
        def _(sp):
            for k, n in enumerate("qkv"):
                sp.dma_start(w[k][:, :, :], io["L1_attn_W" + n].rearrange("d (h e) -> d h e", h=H1)).then_inc(loaded, 16)
            sp.dma_start(wo[:, :, :], io["L1_attn_Wo"].rearrange("(h e) d -> e h d", h=H1)).then_inc(loaded, 16)
            sp.dma_start(norm_w[:, :], io["L1_attn_attn_out_norm_w"].rearrange("(d a) -> d a", a=1)).then_inc(loaded, 16)

        @block.tensor
        def _(pe):
            pe.wait_ge(loaded, 80)
            for h in range(H1 + 1):
                if h < H1:
                    if h >= 2:
                        pe.wait_ge(t_copied, h - 1)
                    for k in range(3):
                        last = pe.transpose(turn_ps[h % 2][:, k, :], w[k][:, h, :], ident[:, :])
                    last.then_inc(turned, 1)
                if h:
                    g = h - 1
                    pe.wait_ge(t_copied, g + 1)
                    pe.wait_ge(scaled, 1)
                    if g >= 2:
                        pe.wait_ge(f_copied, g - 1)
                    pe.matmul(fold_ps[g % 2][:, 0, :], turned_w[:, g % 2, 0, :], turned_w[:, g % 2, 1, :], start=True, stop=True)
                    pe.matmul(fold_ps[g % 2][:, 1, :], turned_w[:, g % 2, 2, :], wo[:, g, :], start=True, stop=True).then_inc(folded, 1)

        @block.vector
        def _(dve):
            dve.wait_ge(loaded, 80)
            dve.tensor_scalar(wo[:, :, :], wo[:, :, :], norm_w[:, 0:1], None, ALU.mult).then_inc(scaled, 1)
            for h in range(H1):
                dve.wait_ge(turned, h + 1)
                if h >= 2:
                    dve.wait_ge(folded, h - 1)
                dve.tensor_copy(turned_w[:, h % 2, :, :], turn_ps[h % 2][:, :, :]).then_inc(t_copied, 1)

        @block.scalar
        def _(act):
            act.wait_ge(loaded, 80)
            for h in range(H1):
                act.wait_ge(folded, h + 1)
                act.copy(a_w[:, h, :], fold_ps[h % 2][:, 0, :])
                act.copy(vm_w[:, h, 0:D], w[2][:, h, :])
                act.copy(vm_w[:, h, D:2 * D], fold_ps[h % 2][:, 1, :]).then_inc(f_copied, 1)


def linear_attention(nc, mem, io):
    with ExitStack() as ctx:
        sb, ps, sem = tools(nc, ctx)
        chunk_t = [sb(f"chunk_t{i}", [P, P]) for i in range(2)]
        chunk_k = [sb(f"chunk_k{i}", [P, D]) for i in range(2)]
        sums = [sb(f"sums{i}", [P, D]) for i in range(2)]
        query = sb("query", [P, H1, P])
        scores = sb("scores", [P, H1, P])
        mixed = sb("mixed", [P, H1, P])
        causal = sb("causal", [P, P])
        squares = sb("squares", [P, H1, D])
        mean, std, inv = sb("o_mean", [P, 2, H1]), sb("o_std", [P, 2, H1]), sb("o_inv", [P, 2, H1])
        heads = sb("heads", [P, H1, D])
        total = sb("heads_sum", [P, D])
        work = [ps(f"work{i}", [P, 4, P]) for i in range(4)]
        outs = [ps(f"outs{i}", [P, 2, 2 * D]) for i in range(4)]
        loaded, set_up, staged = sem("la_loaded"), sem("la_set"), sem("staged")
        q_done, q_copied, s_done, s_copied = sem("q_done"), sem("q_copied"), sem("s_done"), sem("s_copied")
        m_done, m_copied, g_done, g_copied = sem("m_done"), sem("m_copied"), sem("g_done"), sem("g_copied")
        o_done, squared, steps, root_in, root_out, scaled, y_in = (
            sem(n) for n in ("la_o", "squared", "la_steps", "root_in", "root_out", "la_scaled", "y_in"))
        x, y, h_t, h_tok, a_w, vm_w = (mem[n] for n in ("x_tok", "y", "h_t", "h_tok", "a_w", "vm_w"))
        block = ctx.enter_context(nc.Block())
        HH = H1 // 2

        STEPS = 4

        def summed_at(n):
            return n * STEPS + 1

        @block.sync
        def _(sp):
            sp.dma_start(causal[:, :], io["c_causal"]).then_inc(loaded, 16)
            sp.wait_ge(loaded, 16)

        @block.gpsimd
        def _(pool):
            for n in range(NT):
                c = n % 2
                if n >= 2:
                    pool.wait_ge(o_done, n - 1)
                pool.tensor_copy(chunk_t[c][:, :], h_t[:, n * P:(n + 1) * P]).then_inc(staged, 1)
                pool.tensor_copy(chunk_k[c][:, :], h_tok[:, n, :]).then_inc(staged, 1)

        @block.tensor
        def _(pe):
            def queries(n):
                for h in range(H1):
                    if h % HH == 0 and n:
                        pe.wait_ge(m_copied, 2 * (n - 1) + h // HH + 1)
                    last = pe.matmul(work[h // HH][:, h % HH, :], a_w[:, h, :], h_t[:, n * P:(n + 1) * P], start=True, stop=True)
                    if h % HH == HH - 1:
                        last.then_inc(q_done, 1)

            def attend(n):
                c = n % 2
                pe.wait_ge(staged, 2 * n + 2)
                for half in range(2):
                    pe.wait_ge(q_copied, 2 * n + half + 1)
                    if n:
                        pe.wait_ge(g_copied, n)
                    pe.matmul(work[2 + half][:, :, :], chunk_t[c][:, :], query[:, half * HH:(half + 1) * HH, :],
                              start=True, stop=True).then_inc(s_done, 1)

            def mix(n):
                c = n % 2
                for half in range(2):
                    pe.wait_ge(s_copied, 2 * n + half + 1)
                    first = n % NC1 == 0
                    last = pe.matmul(work[half][:, :, :], chunk_k[c][:, :], scores[:, half * HH:(half + 1) * HH, :],
                                     start=True, stop=first)
                    if not first:
                        pe.wait_ge(g_copied, n)
                        last = pe.matmul(work[half][:, :, :], sums[(n - 1) % 2][:, :], query[:, half * HH:(half + 1) * HH, :],
                                         start=False, stop=True)
                    last.then_inc(m_done, 1)

            def gather(n):
                pe.wait_ge(s_copied, 2 * n + 1)
                pe.matmul(work[2][:, 0, :], chunk_k[n % 2][:, :], chunk_k[n % 2][:, :], start=True, stop=True).then_inc(g_done, 1)

            def project(n):
                for h in range(H1):
                    if h % HH == 0:
                        pe.wait_ge(m_copied, 2 * n + h // HH + 1)
                        if n:
                            pe.wait_ge(scaled, n)
                            pe.wait_ge(squared, n)
                    last = pe.matmul(outs[h // 2][:, h % 2, :], mixed[:, h, :], vm_w[:, h, :], start=True, stop=True)
                last.then_inc(o_done, 1)

            for n in range(NT):
                queries(n)
                if n:
                    project(n - 1)
                attend(n)
                gather(n)
                mix(n)
            project(NT - 1)

        @block.scalar
        def _(act):
            def root(n):
                act.wait_ge(root_in, n + 1)
                act.activation(std[:, n % 2, :], mean[:, n % 2, :], ACT.Sqrt).then_inc(root_out, 1)

            for n in range(NT):
                for half in range(2):
                    act.wait_ge(q_done, 2 * n + half + 1)
                    if n:
                        act.wait_ge(m_done, 2 * (n - 1) + half + 1)
                    act.copy(query[:, half * HH:(half + 1) * HH, :], work[half][:, :, :]).then_inc(q_copied, 1)
                if n:
                    act.wait_ge(o_done, n)
                    if n > 1:
                        act.wait_ge(steps, summed_at(n - 2))
                    for k in range(4):
                        last = act.activation(squares[:, 2 * k:2 * k + 2, :], outs[k][:, :, 0:D], ACT.Square)
                    last.then_inc(squared, 1)
                for half in range(2):
                    act.wait_ge(m_done, 2 * n + half + 1)
                    if n:
                        act.wait_ge(o_done, n)
                    act.copy(mixed[:, half * HH:(half + 1) * HH, :], work[half][:, :, :]).then_inc(m_copied, 1)
                if n:
                    root(n - 1)
            act.wait_ge(o_done, NT)
            act.wait_ge(steps, summed_at(NT - 2))
            for k in range(4):
                last = act.activation(squares[:, 2 * k:2 * k + 2, :], outs[k][:, :, 0:D], ACT.Square)
            last.then_inc(squared, 1)
            root(NT - 1)

        @block.vector
        def _(dve):
            step = Steps(dve, steps)
            dve.wait_ge(loaded, 16)

            def mask(n):
                for half in range(2):
                    dve.wait_ge(s_done, 2 * n + half + 1)
                    if n:
                        dve.wait_ge(m_done, 2 * (n - 1) + half + 1)
                    dve.tensor_tensor(scores[:, half * HH:(half + 1) * HH, :], work[2 + half][:, :, :],
                                      causal[:, :].unsqueeze(1).to_broadcast([P, HH, P]), ALU.mult).then_inc(s_copied, 1)

            def add_up(n):
                dve.wait_ge(g_done, n + 1)
                if n:
                    dve.wait_ge(m_done, 2 * n)
                if n % NC1 == 0:
                    dve.tensor_copy(sums[n % 2][:, :], work[2][:, 0, :]).then_inc(g_copied, 1)
                else:
                    dve.wait_ge(g_copied, n)
                    dve.tensor_tensor(sums[n % 2][:, :], sums[(n - 1) % 2][:, :], work[2][:, 0, :], ALU.add).then_inc(g_copied, 1)

            def finish(n):
                dve.wait_ge(squared, n + 1)
                step(dve.tensor_reduce(mean[:, n % 2, :], squares[:, :, :], AX, ALU.add))
                dve.tensor_scalar(mean[:, n % 2, :], mean[:, n % 2, :], 1.0 / P, EPS, ALU.mult, ALU.add).then_inc(root_in, 1)
                dve.wait_ge(root_out, n + 1)
                step(dve.reciprocal(inv[:, n % 2, :], std[:, n % 2, :]))
                for k in range(4):
                    last = dve.tensor_tensor(heads[:, 2 * k:2 * k + 2, :], outs[k][:, :, D:2 * D],
                                             inv[:, n % 2, 2 * k:2 * k + 2].unsqueeze(2).to_broadcast([P, 2, D]), ALU.mult)
                last.then_inc(scaled, 1)
                dve.wait_ge(scaled, n + 1)
                step(dve.tensor_reduce(total[:, :], heads[:, :, :].rearrange("p h d -> p d h"), AX, ALU.add))
                step(dve.tensor_tensor(y[:, n, :], total[:, :], x[:, n, :], ALU.add))

            for n in range(NT):
                mask(n)
                add_up(n)
                if n:
                    finish(n - 1)
            finish(NT - 1)


def gated_mlp(nc, mem, io):
    FC = F0 // P
    with ExitStack() as ctx:
        sb, ps, sem = tools(nc, ctx)
        w_gate, w_up, w_down = sb("w_gate", [P, F0]), sb("w_up1", [P, F0]), sb("w_down1", [P, FC, D])
        acted, hidden = sb("acted1", [P, 2, 512]), sb("hidden1", [P, 2, FC, 512])
        up_ps = [[ps(f"gu_ps{i}{j}", [P, 512]) for j in range(2)] for i in range(2)]
        down_ps = [ps(f"dn_ps{i}", [P, 4, D]) for i in range(2)]
        loaded, upped, acted_in, h_in, downed, added = (sem(n) for n in ("m_loaded", "m_upped", "m_acted", "m_h", "m_downed", "m_added"))
        x, y, h_t = mem["x_tok"], mem["y"], mem["h_t"]
        around = sem("m_around")
        block = ctx.enter_context(nc.Block())
        NB = T // 512

        @block.sync
        def _(sp):
            sp.dma_start(w_gate[:, :], io["L1_attn_Wgate"]).then_inc(loaded, 16)
            sp.dma_start(w_up[:, :], io["L1_attn_Wup"]).then_inc(loaded, 16)
            sp.dma_start(w_down[:, :, :], io["L1_attn_Wdown"].rearrange("(c p) d -> p c d", p=P)).then_inc(loaded, 16)

        @block.tensor
        def _(pe):
            pe.wait_ge(loaded, 48)

            def down(b):
                pe.wait_ge(h_in, (b + 1) * FC)
                if b >= 2:
                    pe.wait_ge(added, b - 1)
                for k in range(4):
                    for c in range(FC):
                        last = pe.matmul(down_ps[b % 2][:, k, :], hidden[:, b % 2, c, k * P:(k + 1) * P], w_down[:, c, :],
                                         start=(c == 0), stop=(c == FC - 1))
                last.then_inc(downed, 1)

            for b in range(NB):
                for c in range(FC):
                    n = b * FC + c
                    if n >= 2:
                        pe.wait_ge(h_in, n - 1)
                    for j, w in enumerate((w_gate, w_up)):
                        last = pe.matmul(up_ps[n % 2][j][:, :], w[:, c * P:(c + 1) * P], h_t[:, b * 512:(b + 1) * 512],
                                         start=True, stop=True)
                    last.then_inc(upped, 1)
                if b:
                    down(b - 1)
            down(NB - 1)

        @block.scalar
        def _(act):
            for n in range(NB * FC):
                act.wait_ge(upped, n + 1)
                if n >= 2:
                    act.wait_ge(h_in, n - 1)
                act.activation(acted[:, n % 2, :], up_ps[n % 2][0][:, :], ACT.Silu).then_inc(acted_in, 1)

        @block.vector
        def _(dve):
            dve.tensor_tensor(y[:, :, :], y[:, :, :], x[:, :, :], ALU.add).then_inc(around, 1)
            dve.wait_ge(around, 1)
            for b in range(NB + 1):
                if b < NB:
                    for c in range(FC):
                        n = b * FC + c
                        dve.wait_ge(acted_in, n + 1)
                        if b >= 2:
                            dve.wait_ge(downed, b - 1)
                        dve.tensor_tensor(hidden[:, b % 2, c, :], acted[:, n % 2, :], up_ps[n % 2][1][:, :], ALU.mult).then_inc(h_in, 1)
                if b:
                    dve.wait_ge(downed, b)
                    dve.tensor_tensor(y[:, 4 * b - 4:4 * b, :], y[:, 4 * b - 4:4 * b, :], down_ps[(b - 1) % 2][:, :, :], ALU.add).then_inc(added, 1)


def two_layers(nc, io, out):
    with ExitStack() as ctx:
        sb, ps, sem = tools(nc, ctx, last=True)
        mem = {
            "x_tok": sb("x_tok", [P, NT, D]), "x_t": sb("x_t", [P, T]), "ident": sb("ident", [P, P]),
            "y": sb("y", [P, NT, D]), "in_index": sb("in_index", [P, 2, NT], I32), "gate": sb("gate", [P, 2, NT]),
            "clamps": sb("clamps", [1, 1], I32),
            "slots0": nc.dram_tensor("slots0", (E * C0, D), F32, kind="Internal").ap(),
            "slots1": nc.dram_tensor("slots1", (E * C1, D), F32, kind="Internal").ap(),
            "results0": nc.dram_tensor("results0", (E * C0, D), F32, kind="Internal").ap(),
            "results1": nc.dram_tensor("results1", (E * C1, D), F32, kind="Internal").ap(),
        }
        for i in range(2):
            mem[f"sent{i}"] = sem(f"sent{i}")
            mem[f"gathered{i}"] = [sem(f"gathered{i}_{c}") for c in range(NT // 4)]
        dram = {"parts": nc.dram_tensor("parts_dram", (2, 2, NG, GH, NPART, HD, S), BF16, kind="Internal").ap()}
        with ExitStack() as layer:
            sb, ps, sem = tools(nc, layer)
            mem.update(v_src=sb("v_src", [P, NG, SB, 32]), o_src=sb("o_src", [P, NG, SB, 32]), rest=sb("rest", [P, 2 * S - P]))
            attention_setup(nc, mem, dram, io)
            attention_scores(nc, mem, dram)
            attention_general(nc, mem, dram, io)
            attention_output(nc, mem, io)
        layer_norm(nc, mem)
        route(nc, mem, io, 0)
        experts(nc, mem, io, 0)
        combine(nc, mem, 0)
        layer_norm(nc, mem)
        with ExitStack() as layer:
            sb, ps, sem = tools(nc, layer)
            mem.update(h_tok=sb("h_tok", [P, NT, D]), h_t=sb("h_t", [P, T]), a_w=sb("a_w", [P, H1, D]), vm_w=sb("vm_w", [P, H1, 2 * D]))
            linear_weights(nc, mem, io)
            rms_norm(nc, mem, io, "L1_attn_attn_norm_w", "x_tok")
            linear_attention(nc, mem, io)
            rms_norm(nc, mem, io, "L1_attn_mlp_norm_w", "y")
            gated_mlp(nc, mem, io)
        layer_norm(nc, mem)
        route(nc, mem, io, 1)
        experts(nc, mem, io, 1)
        combine(nc, mem, 1)
        layer_norm(nc, mem, out)


def kernel(**inputs):
    import numpy as _np
    import concourse.bacc as _bacc
    from concourse import mybir as _mybir
    from concourse.bass_utils import run_bass_kernel_spmd as _run

    nc = _bacc.Bacc("TRN2", target_bir_lowering=False, num_devices=1)
    arrays, io = {}, {}
    for name, value in {**inputs, **host_constants()}.items():
        a = _np.ascontiguousarray(value)
        arrays[f"in_{name}_dram"] = a
        io[name] = nc.dram_tensor(f"in_{name}_dram", a.shape, _mybir.dt.from_np(a.dtype), kind="ExternalInput").ap()
    out = nc.dram_tensor("out_0_dram", (B, S, D), _mybir.dt.float32, kind="ExternalOutput").ap()
    two_layers(nc, io, out)
    r = _run(nc, [arrays], core_ids=[0])
    return r.results[0]["out_0_dram"]
```

```python
from contextlib import ExitStack

import numpy as np

import concourse.bass as bass
from concourse import mybir

ALU = mybir.AluOpType
ACT = mybir.ActivationFunctionType
AX = mybir.AxisListType.X
F32 = mybir.dt.float32
BF16 = mybir.dt.bfloat16
I32 = mybir.dt.int32

P = 128
B, S, D = 2, 1024, 128
T = B * S
NT = T // P
SB = S // P
EPS = 1e-5

H0, HD = 16, 8
GH = 4
NG = B * H0 // GH
LAT = 32
SCALE0 = 1.0 / (np.sqrt(np.float32(D)) + np.float32(1e-8))
CLAMP = 10000.0
DECAY = 0.01 * 0.01
NPART = 3
KR = NPART * NPART * HD
KX = KR + NPART


def host_constants():
    i = np.arange(S, dtype=np.float32)
    p = np.arange(P)
    c = np.float32(-DECAY)
    ramp = np.stack([np.exp(c * i), np.exp(-c * i)]).astype(np.float32)
    u = np.arange(2 * S - P)[None, :] - (S - P) - p[:, None]
    bound = (np.float32(CLAMP) * np.exp(-c * u.astype(np.float32))).astype(np.float32)
    rest = np.where(u > 0, np.exp(2 * c * u.astype(np.float32)), 1.0).astype(np.float32)
    ident = np.eye(P, dtype=np.float32)
    before = (p[:, None] < p[None, :]).astype(np.float32)
    return {
        "c_ramp": np.ascontiguousarray(np.broadcast_to(ramp[None], (P, 2, S))),
        "c_bound": bound, "c_rest": rest, "c_ident": ident, "c_before": before,
        "c_causal": (p[:, None] <= p[None, :]).astype(np.float32),
        "c_order": np.ascontiguousarray(np.broadcast_to(np.arange(E, 0, -1, dtype=np.float32), (P, E))),
        "c_number": np.ascontiguousarray(np.broadcast_to(np.arange(E, dtype=np.float32), (P, E))),
    }


def attention_setup(nc, mem, dram, io):
    with ExitStack() as ctx:
        sb, ps, sem = tools(nc, ctx)
        wq, wk, wv = (sb(n, [P, D]) for n in ("wq", "wk", "wv"))
        wd, wu = sb("wd", [P, LAT]), sb("wu", [LAT, 2, D])
        wkv, wkv_t, l_t = sb("wkv", [P, D]), sb("wkv_t", [P, D]), sb("l_t", [LAT, P])
        w_qk, w_val = sb("w_qk", [P, 2, D]), sb("w_val", [P, D])
        ramp = sb("ramp", [P, 2, S])
        raw = sb("raw", [P, 2, T])
        full = sb("full", [P, 2, T])
        left = sb("left", [P, 2, T])
        parts = sb("parts", [P, 4, NPART, T], BF16)
        ones, extent, limits = sb("ones", [P, 1]), sb("extent", [P, 4]), sb("limits", [1, 8])
        bank = [ps(f"setup{i}", [P, 512]) for i in range(8)]
        x_in = [sem(f"x_in{c}") for c in range(2)]
        weights_in, ramp_in, later_in = sem("weights_in"), sem("ramp_in"), sem("later_in")
        transposed, x_copied, folded, fold_copied = sem("transposed"), sem("x_copied"), sem("folded"), sem("fold_copied")
        kv_summed, q_ordered = sem("kv_summed"), sem("q_ordered")
        projected, raw_copied, valued, v_copied = sem("projected"), sem("raw_copied"), sem("valued"), sem("v_copied")
        scaled, part0, left1, part1, part2, stored = (sem(n) for n in ("scaled", "part0", "left1", "part1", "part2", "stored"))
        ones_in, squared, reached, summed, judged = (sem(n) for n in ("ones_in", "squared", "reached", "summed", "judged"))
        x_tok, x_t, ident, v_src = mem["x_tok"], mem["x_t"], mem["ident"], mem["v_src"]
        block = ctx.enter_context(nc.Block())
        x_view = io["L0_attn_x"].rearrange("b (t p) d -> p (b t) d", p=P)

        def by_feature(w):
            return w.rearrange("p (g h r) -> p g r h", g=NG // B, h=GH)

        @block.sync
        def _(sp):
            sp.dma_start(ident[:, :], io["c_ident"]).then_inc(x_in[0], 16)
            sp.dma_start(x_tok[:, 0:NT // 2, :], x_view[:, 0:NT // 2, :]).then_inc(x_in[0], 16)
            sp.dma_start(wq[:, :], io["L0_attn_Wq"]).then_inc(weights_in, 16)
            sp.dma_start(wk[:, :], io["L0_attn_Wk"]).then_inc(weights_in, 16)
            sp.dma_start(wv[:, :], io["L0_attn_Wv"]).then_inc(weights_in, 16)
            sp.dma_start(x_tok[:, NT // 2:NT, :], x_view[:, NT // 2:NT, :]).then_inc(x_in[1], 16)
            for n in range(4):
                for k in range(NPART):
                    sp.wait_ge((part0, part1, part2)[k], n + 1)
                    for b in range(B):
                        sp.dma_start(
                            dram["parts"][n % 2, n // 2, b * (NG // B):(b + 1) * (NG // B), k, :, :, :].rearrange(
                                "g r h t -> g (r h) t"),
                            parts[:, n, k, b * S:(b + 1) * S]).then_inc(stored, 16)
            sp.wait_ge(stored, 4 * NPART * B * 16)
            sp.wait_ge(later_in, 16)

        @block.tensor
        def _(pe):
            for t in range(NT):
                if t % (NT // 2) == 0:
                    pe.wait_ge(x_in[0], 32)
                    if t:
                        pe.wait_ge(x_in[1], 16)
                last = pe.transpose(bank[t // 4][:, t % 4 * P:t % 4 * P + P], x_tok[:, t, :], ident[:, :])
                if t % 4 == 3:
                    last.then_inc(transposed, 1)
            pe.wait_ge(kv_summed, 1)
            pe.transpose(bank[4][:, 0:P], wkv[:, :], ident[:, :]).then_inc(folded, 1)
            pe.wait_ge(q_ordered, 1)
            for c in range(4):
                pe.wait_ge(x_copied, c + 1)
                pe.matmul(bank[c][:, :], w_qk[:, 0, :], x_t[:, c * 512:(c + 1) * 512],
                          start=True, stop=True).then_inc(projected, 1)
            pe.wait_ge(fold_copied, 1)
            pe.matmul(bank[5][0:LAT, 0:P], wd[:, :], wkv_t[:, :], start=True, stop=True).then_inc(folded, 1)
            pe.wait_ge(fold_copied, 2)
            pe.matmul(bank[6][:, 0:2 * D], l_t[:, :], wu[:, :, :], start=True, stop=True).then_inc(folded, 1)
            pe.wait_ge(fold_copied, 4)
            for c in range(4):
                pe.matmul(bank[4 + c][:, :], w_qk[:, 1, :], x_t[:, c * 512:(c + 1) * 512],
                          start=True, stop=True).then_inc(projected, 1)
            for t in range(NT):
                if t % 4 == 0:
                    pe.wait_ge(raw_copied, t // 4 + 1)
                last = pe.matmul(bank[t // 4][:, t % 4 * P:t % 4 * P + P], x_t[:, t * P:(t + 1) * P],
                                 w_val[:, :], start=True, stop=True)
                if t % 4 == 3:
                    last.then_inc(valued, 1)
            pe.wait_ge(reached, 2)
            pe.wait_ge(squared, 2)
            pe.wait_ge(raw_copied, 5)
            pe.matmul(bank[4][0:1, 0:4], ones[:, :], extent[:, :], start=True, stop=True).then_inc(summed, 1)

        @block.scalar
        def _(act):
            act.dma_start(wd[:, :], io["L0_attn_W_down_kv"]).then_inc(weights_in, 16)
            act.dma_start(wu[:, 0, :], io["L0_attn_W_up_k"]).then_inc(weights_in, 16)
            act.dma_start(wu[:, 1, :], io["L0_attn_W_up_v"]).then_inc(weights_in, 16)
            act.dma_start(ramp[:, :, :], io["c_ramp"]).then_inc(ramp_in, 16)
            act.dma_start(mem["rest"][:, :], io["c_rest"]).then_inc(later_in, 16)
            for c in range(4):
                act.wait_ge(transposed, c + 1)
                act.copy(x_t[:, c * 512:(c + 1) * 512], bank[c][:, :]).then_inc(x_copied, 1)
            for n in range(2):
                for c in range(4):
                    act.wait_ge(projected, 4 * n + c + 1)
                    act.activation(raw[:, n, c * 512:(c + 1) * 512], bank[4 * n + c][:, :], ACT.Copy,
                                   scale=float(SCALE0) if n == 0 else 1.0).then_inc(raw_copied, 1)

            def first_part(n):
                act.wait_ge(scaled, 2 * n + 2)
                act.copy(parts[:, n, 0, :], full[:, n % 2, :]).then_inc(part0, 1)

            def second_part(n):
                act.wait_ge(left1, n + 1)
                act.copy(parts[:, n, 1, :], left[:, n % 2, :]).then_inc(part1, 1)

            first_part(0)
            first_part(1)
            second_part(0)
            second_part(1)
            for t in range(NT):
                if t % 4 == 0:
                    act.wait_ge(valued, t // 4 + 1)
                last = act.copy(
                    v_src[:, t // SB * (NG // B):(t // SB + 1) * (NG // B), t % SB, :],
                    bank[t // 4][:, t % 4 * P:t % 4 * P + P].rearrange("p (g r) -> p g r", r=GH * HD))
            last.then_inc(v_copied, 1)
            first_part(2)
            first_part(3)
            second_part(2)
            second_part(3)
            for n in range(2):
                act.wait_ge(part0, 4)
                act.wait_ge(left1, 4)
                act.activation(full[:, n, :], raw[:, n, :], ACT.Square, accum_out=extent[:, 2 + n:3 + n]).then_inc(squared, 1)

        @block.vector
        def _(dve):
            dve.memset(ones[:, :], 1.0).then_inc(ones_in, 1)
            dve.wait_ge(weights_in, 6 * 16)
            dve.tensor_tensor(wkv[:, :], wk[:, :], wv[:, :], ALU.add).then_inc(kv_summed, 1)
            dve.tensor_copy(w_qk[:, 0, :].rearrange("p (g r h) -> p g r h", g=NG // B, r=HD), by_feature(wq[:, :])).then_inc(q_ordered, 1)
            dve.wait_ge(folded, 1)
            dve.tensor_copy(wkv_t[:, :], bank[4][:, 0:P]).then_inc(fold_copied, 1)
            dve.wait_ge(folded, 2)
            dve.tensor_copy(l_t[:, :], bank[5][0:LAT, 0:P]).then_inc(fold_copied, 1)
            dve.wait_ge(folded, 3)
            dve.tensor_copy(w_qk[:, 1, :].rearrange("p (g r h) -> p g r h", g=NG // B, r=HD),
                            by_feature(bank[6][:, 0:D])).then_inc(fold_copied, 1)
            dve.tensor_copy(w_val[:, :], bank[6][:, D:2 * D]).then_inc(fold_copied, 1)
            dve.wait_ge(ramp_in, 16)

            def scale(n):
                dve.wait_ge(raw_copied, 4 * (n % 2 + 1))
                if n >= 2:
                    dve.wait_ge(part0, n - 1)
                    dve.wait_ge(left1, n - 1)
                for b in range(B):
                    dve.tensor_tensor(full[:, n % 2, b * S:(b + 1) * S], raw[:, n % 2, b * S:(b + 1) * S],
                                      ramp[:, (n // 2 + n) % 2, :], ALU.mult).then_inc(scaled, 1)

            def first_left(n):
                dve.wait_ge(part0, n + 1)
                if n >= 2:
                    dve.wait_ge(part1, n - 1)
                    dve.wait_ge(part2, n - 1)
                dve.tensor_tensor(left[:, n % 2, :], full[:, n % 2, :], parts[:, n, 0, :], ALU.subtract).then_inc(left1, 1)

            def second_left(n):
                dve.wait_ge(part1, n + 1)
                dve.tensor_tensor(parts[:, n, 2, :], left[:, n % 2, :], parts[:, n, 1, :], ALU.subtract).then_inc(part2, 1)

            for pair in range(2):
                for step in (scale, first_left, second_left):
                    step(2 * pair)
                    step(2 * pair + 1)
            for n in range(2):
                dve.wait_ge(squared, n + 1)
                dve.tensor_reduce(extent[:, n:n + 1], full[:, n, :], AX, ALU.max).then_inc(reached, 1)
            dve.wait_ge(summed, 1)
            dve.tensor_copy(limits[:, 0:4], bank[4][0:1, 0:4]).then_inc(judged, 1)
            dve.wait_ge(judged, 1)
            dve.tensor_tensor(limits[:, 4:5], limits[:, 0:1], limits[:, 1:2], ALU.mult).then_inc(judged, 1)
            dve.tensor_tensor(limits[:, 5:6], limits[:, 2:3], limits[:, 3:4], ALU.mult).then_inc(judged, 1)
            dve.wait_ge(judged, 3)
            dve.tensor_scalar(limits[:, 6:7], limits[:, 4:5], 0.9 * CLAMP * CLAMP, None, ALU.is_lt).then_inc(judged, 1)
            dve.tensor_scalar(limits[:, 7:8], limits[:, 5:6], 1e30, None, ALU.is_lt).then_inc(judged, 1)
            dve.wait_ge(judged, 5)
            dve.tensor_tensor(limits[:, 0:1], limits[:, 6:7], limits[:, 7:8], ALU.mult).then_inc(judged, 1)
            dve.wait_ge(judged, 6)
            dve.tensor_scalar(mem["clamps"][:, :], limits[:, 0:1], -1.0, 1.0, ALU.mult, ALU.add).then_inc(judged, 1)


def tools(nc, ctx, last=False):
    stage = nc.next_id()
    taken = []

    def zero():
        for s in taken:
            nc.sync.sem_clear(s)

    if not last:
        ctx.callback(zero)

    def sb(name, shape, dt=F32):
        return ctx.enter_context(nc.sbuf_tensor(f"{name}_{stage}", shape, dt))

    def ps(name, shape, dt=F32):
        return ctx.enter_context(nc.psum_tensor(f"{name}_{stage}", shape, dt))

    def sem(name):
        taken.append(ctx.enter_context(nc.semaphore(f"{name}_{stage}")))
        return taken[-1]

    return sb, ps, sem


TWO_ONES = float(np.array([0x3F803F80], np.uint32).view(np.float32)[0])
LOWEST = -3.0e38
ROW_EVERY = 0.68
COST = {"unit": 0.45, "turn": 0.45, "weigh": 0.94, "late": 0.5, "row": 0.216}


class Group:

    def __init__(self, k, turn=0):
        self.k, self.turn = k, turn
        self.third = k % 3
        self.n = k + 3 * turn
        self.round = k // 3 + turn


def attention_scores(nc, mem, dram):
    with ExitStack() as ctx:
        sb, ps, sem = tools(nc, ctx)
        NU = SB * GH + SB // 2
        HALF = S // 2
        NA = SB * GH * 2
        stack = [sb(f"stack{i}", [P, 2, 2, GH, S], BF16) for i in range(3)]
        v_aug = [sb(f"v_aug{i}", [P, SB, GH, 32]) for i in range(3)]
        prob = [sb(f"prob{i}", [P, GH, S]) for i in range(2)]
        prob_late = [sb(f"prob_late{i}", [P, 2, GH, P]) for i in range(2)]
        junk = sb("junk", [P, 2, HALF], BF16)
        top = sb("top", [P, 2, GH, SB, 2])
        neg = sb("neg", [P, GH, SB])
        neg_left = sb("neg_left", [P, GH, SB])
        neg_parts = sb("neg_parts", [P, GH, NPART, SB], BF16)
        ident_b = sb("ident_b", [P, P], BF16)
        neg_rows = sb("neg_rows", [GH * NPART * SB, P], BF16)
        o_t = sb("o_t", [P, S])
        recip = sb("recip", [P, SB, GH])
        score = [ps(f"score{i}", [P, S]) for i in range(2)]
        out_ps = ps("out_ps", [P, S])
        row = ps("row", [P, 2, HALF])
        rest, ident, v_src, o_src = mem["rest"], mem["ident"], mem["v_src"], mem["o_src"]

        rows_set, values_set, ident_cast = [sem(f"rows_set{i}") for i in range(3)], sem("values_set"), sem("ident_cast")
        dve_passed, pool_passed = sem("dve_passed"), sem("pool_passed")
        stacks_in = [sem(f"stacks_in{i}") for i in range(3)]
        v_staged = sem("v_staged")
        row_ready, row_done = sem("row_ready"), sem("row_done")
        neg_chain, neg_turned, neg_copied = sem("neg_chain"), sem("neg_turned"), sem("neg_copied")
        neg_in = [sem(f"neg_in{i}") for i in range(3)]
        scored, exped, masked, mask_late = sem("scored"), sem("exped"), sem("masked"), sem("mask_late")
        weighted, o_copied, o_turned, o_inv, o_done = sem("weighted"), sem("o_copied"), sem("o_turned"), sem("o_inv"), sem("o_done")
        block = ctx.enter_context(nc.Block())

        units = []
        for pair in range(SB // 2):
            units += [("tile", 2 * pair + k, h) for k in range(2) for h in range(GH)]
            units += [("late", pair, 0)]
        unit_at = {u: n for n, u in enumerate(units)}

        def first(g):
            return isinstance(g.n, int) and g.n == 0

        def run_groups(eng, body):
            body(None, Group(0), None)
            body(Group(0), Group(1), None)
            with eng.Fori(0, (NG - 2) // 3) as turn:
                for k in (1, 2, 3):
                    body(Group(k, turn), Group(k + 1, turn), Group(k - 1, turn))
            body(Group(NG - 1), None, Group(NG - 2))

        LOADS, NEGS = 2 * (NPART + 1), 2 * GH

        schedule = []
        for n, (kind, tile, h) in enumerate(units):
            schedule.append(("unit", n, 0))
            if n == 3:
                schedule.append(("turn", 0, 0))
            if kind == "tile" and tile and h in (1, 3):
                schedule.append(("weigh", tile - 1, h // 2))
            if kind == "tile" and tile and tile % 2 == 0 and h == 2:
                schedule.append(("late", tile // 2 - 1, 0))
        tail = [("weigh", SB - 1, 0), ("weigh", SB - 1, 1), ("late", SB // 2 - 1, 0)]
        merged, clock, n_row = [], 0.0, 0
        for step in schedule:
            merged.append(step)
            clock += COST[step[0]]
            while n_row < NA and n_row * ROW_EVERY < clock:
                merged.append(("row", n_row, 0))
                clock += COST["row"]
                n_row += 1
        merged += [("row", n, 0) for n in range(n_row, NA)]
        rows_before = sum(kind == "row" for kind, _, _ in merged[:merged.index(("weigh", 0, 0))])
        product_order = [(kind, tile) for kind, tile, half in schedule + tail
                         if kind == "late" or (kind == "weigh" and half == 1)]
        product_order = [("tile" if kind == "weigh" else kind, tile) for kind, tile in product_order]
        NW = len(product_order)

        def used_tile(g, tile):
            if tile >= 2:
                return g.n * NW + product_order.index(("tile", tile - 2)) + 1
            return (g.n - 1) * NW + product_order.index(("tile", SB - 2 + tile)) + 1

        def used_late(g, pair):
            if pair >= 2:
                return g.n * NW + product_order.index(("late", pair - 2)) + 1
            return (g.n - 1) * NW + product_order.index(("late", SB // 2 - 2 + pair)) + 1

        @block.sync
        def _(sp):
            with sp.If(sp.value_load(mem["clamps"][0:1, 0:1], min_val=0, max_val=1) == 0):
                def load(g):
                    to = stack[g.third]
                    for half in range(2):
                        for a in range(NPART):
                            sp.dma_start(to[a * NPART * HD:(a + 1) * NPART * HD, half, 0, :, :],
                                         dram["parts"][0, half, g.n, a, :, :, :].unsqueeze(0).to_broadcast([NPART, HD, GH, S])
                                         ).then_inc(stacks_in[g.third], 16)
                        key = dram["parts"][1, half, g.n, :, :, :, :].rearrange("k r h t -> (k r) h t")
                        sp.dma_start(to[0:KR, half, 1, :, :],
                                     key.unsqueeze(0).to_broadcast([NPART, NPART * HD, GH, S])).then_inc(stacks_in[g.third], 16)

                def store_neg(g):
                    sp.wait_ge(neg_copied, g.n + 1)
                    for h in range(GH):
                        for half in range(2):
                            sp.dma_start(stack[g.third][KR:KR + NPART, half, 0, h, :].rearrange("k (t c) -> k t c", c=P),
                                         neg_rows[h * NPART * SB:(h + 1) * NPART * SB, :]
                                         ).then_inc(neg_in[g.third], 16)

                sp.wait_ge(rows_set[0], 1)
                load(Group(0))
                sp.wait_ge(rows_set[1], 1)
                load(Group(1))
                store_neg(Group(0))
                sp.wait_ge(rows_set[2], 1)
                load(Group(2))
                store_neg(Group(1))

                def body(g, ahead):
                    sp.wait_ge(scored, g.n * NU)
                    load(ahead)
                    store_neg(Group(g.k + 1, g.turn))

                with sp.Fori(0, (NG - 2) // 3 - 1) as turn:
                    for k in (1, 2, 3):
                        body(Group(k, turn), Group(k + 2, turn))
                body(Group(NG - 4), Group(NG - 2))
                body(Group(NG - 3), Group(NG - 1))
                store_neg(Group(NG - 1))
                for i in range(3):
                    sp.wait_ge(neg_in[i], (NG - 1 - i + 3) // 3 * NEGS * 16)

        @block.tensor
        def _(pe):
            with pe.If(pe.value_load(mem["clamps"][0:1, 0:1], min_val=0, max_val=1) == 0):
                def row_unit(g, n):
                    tile, h, part = n // (2 * GH), n // 2 % GH, n % 2
                    if n == 0:
                        pe.wait_ge(stacks_in[g.third], (g.round + 1) * LOADS * 16)
                        if not first(g):
                            pe.wait_ge(neg_copied, g.n)
                    if not (first(g) and n < 2):
                        pe.wait_ge(row_done, g.n * NA + n - 1)
                    pe.matmul(row[:, n % 2, :], stack[g.third][0:KR, 0, 0, h, tile * P:(tile + 1) * P],
                              stack[g.third][0:KR, 0, 1, h, part * HALF:(part + 1) * HALF],
                              start=True, stop=True).then_inc(row_ready, 1)

                def turn_neg(g):
                    pe.wait_ge(neg_chain, 6 * (g.n + 1))
                    pe.transpose(row[0:GH * NPART * SB, 0, 0:P // 2].bitcast(BF16),
                                 neg_parts[:, :, :, :], ident_b[:, :]).then_inc(neg_turned, 1)

                def column_unit(g, n):
                    kind, tile, h = units[n]
                    if n == 0:
                        pe.wait_ge(neg_in[g.third], (g.round + 1) * NEGS * 16)
                    if not (first(g) and n < 2):
                        pe.wait_ge(exped, g.n * NU + n - 1)
                    out = score[n % 2]
                    if kind == "tile":
                        at = tile * P
                        pieces = [(1, a, min(b, at)) for a, b in ((0, HALF), (HALF, S)) if a < at]
                        pieces += [(0, max(a, at), b) for a, b in ((0, HALF), (HALF, S)) if b > at]
                        for half, a, b in pieces:
                            last = pe.matmul(out[:, a:b], stack[g.third][0:KX, half, 1, h, at:at + P],
                                             stack[g.third][0:KX, half, 0, h, a:b], start=True, stop=True)
                    else:
                        for k in range(2):
                            at = (2 * tile + k) * P
                            for hh in range(GH):
                                c = (k * GH + hh) * P
                                last = pe.matmul(out[:, c:c + P], stack[g.third][0:KX, 1, 1, hh, at:at + P],
                                                 stack[g.third][0:KX, 1, 0, hh, at:at + P], start=True, stop=True)
                    last.then_inc(scored, 1)

                def weigh(g, tile, part):
                    if tile == 0 and part == 0:
                        pe.wait_ge(v_staged, g.n + 1)
                        if not first(g):
                            pe.wait_ge(o_done, g.n)
                    if part == 0:
                        pe.wait_ge(masked, g.n * SB + tile + 1)
                    for h in range(GH):
                        last = pe.matmul(out_ps[32 * h:32 * h + 32, part * HALF:(part + 1) * HALF],
                                         v_aug[g.third][:, tile, h, :], prob[tile % 2][:, h, part * HALF:(part + 1) * HALF],
                                         start=(tile == 0), stop=False, skip_group_check=True)
                    if part == 1:
                        last.then_inc(weighted, 1)

                def weigh_late(g, pair):
                    pe.wait_ge(mask_late, g.n * (SB // 2) + pair + 1)
                    for k in range(2):
                        tile = 2 * pair + k
                        for h in range(GH):
                            last = pe.matmul(out_ps[32 * h:32 * h + 32, tile * P:(tile + 1) * P],
                                             v_aug[g.third][:, tile, h, :], prob_late[pair % 2][:, k, h, :],
                                             start=False, stop=(pair == SB // 2 - 1), skip_group_check=True)
                    last.then_inc(weighted, 1)

                def turn_out(g):
                    pe.wait_ge(o_copied, g.n + 1)
                    for t in range(SB):
                        last = pe.transpose(out_ps[:, t * P:(t + 1) * P], o_t[:, t * P:(t + 1) * P], ident[:, :])
                    last.then_inc(o_turned, 1)

                def body(g, nxt, before):
                    if g is None:
                        for n in range(NA):
                            row_unit(nxt, n)
                        turn_neg(nxt)
                        return
                    for kind, tile, h in merged:
                        if kind == "row":
                            if nxt is not None:
                                row_unit(nxt, tile)
                        elif kind == "unit":
                            column_unit(g, tile)
                        elif kind == "turn":
                            if not first(g):
                                turn_out(before)
                        elif kind == "weigh":
                            weigh(g, tile, h)
                        else:
                            weigh_late(g, tile)
                    if nxt is not None:
                        turn_neg(nxt)
                    for kind, tile, h in tail:
                        if kind == "weigh":
                            weigh(g, tile, h)
                        else:
                            weigh_late(g, tile)

                pe.wait_ge(ident_cast, 1)
                pe.wait_ge(values_set, 6)
                run_groups(pe, body)
                turn_out(Group(NG - 1))

        @block.scalar
        def _(act):
            with act.If(act.value_load(mem["clamps"][0:1, 0:1], min_val=0, max_val=1) == 0):
                def finish(g):
                    act.wait_ge(weighted, (g.n + 1) * (SB + SB // 2))
                    if not first(g):
                        act.wait_ge(o_turned, g.n)
                    act.copy(o_t[:, :], out_ps[:, :]).then_inc(o_copied, 1)

                def body(g, nxt, before):
                    if g is None:
                        return
                    for n, (kind, tile, h) in enumerate(units):
                        if n == 3 and not first(g):
                            finish(before)
                        act.wait_ge(scored, g.n * NU + n + 1)
                        if kind == "tile":
                            if h == 0 and not (first(g) and tile < 2):
                                act.wait_ge(weighted, used_tile(g, tile))
                            act.activation(prob[tile % 2][:, h, :], score[n % 2][:, :], ACT.Exp).then_inc(exped, 1)
                        else:
                            if not (first(g) and tile < 2):
                                act.wait_ge(weighted, used_late(g, tile))
                            act.activation(prob_late[tile % 2][:, :, :, :],
                                           score[n % 2][:, :].rearrange("p (k h c) -> p k h c", k=2, h=GH),
                                           ACT.Exp).then_inc(exped, 1)

                run_groups(act, body)
                finish(Group(NG - 1))

        @block.gpsimd
        def _(pool):
            with pool.If(pool.value_load(mem["clamps"][0:1, 0:1], min_val=0, max_val=1) == 0):
                def stage(g):
                    if not (isinstance(g.n, int) and g.n < 2):
                        pool.wait_ge(weighted, (g.n - 1) * NW)
                    pool.tensor_copy(v_aug[g.third][:, :, :, 0:HD],
                                     v_src[:, g.n, :, :].rearrange("p t (h r) -> p t h r", r=HD)).then_inc(v_staged, 1)

                def body(g, nxt, before):
                    if g is None:
                        stage(nxt)
                        return
                    if nxt is not None:
                        stage(nxt)
                    for n, (kind, tile, h) in enumerate(units):
                        if kind == "tile" and h == GH - 1:
                            at = tile * P
                            pool.wait_ge(exped, g.n * NU + n + 1)
                            pool.sem_inc(pool_passed, 1)
                            pool.affine_select(out=prob[tile % 2][:, :, at:at + P], in_=prob[tile % 2][:, :, at:at + P],
                                               compare_op=ALU.is_ge, fill=0.0, base=0, pattern=[[0, GH], [1, P]],
                                               channel_multiplier=-1).then_inc(masked, 1)
                        if kind == "late":
                            pool.wait_ge(exped, g.n * NU + n + 1)
                            pool.sem_inc(pool_passed, 1)
                            pool.affine_select(out=prob_late[tile % 2][:, :, :, :], in_=prob_late[tile % 2][:, :, :, :],
                                               compare_op=ALU.is_gt, fill=0.0, base=0, pattern=[[0, 2 * GH], [-1, P]],
                                               channel_multiplier=1).then_inc(mask_late, 1)

                for i in (1, 2):
                    pool.memset(stack[i][64:96, :, 1, :, :].bitcast(F32), TWO_ONES).then_inc(rows_set[i], 1)
                pool.wait_ge(rows_set[2], 1)
                for v in v_aug:
                    pool.memset(v[:, :, :, HD + 1:32], 0.0).then_inc(values_set, 1)
                    pool.memset(v[:, :, :, HD:HD + 1], 1.0).then_inc(values_set, 1)
                pool.tensor_copy(ident_b[:, :], ident[:, :]).then_inc(ident_cast, 1)
                run_groups(pool, body)

        @block.vector
        def _(dve):
            with dve.If(dve.value_load(mem["clamps"][0:1, 0:1], min_val=0, max_val=1) == 0):
                def row_unit(g, n):
                    tile, h, part = n // (2 * GH), n // 2 % GH, n % 2
                    dve.wait_ge(row_ready, g.n * NA + n + 1)
                    at = S - P - tile * P + part * HALF
                    dve.sem_inc(dve_passed, 1)
                    dve.tensor_tensor_reduce(junk[:, n % 2, :], row[:, n % 2, :], rest[:, at:at + HALF], 1.0, LOWEST,
                                             ALU.mult, ALU.max, top[:, 0, h, tile, part:part + 1]).then_inc(row_done, 1)

                def negate(g):
                    base = g.n * 6
                    dve.wait_ge(row_done, (g.n + 1) * NA)
                    dve.tensor_reduce(top[:, 1, :, :, 0], top[:, 0, :, :, :], AX, ALU.max).then_inc(neg_chain, 1)
                    dve.wait_ge(neg_chain, base + 1)
                    dve.tensor_scalar(neg[:, :, :], top[:, 1, :, :, 0], -1.0, None, ALU.mult).then_inc(neg_chain, 1)
                    dve.wait_ge(neg_chain, base + 2)
                    if not first(g):
                        dve.wait_ge(neg_turned, g.n)
                    dve.tensor_copy(neg_parts[:, :, 0, :], neg[:, :, :]).then_inc(neg_chain, 1)
                    dve.wait_ge(neg_chain, base + 3)
                    dve.tensor_tensor(neg_left[:, :, :], neg[:, :, :], neg_parts[:, :, 0, :], ALU.subtract).then_inc(neg_chain, 1)
                    dve.wait_ge(neg_chain, base + 4)
                    dve.tensor_copy(neg_parts[:, :, 1, :], neg_left[:, :, :]).then_inc(neg_chain, 1)
                    dve.wait_ge(neg_chain, base + 5)
                    dve.tensor_tensor(neg_parts[:, :, 2, :], neg_left[:, :, :], neg_parts[:, :, 1, :], ALU.subtract).then_inc(neg_chain, 1)
                    dve.wait_ge(neg_turned, g.n + 1)
                    if not first(g):
                        prev = Group(g.k - 1, g.turn)
                        dve.wait_ge(neg_in[prev.third], (prev.round + 1) * NEGS * 16)
                    dve.tensor_copy(neg_rows[:, :], row[0:GH * NPART * SB, 0, 0:P // 2].bitcast(BF16)).then_inc(neg_copied, 1)

                def finish(g):
                    dve.wait_ge(o_turned, g.n + 1)
                    out = out_ps[:, :].rearrange("p (t h r) -> p t h r", t=SB, h=GH)
                    if not first(g):
                        dve.wait_ge(o_done, g.n)
                    dve.reciprocal(recip[:, :, :], out[:, :, :, HD]).then_inc(o_inv, 1)
                    dve.wait_ge(o_inv, g.n + 1)
                    dve.tensor_tensor(o_src[:, g.n, :, :].rearrange("p t (h r) -> p t h r", r=HD), out[:, :, :, 0:HD],
                                      recip[:, :, :].unsqueeze(3).to_broadcast([P, SB, GH, HD]), ALU.mult).then_inc(o_done, 1)

                def body(g, nxt, before):
                    if nxt is not None:
                        for n in range(NA):
                            row_unit(nxt, n)
                            if n == rows_before - 2 and g is not None and not first(g):
                                finish(before)
                        negate(nxt)
                    else:
                        finish(before)

                dve.memset(stack[0][64:96, :, 1, :, :].bitcast(F32), TWO_ONES).then_inc(rows_set[0], 1)
                run_groups(dve, body)
                finish(Group(NG - 1))


def attention_general(nc, mem, dram, io):
    with ExitStack() as ctx:
        sb, ps, sem = tools(nc, ctx)
        queries, keys = sb("queries", [P, S], BF16), sb("keys", [P, S], BF16)
        bound, low, rest = sb("bound", [P, 2 * S - P]), sb("low", [P, 2 * S - P]), mem["rest"]
        raw, clean, number = sb("raw", [P, S]), sb("clean", [P, S]), sb("number", [P, S], I32)
        prob, prob_t = sb("prob", [P, S]), sb("prob_t", [P, S])
        top, neg, denom, inv = (sb(n, [P, 1]) for n in ("top", "neg", "denom", "inv"))
        score, turned_ps, out_ps = ps("score", [P, S]), ps("turned", [P, S]), ps("out", [P, HD])
        loaded, tables, set_up, scored, steps, maxed, exped, turned, t_copied, weighted, done = (
            sem(n) for n in ("loaded", "tables", "set_up", "scored", "steps", "maxed", "exped", "turned", "t_copied",
                             "weighted", "done"))
        ident, v_src, o_src = mem["ident"], mem["v_src"], mem["o_src"]
        passed = sem("passed")
        block = ctx.enter_context(nc.Block())
        STEPS = 9

        def general(eng):
            return eng.If(eng.value_load(mem["clamps"][0:1, 0:1], min_val=0, max_val=1) == 1)

        def head_tiles(eng, body):
            with eng.Fori(0, NG) as g:
                with eng.Fori(0, GH) as h:
                    with eng.Fori(0, SB) as shift:
                        body(g, h, shift, g * (GH * SB) + h * SB + shift)

        def hold(eng, semaphore, value):
            eng.wait_ge(semaphore, value)
            eng.sem_inc(passed, 1)

        parts = dram["parts"]
        v_heads = v_src[:, :, :, :].rearrange("p g t (h r) -> p g h t r", r=HD)
        o_heads = o_src[:, :, :, :].rearrange("p g t (h r) -> p g h t r", r=HD)

        @block.sync
        def _(sp):
            with general(sp):
                sp.dma_start(bound[:, :], io["c_bound"]).then_inc(tables, 16)
                sp.wait_ge(tables, 16)
                with sp.Fori(0, NG) as g:
                  with sp.Fori(0, GH) as h:
                    hold(sp, done, g * (GH * SB) + h * SB + 1)
                    for a in range(NPART):
                        sp.dma_start(queries[a * NPART * HD:(a + 1) * NPART * HD, :],
                                     parts[0, 0, g, a, :, h, :].unsqueeze(0).to_broadcast([NPART, HD, S])).then_inc(loaded, 16)
                    sp.dma_start(keys[0:KR, :], parts[1, 0, g, :, :, h, :].rearrange("k r t -> (k r) t")
                                 .unsqueeze(0).to_broadcast([NPART, NPART * HD, S])).then_inc(loaded, 16)

        @block.tensor
        def _(pe):
            def body(g, h, shift, n):
                hold(pe, loaded, g * (GH * 16 * (NPART + 1)) + h * (16 * (NPART + 1)) + 16 * (NPART + 1))
                hold(pe, done, n + 1)
                for c in range(2):
                    last = pe.matmul(score[:, c * 512:(c + 1) * 512],
                                     queries[0:KR, bass.ds((SB - 1) * P - shift * P, P)],
                                     keys[0:KR, c * 512:(c + 1) * 512], start=True, stop=True)
                last.then_inc(scored, 1)
                hold(pe, exped, n + 1)
                for t in range(SB):
                    last = pe.transpose(turned_ps[:, t * P:(t + 1) * P], prob[:, t * P:(t + 1) * P], ident[:, :])
                last.then_inc(turned, 1)
                hold(pe, t_copied, n + 1)
                for t in range(SB):
                    last = pe.matmul(out_ps[:, :], prob_t[:, t * P:(t + 1) * P], v_heads[:, g, h, t, :],
                                     start=(t == 0), stop=(t == SB - 1))
                last.then_inc(weighted, 1)

            with general(pe):
                pe.wait_ge(tables, 16)
                head_tiles(pe, body)

        @block.scalar
        def _(act):
            def body(g, h, shift, n):
                hold(act, maxed, n + 1)
                act.activation(prob[:, :], clean[:, :], ACT.Exp, bias=neg[:, 0:1], accum_out=denom[:, 0:1]).then_inc(exped, 1)

            with general(act):
                head_tiles(act, body)

        @block.vector
        def _(dve):
            def body(g, h, shift, n):
                base = n * STEPS

                def step(k, ins):
                    ins.then_inc(steps, 1)
                    hold(dve, steps, base + k)

                hold(dve, scored, n + 1)
                dve.tensor_copy(raw[:, :], score[:, :]).then_inc(steps, 1)

                def at(table):
                    return table[:, bass.ds(shift * P, S)]

                dve.tensor_copy(clean[:, :], at(low)).then_inc(steps, 1)
                hold(dve, steps, base + 2)
                step(3, dve.tensor_tensor(number[:, :], raw[:, :], raw[:, :], ALU.is_equal))
                step(4, dve.copy_predicated(clean[:, :], number[:, :], raw[:, :]))
                step(5, dve.tensor_tensor(clean[:, :], clean[:, :], at(bound), ALU.min))
                step(6, dve.tensor_tensor(clean[:, :], clean[:, :], at(low), ALU.max))
                step(7, dve.tensor_tensor(clean[:, :], clean[:, :], at(rest), ALU.mult))
                step(8, dve.tensor_reduce(top[:, :], clean[:, :], AX, ALU.max))
                dve.tensor_scalar(neg[:, :], top[:, :], -1.0, None, ALU.mult).then_inc(maxed, 1)
                hold(dve, exped, n + 1)
                step(9, dve.reciprocal(inv[:, :], denom[:, :]))
                hold(dve, turned, n + 1)
                dve.tensor_copy(prob_t[:, :], turned_ps[:, :]).then_inc(t_copied, 1)
                hold(dve, weighted, n + 1)
                dve.tensor_scalar(o_heads[:, g, h, (SB - 1) - shift, :], out_ps[:, :], inv[:, 0:1], None, ALU.mult).then_inc(done, 1)

            with general(dve):
                dve.wait_ge(tables, 16)
                dve.tensor_scalar(low[:, :], bound[:, :], -1.0, None, ALU.mult).then_inc(set_up, 1)
                dve.wait_ge(set_up, 1)
                dve.sem_inc(done, 1)
                head_tiles(dve, body)


class Steps:

    def __init__(self, eng, semaphore):
        self.eng, self.semaphore, self.done = eng, semaphore, 0

    def __call__(self, *instructions):
        for ins in instructions:
            ins.then_inc(self.semaphore, 1)
        self.done += len(instructions)
        self.eng.wait_ge(self.semaphore, self.done)


def statistics(dve, mem, step, tiles):
    step(*[dve.bn_stats(mem["stats"][:, t, :], mem["y"][:, t, :]) for t in tiles])
    step(*[dve.bn_aggr(mem["mv"][:, t, :], mem["stats"][:, t, :]) for t in tiles])


def attention_output(nc, mem, io):
    with ExitStack() as ctx:
        sb, ps, sem = tools(nc, ctx)
        wo, a_t = sb("wo", [P, D]), sb("a_t", [P, 2, 512])
        o_tok, ordered = sb("o_tok", [P, NT, D]), sem("ordered")
        turned_ps = [ps(f"turned_ps{i}", [P, 512]) for i in range(2)]
        out_ps = [ps(f"attn_ps{i}", [P, 512]) for i in range(2)]
        loaded, turned, copied, projected, added = (sem(n) for n in ("wo_in", "turned", "copied", "projected", "added"))
        stat_steps = sem("stat_steps")
        ident, o_src, x, y = mem["ident"], mem["o_src"], mem["x_tok"], mem["y"]
        block = ctx.enter_context(nc.Block())

        @block.sync
        def _(sp):
            sp.dma_start(wo[:, :], io["L0_attn_Wo"]).then_inc(loaded, 16)
            load_expert_weights(sp, mem, io, 0)
            sp.wait_ge(loaded, 16)

        @block.tensor
        def _(pe):
            pe.wait_ge(loaded, 16)
            for c in range(NT // 4 + 1):
                if c < NT // 4:
                    pe.wait_ge(ordered, c + 1)
                    if c >= 2:
                        pe.wait_ge(copied, c - 1)
                    for k in range(4):
                        last = pe.transpose(turned_ps[c % 2][:, k * P:(k + 1) * P], o_tok[:, 4 * c + k, :], ident[:, :])
                    last.then_inc(turned, 1)
                if c:
                    n = c - 1
                    pe.wait_ge(copied, n + 1)
                    if n >= 2:
                        pe.wait_ge(added, n - 1)
                    for k in range(4):
                        last = pe.matmul(out_ps[n % 2][:, k * P:(k + 1) * P], a_t[:, n % 2, k * P:(k + 1) * P],
                                         wo[:, :], start=True, stop=True)
                    last.then_inc(projected, 1)

        @block.scalar
        def _(act):
            for c in range(NT // 4):
                act.wait_ge(turned, c + 1)
                if c >= 2:
                    act.wait_ge(projected, c - 1)
                act.copy(a_t[:, c % 2, :], turned_ps[c % 2][:, :]).then_inc(copied, 1)

        @block.vector
        def _(dve):
            for c in range(NT // 4):
                b, t = 4 * c // SB, 4 * c % SB
                dve.tensor_copy(o_tok[:, 4 * c:4 * c + 4, :].rearrange("p t (g r) -> p g t r", r=GH * HD),
                                o_src[:, b * (NG // B):(b + 1) * (NG // B), t:t + 4, :]).then_inc(ordered, 1)
            step = Steps(dve, stat_steps)
            for c in range(NT // 4):
                dve.wait_ge(projected, c + 1)
                dve.tensor_tensor(y[:, 4 * c:4 * c + 4, :], x[:, 4 * c:4 * c + 4, :],
                                  out_ps[c % 2][:, :].rearrange("p (t d) -> p t d", d=D), ALU.add).then_inc(added, 1)
                dve.wait_ge(added, c + 1)
                statistics(dve, mem, step, range(4 * c, 4 * c + 4))


def layer_norm(nc, mem, out=None):
    with ExitStack() as ctx:
        sb, ps, sem = tools(nc, ctx)
        mv = mem["mv"]
        var, std, inv = sb("var", [P, NT]), sb("std", [P, NT]), sb("inv", [P, NT])
        bank = [ps(f"norm_ps{i}", [P, 512]) for i in range(4)]
        steps, var_in, std_in, normed = sem("ln_steps"), sem("var_in"), sem("std_in"), sem("normed")
        turned, copied, stored = sem("ln_turned"), sem("ln_copied"), sem("ln_stored")
        x, x_t, y, ident = mem["x_tok"], mem["x_t"], mem["y"], mem["ident"]
        block = ctx.enter_context(nc.Block())

        @block.vector
        def _(dve):
            step = Steps(dve, steps)
            dve.tensor_scalar(var[:, :], mv[:, :, 1], EPS, None, ALU.add).then_inc(var_in, 1)
            dve.wait_ge(std_in, 1)
            step(dve.reciprocal(inv[:, :], std[:, :]))
            for t in range(NT):
                dve.tensor_scalar(x[:, t, :], y[:, t, :], mv[:, t, 0:1], inv[:, t:t + 1],
                                  ALU.subtract, ALU.mult).then_inc(normed, 1)

        @block.scalar
        def _(act):
            act.wait_ge(var_in, 1)
            act.activation(std[:, :], var[:, :], ACT.Sqrt).then_inc(std_in, 1)
            if out is None:
                for c in range(NT // 4):
                    act.wait_ge(turned, c + 1)
                    act.copy(x_t[:, c * 512:(c + 1) * 512], bank[c][:, :]).then_inc(copied, 1)

        if out is None:
            @block.tensor
            def _(pe):
                for t in range(NT):
                    pe.wait_ge(normed, t + 1)
                    last = pe.transpose(bank[t // 4][:, t % 4 * P:t % 4 * P + P], x[:, t, :], ident[:, :])
                    if t % 4 == 3:
                        last.then_inc(turned, 1)
        else:
            @block.sync
            def _(sp):
                for c in range(4):
                    sp.wait_ge(normed, NT // 4 * (c + 1))
                    sp.dma_start(out.rearrange("b (t p) d -> p (b t) d", p=P)[:, 4 * c:4 * c + 4, :],
                                 x[:, 4 * c:4 * c + 4, :]).then_inc(stored, 16)
                sp.wait_ge(stored, 64)


E = 8
C0 = T // E
C1 = int(1.25 * T / E)
F0 = F1 = 512


def route(nc, mem, io, layer):
    K = 1 + layer
    cap = (C0, C1)[layer]
    rows = E * cap
    table, far = mem[f"slots{layer}"], float(4 * T)
    with ExitStack() as ctx:
        sb, ps, sem = tools(nc, ctx)

        def cube(name, dt=F32):
            return sb(name, [P, NT, E], dt)

        router = sb("router", [P, E])
        router_e = sb("router_e", [E, D])
        before, ones = sb("before", [P, P], BF16), sb("ones", [P, P], BF16)
        before_f = sb("before_f", [P, P])
        order, number = sb("order", [P, E]), sb("number", [P, E])
        logit, e_x, same, ranked, left = cube("logit"), cube("e_x"), cube("same"), cube("ranked"), cube("left")
        pick = [cube(f"pick{k}") for k in range(K)]
        picked_b = cube("picked_b", BF16)
        total, total2, place, prod = cube("total"), cube("total2"), cube("place"), cube("prod")
        kept = cube("kept")
        mx, mx2, denom, inv, prob1, prob2, tie = (sb(n, [P, NT]) for n in ("mx", "mx2", "denom", "inv", "prob1", "prob2", "tie"))
        slot, own, is_kept, at, out_at = (sb(n, [P, NT]) for n in ("slot", "own", "is_kept", "at", "out_at"))
        out_index = [sb(f"out_index{k}", [P, NT], I32) for k in range(K)]
        in_index, gate = mem["in_index"], mem["gate"]
        zeros = sb("zeros", [P, 512])
        weight, above = cube("weight"), cube("above", BF16)
        found, cand, more = sb("found", [P, E], I32), sb("cand", [P, E], I32), sb("more", [P, E], I32)
        count, room, fit = sb("count", [P, E], BF16), sb("room", [P, E]), cube("fit")
        logit_ps = ps("logit_ps", [P, NT, E])
        turn_ps = ps("turn_ps", [P, 512])
        place_ps, total_ps, count_ps = ps("place_ps", [P, NT, E]), ps("total_ps", [P, NT, E]), ps("count_ps", [P, 512])
        loaded, zeroed, set_up, routed, steps, exp_in, exped = (
            sem(n) for n in ("rt_loaded", "rt_zeroed", "rt_set", "rt_routed", "rt_steps", "rt_exp_in", "rt_exped"))
        cum_in, cum_out, count_in, count_out, index_in = (
            sem(n) for n in ("cum_in", "cum_out", "count_in", "count_out", "index_in"))
        sent = mem[f"sent{layer}"]
        turned = sem("rt_turned")
        x, x_t, ident = mem["x_tok"], mem["x_t"], mem["ident"]
        block = ctx.enter_context(nc.Block())

        @block.sync
        def _(sp):
            sp.dma_start(before_f[:, :], io["c_before"]).then_inc(loaded, 16)
            sp.dma_start(order[:, :], io["c_order"]).then_inc(loaded, 16)
            sp.dma_start(number[:, :], io["c_number"]).then_inc(loaded, 16)
            if layer == 0:
                sp.dma_start(router[:, :], io["L0_ffn_router_w"]).then_inc(loaded, 16)
            else:
                sp.dma_start(router_e[:, :], io["L1_ffn_router_w"]).then_inc(loaded, 16)
            sp.wait_ge(set_up, 1)
            for r in range(0, rows, 4 * P):
                sp.dma_start(table[r:r + 4 * P, :].rearrange("(p k) d -> p (k d)", k=4), zeros[:, :]).then_inc(zeroed, 16)
            sp.wait_ge(zeroed, 16 * (rows // (4 * P)))

        @block.tensor
        def _(pe):
            pe.wait_ge(loaded, 64)
            if layer == 1:
                pe.transpose(turn_ps[:, 0:E], router_e[:, :], ident[0:E, 0:E]).then_inc(turned, 1)
                pe.wait_ge(steps, 1)
            for t in range(NT):
                last = pe.matmul(logit_ps[:, t, :], x_t[:, t * P:(t + 1) * P], router[:, :], start=True, stop=True)
            last.then_inc(routed, 1)

            def cumulate(n):
                pe.wait_ge(cum_in, n + 1)
                pe.matmul(place_ps[:, :, :], before[:, :], picked_b[:, :, :], start=True, stop=True)
                pe.matmul(total_ps[:, :, :], ones[:, :], picked_b[:, :, :], start=True, stop=True).then_inc(cum_out, 1)

            if layer == 1:
                for n in range(BITS + 1):
                    pe.wait_ge(count_in, n + 1)
                    pe.matmul(count_ps[:, 0:E], ones[:, :], count[:, :], start=True, stop=True).then_inc(count_out, 1)
            for n in range(1 + layer):
                cumulate(n)

        @block.scalar
        def _(act):
            act.wait_ge(exp_in, 1)
            act.activation(e_x[:, :, :], left[:, :, :], ACT.Exp).then_inc(exped, 1)

        def wide(a):
            return a.unsqueeze(2).to_broadcast([P, NT, E])

        def tiles(a):
            return a.unsqueeze(1).to_broadcast([P, NT, E])

        @block.vector
        def _(dve):
            step = Steps(dve, steps)
            dve.wait_ge(loaded, 64)
            if layer == 1:
                dve.wait_ge(turned, 1)
                step(dve.tensor_copy(router[:, :], turn_ps[:, 0:E]))
            dve.memset(zeros[:, :], 0.0).then_inc(set_up, 1)
            step(dve.memset(ones[:, :], 1.0), dve.tensor_copy(before[:, :], before_f[:, :]))
            dve.wait_ge(routed, 1)
            step(dve.tensor_copy(logit[:, :, :], logit_ps[:, :, :]))
            step(dve.tensor_reduce(mx[:, :], logit[:, :, :], AX, ALU.max))
            dve.tensor_tensor(left[:, :, :], logit[:, :, :], wide(mx[:, :]), ALU.subtract).then_inc(exp_in, 1)
            dve.wait_ge(exped, 1)
            step(dve.tensor_reduce(denom[:, :], e_x[:, :, :], AX, ALU.add), dve.tensor_reduce(mx[:, :], e_x[:, :, :], AX, ALU.max))
            step(dve.reciprocal(inv[:, :], denom[:, :]))
            step(dve.tensor_tensor(prob1[:, :], mx[:, :], inv[:, :], ALU.mult))

            def first_of(values, top, to):
                step(dve.tensor_tensor(same[:, :, :], values, wide(top), ALU.is_equal))
                step(dve.tensor_tensor(ranked[:, :, :], same[:, :, :], tiles(order[:, :]), ALU.mult))
                step(dve.tensor_reduce(tie[:, :], ranked[:, :, :], AX, ALU.max))
                step(dve.tensor_tensor(to[:, :, :], ranked[:, :, :], wide(tie[:, :]), ALU.is_equal))

            first_of(e_x[:, :, :], mx[:, :], pick[0])
            if layer == 1:
                step(dve.scalar_tensor_tensor(left[:, :, :], pick[0][:, :, :], -2.0, e_x[:, :, :], ALU.mult, ALU.add))
                step(dve.tensor_reduce(mx2[:, :], left[:, :, :], AX, ALU.max))
                first_of(left[:, :, :], mx2[:, :], pick[1])
                step(dve.tensor_tensor(prob2[:, :], mx2[:, :], inv[:, :], ALU.mult))
                step(dve.tensor_tensor(denom[:, :], prob1[:, :], prob2[:, :], ALU.add))
                step(dve.tensor_scalar(denom[:, :], denom[:, :], 1e-6, None, ALU.add))
                step(dve.reciprocal(inv[:, :], denom[:, :]))
                step(dve.tensor_tensor(prob1[:, :], prob1[:, :], inv[:, :], ALU.mult),
                     dve.tensor_tensor(prob2[:, :], prob2[:, :], inv[:, :], ALU.mult))
                step(dve.tensor_tensor(prod[:, :, :], pick[0][:, :, :], wide(prob1[:, :]), ALU.mult),
                     dve.tensor_tensor(left[:, :, :], pick[1][:, :, :], wide(prob2[:, :]), ALU.mult),
                     dve.tensor_tensor(same[:, :, :], pick[0][:, :, :], pick[1][:, :, :], ALU.add))
                step(dve.tensor_tensor(weight[:, :, :], prod[:, :, :], left[:, :, :], ALU.add))
                step(dve.scalar_tensor_tensor(weight[:, :, :], same[:, :, :], -1.0, weight[:, :, :], ALU.add, ALU.add))
                step(dve.memset(found[:, :], 0))
                for n in range(BITS):
                    step(dve.tensor_scalar(cand[:, :], found[:, :], 1 << (BITS - 1 - n), None, ALU.bitwise_or))
                    step(dve.tensor_tensor(above[:, :, :], weight[:, :, :], tiles(cand[:, :].bitcast(F32)), ALU.is_ge))
                    with nc.allow_low_precision(reason="counts up to NT are exact"):
                        dve.tensor_reduce(count[:, :], above[:, :, :].rearrange("p t e -> p e t"), AX, ALU.add).then_inc(count_in, 1)
                    dve.wait_ge(count_out, n + 1)
                    step(dve.tensor_scalar(more[:, :], count_ps[:, 0:E], float(cap), None, ALU.is_ge))
                    step(dve.copy_predicated(found[:, :], more[:, :], cand[:, :]))
                bound = found[:, :].bitcast(F32)
                step(dve.tensor_tensor(above[:, :, :], weight[:, :, :], tiles(bound), ALU.is_gt),
                     dve.tensor_tensor(picked_b[:, :, :], weight[:, :, :], tiles(bound), ALU.is_equal))
                with nc.allow_low_precision(reason="counts up to NT are exact"):
                    dve.tensor_reduce(count[:, :], above[:, :, :].rearrange("p t e -> p e t"), AX, ALU.add).then_inc(count_in, 1)
                dve.wait_ge(count_out, BITS + 1)
                step(dve.tensor_scalar(room[:, :], count_ps[:, 0:E], -1.0, float(cap), ALU.mult, ALU.add))
            else:
                step(dve.tensor_copy(picked_b[:, :, :], pick[0][:, :, :]))

            def earlier(n):
                dve.sem_inc(cum_in, 1)
                dve.wait_ge(cum_out, n + 1)
                step(dve.memset(total[:, 0, :], 0.0), dve.tensor_copy(total[:, 1:NT, :], total_ps[:, 0:NT - 1, :]))
                a, b, d = total, total2, 1
                while d < NT:
                    step(dve.tensor_tensor(b[:, d:NT, :], a[:, d:NT, :], a[:, 0:NT - d, :], ALU.add),
                         dve.tensor_copy(b[:, 0:d, :], a[:, 0:d, :]))
                    a, b, d = b, a, 2 * d
                step(dve.tensor_tensor(place[:, :, :], a[:, :, :], place_ps[:, :, :], ALU.add))

            earlier(0)
            if layer == 1:
                step(dve.tensor_tensor(fit[:, :, :], place[:, :, :], tiles(room[:, :]), ALU.is_lt))
                step(dve.tensor_tensor(fit[:, :, :], fit[:, :, :], picked_b[:, :, :], ALU.mult))
                step(dve.tensor_tensor(kept[:, :, :], fit[:, :, :], above[:, :, :], ALU.add))
                step(dve.tensor_copy(picked_b[:, :, :], kept[:, :, :]))
                earlier(1)
            for k in range(K):
                step(dve.tensor_tensor(prod[:, :, :], pick[k][:, :, :], place[:, :, :], ALU.mult))
                step(dve.tensor_reduce(slot[:, :], prod[:, :, :], AX, ALU.add))
                step(dve.tensor_tensor(prod[:, :, :], pick[k][:, :, :], tiles(number[:, :]), ALU.mult))
                step(dve.tensor_reduce(own[:, :], prod[:, :, :], AX, ALU.add))
                if layer == 0:
                    step(dve.tensor_scalar(is_kept[:, :], slot[:, :], float(cap), None, ALU.is_lt))
                else:
                    step(dve.tensor_tensor(prod[:, :, :], pick[k][:, :, :], kept[:, :, :], ALU.mult))
                    step(dve.tensor_reduce(is_kept[:, :], prod[:, :, :], AX, ALU.add))
                step(dve.tensor_scalar(slot[:, :], slot[:, :], float(cap - 1), None, ALU.min))
                step(dve.scalar_tensor_tensor(at[:, :], own[:, :], float(cap), slot[:, :], ALU.mult, ALU.add))
                step(dve.tensor_scalar(out_at[:, :], is_kept[:, :], -far, far, ALU.mult, ALU.add))
                step(dve.tensor_tensor(out_at[:, :], out_at[:, :], at[:, :], ALU.add))
                step(dve.tensor_copy(out_index[k][:, :], out_at[:, :]),
                     dve.tensor_copy(in_index[:, k, :], at[:, :]),
                     dve.tensor_tensor(gate[:, k, :], (prob1, prob2)[k][:, :], is_kept[:, :], ALU.mult))
                dve.sem_inc(index_in, 1)

        @block.gpsimd
        def _(pool):
            pool.wait_ge(zeroed, 16 * (rows // (4 * P)))
            for k in range(K):
                pool.wait_ge(index_in, k + 1)
                for t in range(NT):
                    pool.indirect_dma_start(table[:, :], bass.IndirectOffsetOnAxis(out_index[k][:, t:t + 1], 0),
                                            x[:, t, :], None, bounds_check=rows - 1, oob_is_err=False).then_inc(sent, 16)
            pool.wait_ge(sent, 16 * NT * K)


BITS = 30


def expert_names(layer):
    return (("w1", "w2"), ("wg", "wu", "wd"))[layer]


def load_expert_weights(sp, mem, io, layer):
    names = expert_names(layer)
    up, down, loaded = mem[f"up_w{layer}"], mem[f"down_w{layer}"], mem[f"weights_in{layer}"]
    for j, name in enumerate(names[:-1]):
        sp.dma_start(up[:, j, :, :], io[f"L{layer}_ffn_{name}"].rearrange("e d f -> d e f")).then_inc(loaded, 16)
    sp.dma_start(down[:, :, :], io[f"L{layer}_ffn_{names[-1]}"].rearrange("e (c p) d -> p (e c) d", p=P)).then_inc(loaded, 16)


def experts(nc, mem, io, layer):
    cap = (C0, C1)[layer]
    F, FC = F0, F0 // P
    ups = len(expert_names(layer)) - 1
    tiles = E * cap // P
    chunks = tiles // 4
    pair_tiles = 2 * cap // P

    def pieces(e):
        at = e * cap
        while at < (e + 1) * cap:
            end = min((at // P + 1) * P, (e + 1) * cap)
            yield at // P, at % P, at % P + end - at
            at = end

    with ExitStack() as ctx:
        sb, ps, sem = tools(nc, ctx)
        rows_in, rows_t = sb("rows_in", [P, tiles, D]), sb("rows_t", [P, E * cap])
        hidden = [sb(f"hidden{i}", [P, FC, cap]) for i in range(2)]
        acted = sb("acted", [P, 2, cap])
        rows_out = sb("rows_out", [P, tiles, D])
        turn_ps = [ps(f"xturn_ps{i}", [P, 512]) for i in range(2)]
        up_ps = [[ps(f"up_ps{i}{j}", [P, 512]) for j in range(ups)] for i in range(2)]
        down_ps = [ps(f"down_ps{i}", [P, 3, D]) for i in range(2)]
        r_in = [sem(f"r_in{c}") for c in range(chunks)]
        turned, t_copied, upped, h_in, downed, out_in = (sem(n) for n in ("xturned", "t_copied", "upped", "h_in", "downed", "out_in"))
        acted_in, stored = sem("acted_in"), sem("r_stored")
        ident = mem["ident"]
        w_up, w_down = mem[f"up_w{layer}"], mem[f"down_w{layer}"]
        table, results = mem[f"slots{layer}"], mem[f"results{layer}"]
        block = ctx.enter_context(nc.Block())

        @block.sync
        def _(sp):
            for c in range(chunks):
                sp.dma_start(rows_in[:, 4 * c:4 * c + 4, :],
                             table[4 * c * P:(4 * c + 4) * P, :].rearrange("(k p) d -> p k d", p=P)).then_inc(r_in[c], 16)
            if layer == 0:
                load_linear_weights(sp, mem, io)
            for pair in range(E // 2):
                sp.wait_ge(out_in, 2 * pair + 2)
                a, b = pair * pair_tiles, (pair + 1) * pair_tiles
                sp.dma_start(results[a * P:b * P, :].rearrange("(k p) d -> p k d", p=P),
                             rows_out[:, a:b, :]).then_inc(stored, 16)
            sp.wait_ge(stored, E // 2 * 16)

        @block.tensor
        def _(pe):
            def turn(c):
                pe.wait_ge(r_in[c], 16)
                if c >= 2:
                    pe.wait_ge(t_copied, c - 1)
                for k in range(4):
                    last = pe.transpose(turn_ps[c % 2][:, k * P:(k + 1) * P], rows_in[:, 4 * c + k, :], ident[:, :])
                last.then_inc(turned, 1)

            def up(e, c):
                n = e * FC + c
                if c == 0:
                    pe.wait_ge(t_copied, -(-(e + 1) * cap // (4 * P)))
                if n >= 2:
                    pe.wait_ge(h_in, n - 1)
                for j in range(ups):
                    last = pe.matmul(up_ps[n % 2][j][:, 0:cap], w_up[:, j, e, c * P:(c + 1) * P],
                                     rows_t[:, e * cap:(e + 1) * cap], start=True, stop=True)
                last.then_inc(upped, 1)

            def down(e, k):
                found = list(pieces(e))
                if k < len(found):
                    tile, a, b = found[k]
                    at = tile * P + a - e * cap
                    if k == 0:
                        pe.wait_ge(h_in, (e + 1) * FC)
                        if e >= 2:
                            pe.wait_ge(out_in, e - 1)
                    for c in range(FC):
                        last = pe.matmul(down_ps[e % 2][a:b, k, :], hidden[e % 2][:, c, at:at + b - a],
                                         w_down[:, e * FC + c, :], start=(c == 0), stop=(c == FC - 1))
                    if k == len(found) - 1:
                        last.then_inc(downed, 1)

            turns = 0
            for e in range(E + 1):
                while turns < chunks and turns * 4 * P < (e + 2) * cap:
                    turn(turns)
                    turns += 1
                if e == 0:
                    pe.wait_ge(mem[f"weights_in{layer}"], (ups + 1) * 16)
                for c in range(FC):
                    if e < E:
                        up(e, c)
                    if e and c:
                        down(e - 1, c - 1)

        @block.scalar
        def _(act):
            for n in range(E * FC):
                e, c = n // FC, n % FC
                act.wait_ge(upped, n + 1)
                if layer == 0:
                    if c == 0 and e >= 2:
                        act.wait_ge(downed, e - 1)
                    act.activation(hidden[e % 2][:, c, :], up_ps[n % 2][0][:, 0:cap], ACT.Gelu_apprx_tanh).then_inc(h_in, 1)
                else:
                    if n >= 2:
                        act.wait_ge(h_in, n - 1)
                    act.activation(acted[:, n % 2, :], up_ps[n % 2][0][:, 0:cap], ACT.Silu).then_inc(acted_in, 1)

        @block.vector
        def _(dve):
            def rows(c):
                dve.wait_ge(turned, c + 1)
                dve.tensor_copy(rows_t[:, 4 * c * P:(4 * c + 4) * P], turn_ps[c % 2][:, :]).then_inc(t_copied, 1)

            def gates(e):
                for c in range(FC):
                    n = e * FC + c
                    dve.wait_ge(acted_in, n + 1)
                    if c == 0 and e >= 2:
                        dve.wait_ge(downed, e - 1)
                    dve.tensor_tensor(hidden[e % 2][:, c, :], acted[:, n % 2, :], up_ps[n % 2][1][:, 0:cap],
                                      ALU.mult).then_inc(h_in, 1)

            def results_out(e):
                dve.wait_ge(downed, e + 1)
                for k, (tile, a, b) in enumerate(pieces(e)):
                    last = dve.tensor_copy(rows_out[a:b, tile, :], down_ps[e % 2][a:b, k, :])
                last.then_inc(out_in, 1)

            turns = 0
            for e in range(E + 1):
                while turns < chunks and turns * 4 * P < (e + 2) * cap:
                    rows(turns)
                    turns += 1
                if e < E and layer == 1:
                    gates(e)
                if e:
                    results_out(e - 1)


def combine(nc, mem, io, layer):
    K = 1 + layer
    with ExitStack() as ctx:
        sb, ps, sem = tools(nc, ctx)
        got = [sb(f"got{k}", [P, NT, D]) for k in range(K)]
        gathered = mem[f"gathered{layer}"]
        summed, stat_steps = sem("summed"), sem("stat_steps")
        x, y, in_index, gate = mem["x_tok"], mem["y"], mem["in_index"], mem["gate"]
        folding = weight_folding(mem, sb, ps, sem) if layer == 0 else None
        block = ctx.enter_context(nc.Block())

        @block.gpsimd
        def _(pool):
            for t in range(NT):
                for k in range(K):
                    pool.indirect_dma_start(got[k][:, t, :], None, mem[f"results{layer}"][:, :],
                                            bass.IndirectOffsetOnAxis(in_index[:, k, t:t + 1], 0)).then_inc(gathered[t // 4], 16)

        @block.vector
        def _(dve):
            if folding:
                scale_output_weights(dve, mem, folding)
            step = Steps(dve, stat_steps)
            for c in range(NT // 4):
                dve.wait_ge(gathered[c], 4 * K * 16)
                for k in range(K):
                    for t in range(4 * c, 4 * c + 4):
                        last = dve.scalar_tensor_tensor(y[:, t, :], got[k][:, t, :], gate[:, k, t:t + 1],
                                                        (x, y)[k][:, t, :], ALU.mult, ALU.add)
                    last.then_inc(summed, 1)
                    dve.wait_ge(summed, K * c + k + 1)
                statistics(dve, mem, step, range(4 * c, 4 * c + 4))

        if folding:
            @block.tensor
            def _(pe):
                fold_weights_products(pe, mem, folding)

            @block.scalar
            def _(act):
                fold_weights_copies(act, mem, folding)


H1 = 8
NC1 = S // P


def rms_scale(dve, act_ready, step, x, square, mean, eps, var_in, std_in, std, inv):
    step(dve.tensor_tensor(square[:, :, :], x[:, :, :], x[:, :, :], ALU.mult))
    step(dve.tensor_reduce(mean[:, :], square[:, :, :], AX, ALU.add))
    dve.tensor_scalar(mean[:, :], mean[:, :], 1.0 / D, eps, ALU.mult, ALU.add).then_inc(var_in, 1)
    dve.wait_ge(std_in, act_ready)
    step(dve.reciprocal(inv[:, :], std[:, :]))


def rms_norm(nc, mem, io, weight, source):
    with ExitStack() as ctx:
        sb, ps, sem = tools(nc, ctx)
        w_row = sb("w_row", [P, D])
        square = sb("square", [P, NT, D])
        mean, std, inv = sb("mean", [P, NT]), sb("std", [P, NT]), sb("inv", [P, NT])
        bank = [ps(f"rms_ps{i}", [P, 512]) for i in range(4)]
        loaded, steps, var_in, std_in, normed, turned, copied = (
            sem(n) for n in ("rms_loaded", "rms_steps", "rms_var", "rms_std", "rms_normed", "rms_turned", "rms_copied"))
        x, h_tok, h_t, ident = mem[source], mem["h_tok"], mem["h_t"], mem["ident"]
        block = ctx.enter_context(nc.Block())

        @block.sync
        def _(sp):
            sp.dma_start(w_row[:, :], io[weight].rearrange("(a d) -> a d", a=1).to_broadcast([P, D])).then_inc(loaded, 16)
            sp.wait_ge(loaded, 16)

        @block.vector
        def _(dve):
            step = Steps(dve, steps)
            rms_scale(dve, 1, step, x, square, mean, EPS, var_in, std_in, std, inv)
            dve.wait_ge(loaded, 16)
            for t in range(NT):
                dve.scalar_tensor_tensor(h_tok[:, t, :], x[:, t, :], inv[:, t:t + 1], w_row[:, :],
                                         ALU.mult, ALU.mult).then_inc(normed, 1)

        @block.scalar
        def _(act):
            act.wait_ge(var_in, 1)
            act.activation(std[:, :], mean[:, :], ACT.Sqrt).then_inc(std_in, 1)
            for c in range(NT // 4):
                act.wait_ge(turned, c + 1)
                act.copy(h_t[:, c * 512:(c + 1) * 512], bank[c][:, :]).then_inc(copied, 1)

        @block.tensor
        def _(pe):
            for t in range(NT):
                pe.wait_ge(normed, t + 1)
                last = pe.transpose(bank[t // 4][:, t % 4 * P:t % 4 * P + P], h_tok[:, t, :], ident[:, :])
                if t % 4 == 3:
                    last.then_inc(turned, 1)


def load_linear_weights(sp, mem, io):
    loaded = mem["linear_in"]
    for n in "qkv":
        sp.dma_start(mem[f"w_{n}"][:, :, :], io["L1_attn_W" + n].rearrange("d (h e) -> d h e", h=H1)).then_inc(loaded, 16)
    sp.dma_start(mem["w_o"][:, :, :], io["L1_attn_Wo"].rearrange("(h e) d -> e h d", h=H1)).then_inc(loaded, 16)
    sp.dma_start(mem["norm_w"][:, :], io["L1_attn_attn_out_norm_w"].rearrange("(d a) -> d a", a=1)).then_inc(loaded, 16)


def weight_folding(mem, sb, ps, sem):
    fold = {n: sem("lw_" + n) for n in ("scaled", "turned", "t_copied", "folded", "f_copied")}
    fold["turned_w"] = sb("turned_w", [P, 2, 3, P])
    fold["turn_ps"] = [ps(f"wturn_ps{i}", [P, 3, P]) for i in range(2)]
    fold["fold_ps"] = [ps(f"fold_ps{i}", [P, 2, D]) for i in range(2)]
    return fold


def scale_output_weights(dve, mem, fold):
    dve.wait_ge(mem["linear_in"], 80)
    w_o = mem["w_o"]
    dve.tensor_scalar(w_o[:, :, :], w_o[:, :, :], mem["norm_w"][:, 0:1], None, ALU.mult).then_inc(fold["scaled"], 1)


def fold_weights_products(pe, mem, fold):
    turn_ps, fold_ps, turned_w = fold["turn_ps"], fold["fold_ps"], fold["turned_w"]
    pe.wait_ge(mem["linear_in"], 80)
    for h in range(H1 + 1):
        if h < H1:
            if h >= 2:
                pe.wait_ge(fold["t_copied"], h - 1)
            for k, n in enumerate("qkv"):
                last = pe.transpose(turn_ps[h % 2][:, k, :], mem[f"w_{n}"][:, h, :], mem["ident"][:, :])
            last.then_inc(fold["turned"], 1)
        if h:
            g = h - 1
            pe.wait_ge(fold["t_copied"], g + 1)
            pe.wait_ge(fold["scaled"], 1)
            if g >= 2:
                pe.wait_ge(fold["f_copied"], g - 1)
            pe.matmul(fold_ps[g % 2][:, 0, :], turned_w[:, g % 2, 0, :], turned_w[:, g % 2, 1, :], start=True, stop=True)
            pe.matmul(fold_ps[g % 2][:, 1, :], turned_w[:, g % 2, 2, :], mem["w_o"][:, g, :],
                      start=True, stop=True).then_inc(fold["folded"], 1)


def fold_weights_copies(act, mem, fold):
    a_w, vm_w = mem["a_w"], mem["vm_w"]
    for h in range(H1 + 1):
        if h < H1:
            act.wait_ge(fold["turned"], h + 1)
            if h >= 2:
                act.wait_ge(fold["folded"], h - 1)
            act.copy(fold["turned_w"][:, h % 2, :, :], fold["turn_ps"][h % 2][:, :, :]).then_inc(fold["t_copied"], 1)
        if h:
            g = h - 1
            act.wait_ge(fold["folded"], g + 1)
            act.copy(a_w[:, g, :], fold["fold_ps"][g % 2][:, 0, :])
            act.copy(vm_w[:, g, 0:D], mem["w_v"][:, g, :])
            act.copy(vm_w[:, g, D:2 * D], fold["fold_ps"][g % 2][:, 1, :]).then_inc(fold["f_copied"], 1)


def linear_attention(nc, mem, io):
    with ExitStack() as ctx:
        sb, ps, sem = tools(nc, ctx)
        chunk_t = [sb(f"chunk_t{i}", [P, P]) for i in range(2)]
        chunk_k = [sb(f"chunk_k{i}", [P, D]) for i in range(2)]
        sums = [sb(f"sums{i}", [P, D]) for i in range(2)]
        query = sb("query", [P, H1, P])
        scores = sb("scores", [P, H1, P])
        mixed = sb("mixed", [P, H1, P])
        causal = sb("causal", [P, P])
        squares = sb("squares", [P, H1, D])
        mean, std, inv = sb("o_mean", [P, 2, H1]), sb("o_std", [P, 2, H1]), sb("o_inv", [P, 2, H1])
        heads = sb("heads", [P, H1, D])
        total = sb("heads_sum", [P, D])
        work = [ps(f"work{i}", [P, 4, P]) for i in range(4)]
        outs = [ps(f"outs{i}", [P, 2, 2 * D]) for i in range(4)]
        loaded, set_up, staged = sem("la_loaded"), sem("la_set"), sem("staged")
        q_done, q_copied, s_done, s_copied = sem("q_done"), sem("q_copied"), sem("s_done"), sem("s_copied")
        m_done, m_copied, g_done, g_copied = sem("m_done"), sem("m_copied"), sem("g_done"), sem("g_copied")
        o_done, squared, steps, root_in, root_out, scaled, y_in = (
            sem(n) for n in ("la_o", "squared", "la_steps", "root_in", "root_out", "la_scaled", "y_in"))
        x, y, h_t, h_tok, a_w, vm_w = (mem[n] for n in ("x_tok", "y", "h_t", "h_tok", "a_w", "vm_w"))
        block = ctx.enter_context(nc.Block())
        HH = H1 // 2

        STEPS = 4

        def summed_at(n):
            return n * STEPS + 1

        @block.sync
        def _(sp):
            sp.dma_start(causal[:, :], io["c_causal"]).then_inc(loaded, 16)
            sp.dma_start(mem["w_gate"][:, :], io["L1_attn_Wgate"]).then_inc(mem["mlp_in"], 16)
            sp.dma_start(mem["w_up"][:, :], io["L1_attn_Wup"]).then_inc(mem["mlp_in"], 16)
            sp.dma_start(mem["w_down"][:, :, :], io["L1_attn_Wdown"].rearrange("(c p) d -> p c d", p=P)).then_inc(mem["mlp_in"], 16)
            load_expert_weights(sp, mem, io, 1)
            sp.wait_ge(loaded, 16)

        @block.gpsimd
        def _(pool):
            for n in range(NT):
                c = n % 2
                if n >= 2:
                    pool.wait_ge(o_done, n - 1)
                pool.tensor_copy(chunk_t[c][:, :], h_t[:, n * P:(n + 1) * P]).then_inc(staged, 1)
                pool.tensor_copy(chunk_k[c][:, :], h_tok[:, n, :]).then_inc(staged, 1)

        @block.tensor
        def _(pe):
            def queries(n):
                for h in range(H1):
                    if h % HH == 0 and n:
                        pe.wait_ge(m_copied, 2 * (n - 1) + h // HH + 1)
                    last = pe.matmul(work[h // HH][:, h % HH, :], a_w[:, h, :], h_t[:, n * P:(n + 1) * P], start=True, stop=True)
                    if h % HH == HH - 1:
                        last.then_inc(q_done, 1)

            def attend(n):
                c = n % 2
                pe.wait_ge(staged, 2 * n + 2)
                for half in range(2):
                    pe.wait_ge(q_copied, 2 * n + half + 1)
                    if n:
                        pe.wait_ge(g_copied, n)
                    pe.matmul(work[2 + half][:, :, :], chunk_t[c][:, :], query[:, half * HH:(half + 1) * HH, :],
                              start=True, stop=True).then_inc(s_done, 1)

            def mix(n):
                c = n % 2
                for half in range(2):
                    pe.wait_ge(s_copied, 2 * n + half + 1)
                    first = n % NC1 == 0
                    last = pe.matmul(work[half][:, :, :], chunk_k[c][:, :], scores[:, half * HH:(half + 1) * HH, :],
                                     start=True, stop=first)
                    if not first:
                        pe.wait_ge(g_copied, n)
                        last = pe.matmul(work[half][:, :, :], sums[(n - 1) % 2][:, :], query[:, half * HH:(half + 1) * HH, :],
                                         start=False, stop=True)
                    last.then_inc(m_done, 1)

            def gather(n):
                pe.wait_ge(s_copied, 2 * n + 1)
                pe.matmul(work[2][:, 0, :], chunk_k[n % 2][:, :], chunk_k[n % 2][:, :], start=True, stop=True).then_inc(g_done, 1)

            def project(n):
                for h in range(H1):
                    if h % HH == 0:
                        pe.wait_ge(m_copied, 2 * n + h // HH + 1)
                        if n:
                            pe.wait_ge(scaled, n)
                            pe.wait_ge(squared, n)
                    last = pe.matmul(outs[h // 2][:, h % 2, :], mixed[:, h, :], vm_w[:, h, :], start=True, stop=True)
                last.then_inc(o_done, 1)

            for n in range(NT):
                queries(n)
                if n:
                    project(n - 1)
                attend(n)
                gather(n)
                mix(n)
            project(NT - 1)

        @block.scalar
        def _(act):
            def root(n):
                act.wait_ge(root_in, n + 1)
                act.activation(std[:, n % 2, :], mean[:, n % 2, :], ACT.Sqrt).then_inc(root_out, 1)

            for n in range(NT):
                for half in range(2):
                    act.wait_ge(q_done, 2 * n + half + 1)
                    if n:
                        act.wait_ge(m_done, 2 * (n - 1) + half + 1)
                    act.copy(query[:, half * HH:(half + 1) * HH, :], work[half][:, :, :]).then_inc(q_copied, 1)
                if n:
                    act.wait_ge(o_done, n)
                    if n > 1:
                        act.wait_ge(steps, summed_at(n - 2))
                    for k in range(4):
                        last = act.activation(squares[:, 2 * k:2 * k + 2, :], outs[k][:, :, 0:D], ACT.Square)
                    last.then_inc(squared, 1)
                for half in range(2):
                    act.wait_ge(m_done, 2 * n + half + 1)
                    if n:
                        act.wait_ge(o_done, n)
                    act.copy(mixed[:, half * HH:(half + 1) * HH, :], work[half][:, :, :]).then_inc(m_copied, 1)
                if n:
                    root(n - 1)
            act.wait_ge(o_done, NT)
            act.wait_ge(steps, summed_at(NT - 2))
            for k in range(4):
                last = act.activation(squares[:, 2 * k:2 * k + 2, :], outs[k][:, :, 0:D], ACT.Square)
            last.then_inc(squared, 1)
            root(NT - 1)

        @block.vector
        def _(dve):
            step = Steps(dve, steps)
            dve.wait_ge(loaded, 16)

            def mask(n):
                for half in range(2):
                    dve.wait_ge(s_done, 2 * n + half + 1)
                    if n:
                        dve.wait_ge(m_done, 2 * (n - 1) + half + 1)
                    dve.tensor_tensor(scores[:, half * HH:(half + 1) * HH, :], work[2 + half][:, :, :],
                                      causal[:, :].unsqueeze(1).to_broadcast([P, HH, P]), ALU.mult).then_inc(s_copied, 1)

            def add_up(n):
                dve.wait_ge(g_done, n + 1)
                if n:
                    dve.wait_ge(m_done, 2 * n)
                if n % NC1 == 0:
                    dve.tensor_copy(sums[n % 2][:, :], work[2][:, 0, :]).then_inc(g_copied, 1)
                else:
                    dve.wait_ge(g_copied, n)
                    dve.tensor_tensor(sums[n % 2][:, :], sums[(n - 1) % 2][:, :], work[2][:, 0, :], ALU.add).then_inc(g_copied, 1)

            def finish(n):
                dve.wait_ge(squared, n + 1)
                step(dve.tensor_reduce(mean[:, n % 2, :], squares[:, :, :], AX, ALU.add))
                dve.tensor_scalar(mean[:, n % 2, :], mean[:, n % 2, :], 1.0 / P, EPS, ALU.mult, ALU.add).then_inc(root_in, 1)
                dve.wait_ge(root_out, n + 1)
                step(dve.reciprocal(inv[:, n % 2, :], std[:, n % 2, :]))
                for k in range(4):
                    last = dve.tensor_tensor(heads[:, 2 * k:2 * k + 2, :], outs[k][:, :, D:2 * D],
                                             inv[:, n % 2, 2 * k:2 * k + 2].unsqueeze(2).to_broadcast([P, 2, D]), ALU.mult)
                last.then_inc(scaled, 1)
                dve.wait_ge(scaled, n + 1)
                step(dve.tensor_reduce(total[:, :], heads[:, :, :].rearrange("p h d -> p d h"), AX, ALU.add))
                step(dve.tensor_tensor(y[:, n, :], total[:, :], x[:, n, :], ALU.add))

            for n in range(NT):
                mask(n)
                add_up(n)
                if n:
                    finish(n - 1)
            finish(NT - 1)


def gated_mlp(nc, mem, io):
    FC = F0 // P
    with ExitStack() as ctx:
        sb, ps, sem = tools(nc, ctx)
        w_gate, w_up, w_down = mem["w_gate"], mem["w_up"], mem["w_down"]
        acted, hidden = sb("acted1", [P, 2, 512]), sb("hidden1", [P, 2, FC, 512])
        up_ps = [[ps(f"gu_ps{i}{j}", [P, 512]) for j in range(2)] for i in range(2)]
        down_ps = [ps(f"dn_ps{i}", [P, 4, D]) for i in range(2)]
        upped, acted_in, h_in, downed, added = (sem(n) for n in ("m_upped", "m_acted", "m_h", "m_downed", "m_added"))
        stat_steps = sem("stat_steps")
        x, y, h_t = mem["x_tok"], mem["y"], mem["h_t"]
        around = sem("m_around")
        block = ctx.enter_context(nc.Block())
        NB = T // 512

        @block.tensor
        def _(pe):
            pe.wait_ge(mem["mlp_in"], 48)

            def down(b):
                pe.wait_ge(h_in, (b + 1) * FC)
                if b >= 2:
                    pe.wait_ge(added, b - 1)
                for k in range(4):
                    for c in range(FC):
                        last = pe.matmul(down_ps[b % 2][:, k, :], hidden[:, b % 2, c, k * P:(k + 1) * P], w_down[:, c, :],
                                         start=(c == 0), stop=(c == FC - 1))
                last.then_inc(downed, 1)

            for b in range(NB):
                for c in range(FC):
                    n = b * FC + c
                    if n >= 2:
                        pe.wait_ge(h_in, n - 1)
                    for j, w in enumerate((w_gate, w_up)):
                        last = pe.matmul(up_ps[n % 2][j][:, :], w[:, c * P:(c + 1) * P], h_t[:, b * 512:(b + 1) * 512],
                                         start=True, stop=True)
                    last.then_inc(upped, 1)
                if b:
                    down(b - 1)
            down(NB - 1)

        @block.scalar
        def _(act):
            for n in range(NB * FC):
                act.wait_ge(upped, n + 1)
                if n >= 2:
                    act.wait_ge(h_in, n - 1)
                act.activation(acted[:, n % 2, :], up_ps[n % 2][0][:, :], ACT.Silu).then_inc(acted_in, 1)

        @block.vector
        def _(dve):
            step = Steps(dve, stat_steps)
            dve.tensor_tensor(y[:, :, :], y[:, :, :], x[:, :, :], ALU.add).then_inc(around, 1)
            dve.wait_ge(around, 1)
            for b in range(NB + 1):
                if b < NB:
                    for c in range(FC):
                        n = b * FC + c
                        dve.wait_ge(acted_in, n + 1)
                        if b >= 2:
                            dve.wait_ge(downed, b - 1)
                        dve.tensor_tensor(hidden[:, b % 2, c, :], acted[:, n % 2, :], up_ps[n % 2][1][:, :], ALU.mult).then_inc(h_in, 1)
                if b:
                    dve.wait_ge(downed, b)
                    dve.tensor_tensor(y[:, 4 * b - 4:4 * b, :], y[:, 4 * b - 4:4 * b, :], down_ps[(b - 1) % 2][:, :, :], ALU.add).then_inc(added, 1)
                    dve.wait_ge(added, b)
                    statistics(dve, mem, step, range(4 * b - 4, 4 * b))


def two_layers(nc, io, out):
    with ExitStack() as ctx:
        sb, ps, sem = tools(nc, ctx, last=True)
        mem = {
            "x_tok": sb("x_tok", [P, NT, D]), "x_t": sb("x_t", [P, T]), "ident": sb("ident", [P, P]),
            "y": sb("y", [P, NT, D]), "in_index": sb("in_index", [P, 2, NT], I32), "gate": sb("gate", [P, 2, NT]),
            "clamps": sb("clamps", [1, 1], I32),
            "slots0": nc.dram_tensor("slots0", (E * C0, D), F32, kind="Internal").ap(),
            "slots1": nc.dram_tensor("slots1", (E * C1, D), F32, kind="Internal").ap(),
            "results0": nc.dram_tensor("results0", (E * C0, D), F32, kind="Internal").ap(),
            "results1": nc.dram_tensor("results1", (E * C1, D), F32, kind="Internal").ap(),
        }
        for i in range(2):
            mem[f"sent{i}"] = sem(f"sent{i}")
            mem[f"gathered{i}"] = [sem(f"gathered{i}_{c}") for c in range(NT // 4)]
        dram = {"parts": nc.dram_tensor("parts_dram", (2, 2, NG, NPART, HD, GH, S), BF16, kind="Internal").ap()}
        for i in range(2):
            mem[f"weights_in{i}"] = sem(f"weights_in{i}")
        mem["linear_in"], mem["mlp_in"] = sem("linear_in"), sem("mlp_in")
        mem.update(stats=sb("stats", [P, NT, 6]), mv=sb("mv", [P, NT, 2]))
        with ExitStack() as layer:
            sb, ps, sem = tools(nc, layer)
            mem.update(v_src=sb("v_src", [P, NG, SB, 32]), o_src=sb("o_src", [P, NG, SB, 32]), rest=sb("rest", [P, 2 * S - P]))
            attention_setup(nc, mem, dram, io)
            attention_scores(nc, mem, dram)
            attention_general(nc, mem, dram, io)
            mem.update(up_w0=sb("up_w0", [P, 1, E, F0]), down_w0=sb("down_w0", [P, E * F0 // P, D]))
            mem.update({f"w_{n}": sb(f"w_{n}", [P, H1, P]) for n in "qkvo"}, norm_w=sb("norm_w", [P, 1]))
            attention_output(nc, mem, io)
            layer_norm(nc, mem)
            route(nc, mem, io, 0)
            experts(nc, mem, io, 0)
            mem.update(a_w=sb("a_w", [P, H1, D]), vm_w=sb("vm_w", [P, H1, 2 * D]))
            combine(nc, mem, io, 0)
            layer_norm(nc, mem)
            mem.update(up_w1=sb("up_w1", [P, 2, E, F0]), down_w1=sb("down_w1", [P, E * F0 // P, D]))
            with ExitStack() as linear:
                sb, ps, sem = tools(nc, linear)
                mem.update(h_tok=sb("h_tok", [P, NT, D]), h_t=sb("h_t", [P, T]))
                mem.update(w_gate=sb("w_gate", [P, F0]), w_up=sb("w_up", [P, F0]), w_down=sb("w_down", [P, F0 // P, D]))
                rms_norm(nc, mem, io, "L1_attn_attn_norm_w", "x_tok")
                linear_attention(nc, mem, io)
                rms_norm(nc, mem, io, "L1_attn_mlp_norm_w", "y")
                gated_mlp(nc, mem, io)
            layer_norm(nc, mem)
            route(nc, mem, io, 1)
            experts(nc, mem, io, 1)
            combine(nc, mem, io, 1)
            layer_norm(nc, mem, out)


def kernel(**inputs):
    import numpy as _np
    import concourse.bacc as _bacc
    from concourse import mybir as _mybir
    from concourse.bass_utils import run_bass_kernel_spmd as _run

    nc = _bacc.Bacc("TRN2", target_bir_lowering=False, num_devices=1)
    arrays, io = {}, {}
    for name, value in {**inputs, **host_constants()}.items():
        a = _np.ascontiguousarray(value)
        arrays[f"in_{name}_dram"] = a
        io[name] = nc.dram_tensor(f"in_{name}_dram", a.shape, _mybir.dt.from_np(a.dtype), kind="ExternalInput").ap()
    out = nc.dram_tensor("out_0_dram", (B, S, D), _mybir.dt.float32, kind="ExternalOutput").ap()
    two_layers(nc, io, out)
    r = _run(nc, [arrays], core_ids=[0])
    return r.results[0]["out_0_dram"]
```

```python
from contextlib import ExitStack

import numpy as np

import concourse.bass as bass
from concourse import mybir

ALU = mybir.AluOpType
ACT = mybir.ActivationFunctionType
AX = mybir.AxisListType.X
F32 = mybir.dt.float32
BF16 = mybir.dt.bfloat16
I32 = mybir.dt.int32

P = 128
B, S, D = 2, 1024, 128
T = B * S
NT = T // P
SB = S // P
EPS = 1e-5

H0, HD = 16, 8
GH = 4
NG = B * H0 // GH
LAT = 32
SCALE0 = 1.0 / (np.sqrt(np.float32(D)) + np.float32(1e-8))
CLAMP = 10000.0
DECAY = 0.01 * 0.01
NPART = 3
KR = NPART * NPART * HD
KX = KR + NPART


TWO_ONES = float(np.array([0x3F803F80], np.uint32).view(np.float32)[0])


def load_stack(sp, dram, stack, group, half, loaded):
    for a in range(NPART):
        sp.dma_start(stack[a * NPART * HD:(a + 1) * NPART * HD, half, 0, :, :],
                     dram["parts"][0, half, group, a, :, :, :].unsqueeze(0).to_broadcast([NPART, HD, GH, S])
                     ).then_inc(loaded, 16)
    keys = dram["parts"][1, half, group, :, :, :, :].rearrange("k r h t -> (k r) h t")
    sp.dma_start(stack[0:KR, half, 1, :, :], keys.unsqueeze(0).to_broadcast([NPART, NPART * HD, GH, S])).then_inc(loaded, 16)


def host_constants():
    i = np.arange(S, dtype=np.float32)
    p = np.arange(P)
    c = np.float32(-DECAY)
    ramp = np.stack([np.exp(c * i), np.exp(-c * i)]).astype(np.float32)
    u = np.arange(2 * S - P)[None, :] - (S - P) - p[:, None]
    bound = (np.float32(CLAMP) * np.exp(-c * u.astype(np.float32))).astype(np.float32)
    rest = np.where(u > 0, np.exp(2 * c * u.astype(np.float32)), 1.0).astype(np.float32)
    ident = np.eye(P, dtype=np.float32)
    before = (p[:, None] < p[None, :]).astype(np.float32)
    return {
        "c_ramp": np.ascontiguousarray(np.broadcast_to(ramp[None], (P, 2, S))),
        "c_bound": bound, "c_rest": rest, "c_ident": ident, "c_before": before,
        "c_causal": (p[:, None] <= p[None, :]).astype(np.float32),
        "c_order": np.ascontiguousarray(np.broadcast_to(np.arange(E, 0, -1, dtype=np.float32), (P, E))),
        "c_token": (np.arange(NT, dtype=np.int32)[None, :] * P + p[:, None].astype(np.int32)),
        "c_number": np.ascontiguousarray(np.broadcast_to(np.arange(E, dtype=np.float32), (P, E))),
    }


def attention_setup(nc, mem, dram, io):
    with ExitStack() as ctx:
        sb, ps, sem = tools(nc, ctx)
        wq, wk, wv = (sb(n, [P, D]) for n in ("wq", "wk", "wv"))
        wd, wu = sb("wd", [P, LAT]), sb("wu", [LAT, 2, D])
        wkv, wkv_t, l_t = sb("wkv", [P, D]), sb("wkv_t", [P, D]), sb("l_t", [LAT, P])
        w_qk, w_val = sb("w_qk", [P, 2, D]), sb("w_val", [P, D])
        ramp = sb("ramp", [P, 2, S])
        raw = sb("raw", [P, 2, T])
        full = sb("full", [P, 2, T])
        left = sb("left", [P, 2, T])
        parts = sb("parts", [P, 4, NPART, T], BF16)
        ones, extent, limits = sb("ones", [P, 1]), sb("extent", [P, 4]), sb("limits", [1, 8])
        bank = [ps(f"setup{i}", [P, 512]) for i in range(8)]
        x_in = [sem(f"x_in{c}") for c in range(2)]
        weights_in, ramp_in, later_in = sem("weights_in"), sem("ramp_in"), sem("later_in")
        transposed, x_copied, folded, fold_copied = sem("transposed"), sem("x_copied"), sem("folded"), sem("fold_copied")
        kv_summed, q_ordered = sem("kv_summed"), sem("q_ordered")
        projected, raw_copied, valued, v_copied = sem("projected"), sem("raw_copied"), sem("valued"), sem("v_copied")
        scaled, part0, left1, part1, part2, stored = (sem(n) for n in ("scaled", "part0", "left1", "part1", "part2", "stored"))
        ones_in, squared, reached, summed, judged = (sem(n) for n in ("ones_in", "squared", "reached", "summed", "judged"))
        first_stored, rows_set, first_in = sem("first_stored"), sem("rows_set"), sem("first_in")
        stack0 = mem["stack0"]
        x_tok, x_t, ident, v_src = mem["x_tok"], mem["x_t"], mem["ident"], mem["v_src"]
        block = ctx.enter_context(nc.Block())
        x_view = io["L0_attn_x"].rearrange("b (t p) d -> p (b t) d", p=P)

        def by_feature(w):
            return w.rearrange("p (g h r) -> p g r h", g=NG // B, h=GH)

        @block.sync
        def _(sp):
            sp.dma_start(ident[:, :], io["c_ident"]).then_inc(x_in[0], 16)
            sp.dma_start(x_tok[:, 0:NT // 2, :], x_view[:, 0:NT // 2, :]).then_inc(x_in[0], 16)
            sp.dma_start(wq[:, :], io["L0_attn_Wq"]).then_inc(weights_in, 16)
            sp.dma_start(wk[:, :], io["L0_attn_Wk"]).then_inc(weights_in, 16)
            sp.dma_start(wv[:, :], io["L0_attn_Wv"]).then_inc(weights_in, 16)
            sp.dma_start(x_tok[:, NT // 2:NT, :], x_view[:, NT // 2:NT, :]).then_inc(x_in[1], 16)
            for n in range(4):
                for k in range(NPART):
                    sp.wait_ge((part0, part1, part2)[k], n + 1)
                    for b in range(B):
                        sp.dma_start(
                            dram["parts"][n % 2, n // 2, b * (NG // B):(b + 1) * (NG // B), k, :, :, :].rearrange(
                                "g r h t -> g (r h) t"),
                            parts[:, n, k, b * S:(b + 1) * S]).then_inc(first_stored if n < 2 else stored, 16)
                if n == 1:
                    sp.wait_ge(first_stored, 2 * NPART * B * 16)
                    sp.wait_ge(rows_set, 1)
                    load_stack(sp, dram, stack0, 0, 0, first_in)
            sp.wait_ge(stored, 2 * NPART * B * 16)
            sp.wait_ge(first_in, (NPART + 1) * 16)
            sp.wait_ge(later_in, 16)

        @block.tensor
        def _(pe):
            for t in range(NT):
                if t % (NT // 2) == 0:
                    pe.wait_ge(x_in[0], 32)
                    if t:
                        pe.wait_ge(x_in[1], 16)
                last = pe.transpose(bank[t // 4][:, t % 4 * P:t % 4 * P + P], x_tok[:, t, :], ident[:, :])
                if t % 4 == 3:
                    last.then_inc(transposed, 1)
            pe.wait_ge(kv_summed, 1)
            pe.transpose(bank[4][:, 0:P], wkv[:, :], ident[:, :]).then_inc(folded, 1)
            pe.wait_ge(q_ordered, 1)
            for c in range(4):
                pe.wait_ge(x_copied, c + 1)
                pe.matmul(bank[c][:, :], w_qk[:, 0, :], x_t[:, c * 512:(c + 1) * 512],
                          start=True, stop=True).then_inc(projected, 1)
            pe.wait_ge(fold_copied, 1)
            pe.matmul(bank[5][0:LAT, 0:P], wd[:, :], wkv_t[:, :], start=True, stop=True).then_inc(folded, 1)
            pe.wait_ge(fold_copied, 2)
            pe.matmul(bank[6][:, 0:2 * D], l_t[:, :], wu[:, :, :], start=True, stop=True).then_inc(folded, 1)
            pe.wait_ge(fold_copied, 4)
            for c in range(4):
                pe.matmul(bank[4 + c][:, :], w_qk[:, 1, :], x_t[:, c * 512:(c + 1) * 512],
                          start=True, stop=True).then_inc(projected, 1)
            for t in range(NT):
                if t % 4 == 0:
                    pe.wait_ge(raw_copied, t // 4 + 1)
                last = pe.matmul(bank[t // 4][:, t % 4 * P:t % 4 * P + P], x_t[:, t * P:(t + 1) * P],
                                 w_val[:, :], start=True, stop=True)
                if t % 4 == 3:
                    last.then_inc(valued, 1)
            pe.wait_ge(reached, 2)
            pe.wait_ge(squared, 2)
            pe.wait_ge(raw_copied, 5)
            pe.matmul(bank[4][0:1, 0:4], ones[:, :], extent[:, :], start=True, stop=True).then_inc(summed, 1)

        @block.scalar
        def _(act):
            act.dma_start(wd[:, :], io["L0_attn_W_down_kv"]).then_inc(weights_in, 16)
            act.dma_start(wu[:, 0, :], io["L0_attn_W_up_k"]).then_inc(weights_in, 16)
            act.dma_start(wu[:, 1, :], io["L0_attn_W_up_v"]).then_inc(weights_in, 16)
            act.dma_start(ramp[:, :, :], io["c_ramp"]).then_inc(ramp_in, 16)
            act.dma_start(mem["rest"][:, :], io["c_rest"]).then_inc(later_in, 16)
            for c in range(4):
                act.wait_ge(transposed, c + 1)
                act.copy(x_t[:, c * 512:(c + 1) * 512], bank[c][:, :]).then_inc(x_copied, 1)
            for n in range(2):
                for c in range(4):
                    act.wait_ge(projected, 4 * n + c + 1)
                    act.activation(raw[:, n, c * 512:(c + 1) * 512], bank[4 * n + c][:, :], ACT.Copy,
                                   scale=float(SCALE0) if n == 0 else 1.0).then_inc(raw_copied, 1)

            def first_part(n):
                act.wait_ge(scaled, 2 * n + 2)
                act.copy(parts[:, n, 0, :], full[:, n % 2, :]).then_inc(part0, 1)

            def second_part(n):
                act.wait_ge(left1, n + 1)
                act.copy(parts[:, n, 1, :], left[:, n % 2, :]).then_inc(part1, 1)

            first_part(0)
            first_part(1)
            second_part(0)
            second_part(1)
            for t in range(NT):
                if t % 4 == 0:
                    act.wait_ge(valued, t // 4 + 1)
                last = act.copy(
                    v_src[:, t // SB * (NG // B):(t // SB + 1) * (NG // B), t % SB, :],
                    bank[t // 4][:, t % 4 * P:t % 4 * P + P].rearrange("p (g r) -> p g r", r=GH * HD))
            last.then_inc(v_copied, 1)
            first_part(2)
            first_part(3)
            second_part(2)
            second_part(3)
            for n in range(2):
                act.wait_ge(part0, 4)
                act.wait_ge(left1, 4)
                act.activation(full[:, n, :], raw[:, n, :], ACT.Square, accum_out=extent[:, 2 + n:3 + n]).then_inc(squared, 1)

        @block.gpsimd
        def _(pool):
            pool.memset(stack0[64:96, :, 1, :, :].bitcast(F32), TWO_ONES).then_inc(rows_set, 1)

        @block.vector
        def _(dve):
            dve.memset(ones[:, :], 1.0).then_inc(ones_in, 1)
            dve.wait_ge(weights_in, 6 * 16)
            dve.tensor_tensor(wkv[:, :], wk[:, :], wv[:, :], ALU.add).then_inc(kv_summed, 1)
            dve.tensor_copy(w_qk[:, 0, :].rearrange("p (g r h) -> p g r h", g=NG // B, r=HD), by_feature(wq[:, :])).then_inc(q_ordered, 1)
            dve.wait_ge(folded, 1)
            dve.tensor_copy(wkv_t[:, :], bank[4][:, 0:P]).then_inc(fold_copied, 1)
            dve.wait_ge(folded, 2)
            dve.tensor_copy(l_t[:, :], bank[5][0:LAT, 0:P]).then_inc(fold_copied, 1)
            dve.wait_ge(folded, 3)
            dve.tensor_copy(w_qk[:, 1, :].rearrange("p (g r h) -> p g r h", g=NG // B, r=HD),
                            by_feature(bank[6][:, 0:D])).then_inc(fold_copied, 1)
            dve.tensor_copy(w_val[:, :], bank[6][:, D:2 * D]).then_inc(fold_copied, 1)
            dve.wait_ge(ramp_in, 16)

            def scale(n):
                dve.wait_ge(raw_copied, 4 * (n % 2 + 1))
                if n >= 2:
                    dve.wait_ge(part0, n - 1)
                    dve.wait_ge(left1, n - 1)
                for b in range(B):
                    dve.tensor_tensor(full[:, n % 2, b * S:(b + 1) * S], raw[:, n % 2, b * S:(b + 1) * S],
                                      ramp[:, (n // 2 + n) % 2, :], ALU.mult).then_inc(scaled, 1)

            def first_left(n):
                dve.wait_ge(part0, n + 1)
                if n >= 2:
                    dve.wait_ge(part1, n - 1)
                    dve.wait_ge(part2, n - 1)
                dve.tensor_tensor(left[:, n % 2, :], full[:, n % 2, :], parts[:, n, 0, :], ALU.subtract).then_inc(left1, 1)

            def second_left(n):
                dve.wait_ge(part1, n + 1)
                dve.tensor_tensor(parts[:, n, 2, :], left[:, n % 2, :], parts[:, n, 1, :], ALU.subtract).then_inc(part2, 1)

            for pair in range(2):
                for step in (scale, first_left, second_left):
                    step(2 * pair)
                    step(2 * pair + 1)
            for n in range(2):
                dve.wait_ge(squared, n + 1)
                dve.tensor_reduce(extent[:, n:n + 1], full[:, n, :], AX, ALU.max).then_inc(reached, 1)
            dve.wait_ge(summed, 1)
            dve.tensor_copy(limits[:, 0:4], bank[4][0:1, 0:4]).then_inc(judged, 1)
            dve.wait_ge(judged, 1)
            dve.tensor_tensor(limits[:, 4:5], limits[:, 0:1], limits[:, 1:2], ALU.mult).then_inc(judged, 1)
            dve.tensor_tensor(limits[:, 5:6], limits[:, 2:3], limits[:, 3:4], ALU.mult).then_inc(judged, 1)
            dve.wait_ge(judged, 3)
            dve.tensor_scalar(limits[:, 6:7], limits[:, 4:5], 0.9 * CLAMP * CLAMP, None, ALU.is_lt).then_inc(judged, 1)
            dve.tensor_scalar(limits[:, 7:8], limits[:, 5:6], 1e30, None, ALU.is_lt).then_inc(judged, 1)
            dve.wait_ge(judged, 5)
            dve.tensor_tensor(limits[:, 0:1], limits[:, 6:7], limits[:, 7:8], ALU.mult).then_inc(judged, 1)
            dve.wait_ge(judged, 6)
            dve.tensor_scalar(mem["clamps"][:, :], limits[:, 0:1], -1.0, 1.0, ALU.mult, ALU.add).then_inc(judged, 1)


def tools(nc, ctx, last=False):
    stage = nc.next_id()
    taken = []

    def zero():
        for s in taken:
            nc.sync.sem_clear(s)

    if not last:
        ctx.callback(zero)

    def sb(name, shape, dt=F32):
        return ctx.enter_context(nc.sbuf_tensor(f"{name}_{stage}", shape, dt))

    def ps(name, shape, dt=F32):
        return ctx.enter_context(nc.psum_tensor(f"{name}_{stage}", shape, dt))

    def sem(name):
        taken.append(ctx.enter_context(nc.semaphore(f"{name}_{stage}")))
        return taken[-1]

    return sb, ps, sem


LOWEST = -3.0e38
RESERVE = 10
NEG_AFTER = 4
EARLY = 6
TURN_AT = 1


class Group:

    def __init__(self, k, turn=0):
        self.k, self.turn = k, turn
        self.third = k % 3
        self.n = k + 3 * turn
        self.round = k // 3 + turn


def attention_scores(nc, mem, dram):
    with ExitStack() as ctx:
        sb, ps, sem = tools(nc, ctx)
        NU = SB * GH + SB // 2
        HALF = S // 2
        NA = SB * GH * 2
        stack = [mem["stack0"]] + [sb(f"stack{i}", [P, 2, 2, GH, S], BF16) for i in (1, 2)]
        v_aug = [sb(f"v_aug{i}", [P, SB, GH, 32]) for i in range(3)]
        prob = [sb(f"prob{i}", [P, GH, S]) for i in range(2)]
        prob_late = [sb(f"prob_late{i}", [P, 2, GH, P]) for i in range(2)]
        junk = sb("junk", [P, 2, HALF], BF16)
        top = sb("top", [P, 2, GH, SB, 2])
        neg = sb("neg", [P, GH, SB])
        neg_left = sb("neg_left", [P, GH, SB])
        neg_parts = sb("neg_parts", [P, NPART, GH, SB], BF16)
        ident_b = sb("ident_b", [P, P], BF16)
        neg_rows = sb("neg_rows", [GH * NPART * SB, P], BF16)
        o_t = sb("o_t", [P, S])
        recip = sb("recip", [P, SB, GH])
        score = [ps(f"score{i}", [P, S]) for i in range(2)]
        out_ps = ps("out_ps", [P, S])
        row = ps("row", [P, 2, HALF])
        rest, ident, v_src, o_src = mem["rest"], mem["ident"], mem["v_src"], mem["o_src"]

        rows_set, values_set, ident_cast = {i: sem(f"rows_set{i}") for i in (1, 2)}, sem("values_set"), sem("ident_cast")
        dve_passed, pool_passed = sem("dve_passed"), sem("pool_passed")
        stacks_in = [[sem(f"stacks_in{half}_{i}") for i in range(3)] for half in range(2)]
        lowest_in = sem("lowest_in")
        v_staged = sem("v_staged")
        row_ready, row_done = sem("row_ready"), sem("row_done")
        neg_chain, neg_turned, neg_copied = sem("neg_chain"), sem("neg_turned"), sem("neg_copied")
        neg_in = [sem(f"neg_in{i}") for i in range(3)]
        scored, exped, masked, mask_late = sem("scored"), sem("exped"), sem("masked"), sem("mask_late")
        weighted, o_copied, o_turned, o_inv, o_done = sem("weighted"), sem("o_copied"), sem("o_turned"), sem("o_inv"), sem("o_done")
        block = ctx.enter_context(nc.Block())

        units = []
        for pair in range(SB // 2):
            units += [("tile", 2 * pair + k, h) for k in range(2) for h in range(GH)]
            units += [("late", pair, 0)]
        unit_at = {u: n for n, u in enumerate(units)}

        def first(g):
            return isinstance(g.n, int) and g.n == 0

        def run_groups(eng, body):
            body(None, Group(0), None, None, 0, 0)
            body(Group(0), Group(1), None, None, 0, 0)
            with eng.Fori(0, (NG - 2) // 3) as turn:
                for k, begin, early in ((1, 0, EARLY), (2, EARLY, EARLY), (3, EARLY, 0)):
                    body(Group(k, turn), Group(k + 1, turn), Group(k - 1, turn), Group(k + 2, turn), begin, early)
            body(Group(NG - 1), None, Group(NG - 2), None, 0, 0)

        LOADS, NEGS = NPART + 1, 2

        schedule = []
        for n, (kind, tile, h) in enumerate(units):
            schedule.append(("unit", n, 0))
            if n == TURN_AT:
                schedule.append(("turn", 0, 0))
            if kind == "tile" and tile and h in (1, 3):
                schedule.append(("weigh", tile - 1, h // 2))
            if kind == "tile" and tile and tile % 2 == 0 and h == 2:
                schedule.append(("late", tile // 2 - 1, 0))
        tail = [("weigh", SB - 1, 0), ("weigh", SB - 1, 1), ("late", SB // 2 - 1, 0)]
        def merge(begin, early):
            order, rows, later = [], list(range(begin, NA)), list(range(early))
            steps, count = schedule + tail, NA - begin
            spread = len(steps) - RESERVE
            for n, step in enumerate(steps):
                order.append(step)
                while rows and (count - len(rows)) * spread < count * (n + 1):
                    order.append(("row", rows.pop(0), 0))
                if n == spread - 1 + NEG_AFTER:
                    order.append(("neg", 0, 0))
                elif n > spread - 1 + NEG_AFTER and later:
                    order.append(("early", later.pop(0), 0))
            return order + [("early", n, 0) for n in later]

        orders = {(begin, early): merge(begin, early) for begin in (0, EARLY) for early in (0, EARLY)}
        finish_at = {key: key[0] + sum(kind == "row" for kind, _, _ in order[:order.index(("turn", 0, 0))])
                     for key, order in orders.items()}
        product_order = [(kind, tile) for kind, tile, half in schedule + tail if kind == "late" or (kind == "weigh" and half == 1)]
        product_order = [("tile" if kind == "weigh" else kind, tile) for kind, tile in product_order]
        NW = len(product_order)

        def used_tile(g, tile):
            if tile >= 2:
                return g.n * NW + product_order.index(("tile", tile - 2)) + 1
            return (g.n - 1) * NW + product_order.index(("tile", SB - 2 + tile)) + 1

        def used_late(g, pair):
            if pair >= 2:
                return g.n * NW + product_order.index(("late", pair - 2)) + 1
            return (g.n - 1) * NW + product_order.index(("late", SB // 2 - 2 + pair)) + 1

        @block.sync
        def _(sp):
            with sp.If(sp.value_load(mem["clamps"][0:1, 0:1], min_val=0, max_val=1) == 0):
                def load(g):
                    for half in range(2):
                        load_half(g, half)

                def load_half(g, half):
                    load_stack(sp, dram, stack[g.third], g.n, half, stacks_in[half][g.third])

                def store_neg(g):
                    sp.wait_ge(neg_copied, g.n + 1)
                    for half in range(2):
                        sp.dma_start(stack[g.third][KR:KR + NPART, half, 0, :, :].rearrange("k h (t c) -> k (h t) c", c=P),
                                     neg_rows[:, :]).then_inc(neg_in[g.third], 16)

                load_half(Group(0), 1)
                sp.wait_ge(rows_set[1], 1)
                load(Group(1))
                store_neg(Group(0))
                sp.wait_ge(rows_set[2], 1)
                load(Group(2))
                store_neg(Group(1))

                def body(g, ahead):
                    sp.wait_ge(scored, g.n * NU)
                    load(ahead)
                    store_neg(Group(g.k + 1, g.turn))

                with sp.Fori(0, (NG - 2) // 3 - 1) as turn:
                    for k in (1, 2, 3):
                        body(Group(k, turn), Group(k + 2, turn))
                body(Group(NG - 4), Group(NG - 2))
                body(Group(NG - 3), Group(NG - 1))
                store_neg(Group(NG - 1))
                for i in range(3):
                    sp.wait_ge(neg_in[i], (NG - 1 - i + 3) // 3 * NEGS * 16)

        @block.tensor
        def _(pe):
            with pe.If(pe.value_load(mem["clamps"][0:1, 0:1], min_val=0, max_val=1) == 0):
                def row_unit(g, n):
                    tile, h, part = n // (2 * GH), n // 2 % GH, n % 2
                    if n == 0:
                        pe.wait_ge(stacks_in[0][g.third], (g.round + (g.third != 0)) * LOADS * 16)
                        if not first(g):
                            pe.wait_ge(neg_copied, g.n)
                    if not (first(g) and n < 2):
                        pe.wait_ge(row_done, g.n * NA + n - 1)
                    pe.matmul(row[:, n % 2, :], stack[g.third][0:KR, 0, 0, h, tile * P:(tile + 1) * P],
                              stack[g.third][0:KR, 0, 1, h, part * HALF:(part + 1) * HALF],
                              start=True, stop=True).then_inc(row_ready, 1)

                def wide_row_unit(n):
                    if n >= 2:
                        pe.wait_ge(row_done, 2 * (n - 1))
                    tile, h = n // GH, n % GH
                    for part in range(2):
                        last = pe.matmul(score[n % 2][:, part * HALF:(part + 1) * HALF],
                                         stack[0][0:KR, 0, 0, h, tile * P:(tile + 1) * P],
                                         stack[0][0:KR, 0, 1, h, part * HALF:(part + 1) * HALF], start=True, stop=True)
                    last.then_inc(row_ready, 2)

                def turn_neg(g):
                    pe.wait_ge(neg_chain, 6 * (g.n + 1))
                    pe.transpose(row[0:GH * NPART * SB, 0, 0:P // 2].bitcast(BF16),
                                 neg_parts[:, :, :, :], ident_b[:, :]).then_inc(neg_turned, 1)

                def column_unit(g, n):
                    kind, tile, h = units[n]
                    if n == 0:
                        pe.wait_ge(stacks_in[1][g.third], (g.round + 1) * LOADS * 16)
                        pe.wait_ge(neg_in[g.third], (g.round + 1) * NEGS * 16)
                    if not (first(g) and n < 2):
                        pe.wait_ge(exped, g.n * NU + n - 1)
                    out = score[n % 2]
                    if kind == "tile":
                        at = tile * P
                        for begin in (0, HALF):
                            for half, a, b in ((1, begin, min(begin + HALF, at)), (0, max(begin, at), begin + HALF)):
                                if a < b:
                                    last = pe.matmul(out[:, a:b], stack[g.third][0:KX, half, 1, h, at:at + P],
                                                     stack[g.third][0:KX, half, 0, h, a:b], start=True, stop=True)
                    else:
                        for c in range(2 * GH):
                            at, hh = (2 * tile + c // GH) * P, c % GH
                            last = pe.matmul(out[:, c * P:(c + 1) * P], stack[g.third][0:KX, 1, 1, hh, at:at + P],
                                             stack[g.third][0:KX, 1, 0, hh, at:at + P], start=True, stop=True)
                    last.then_inc(scored, 1)

                def weigh(g, tile, part):
                    if tile == 0 and part == 0:
                        pe.wait_ge(v_staged, g.n + 1)
                        if not first(g):
                            pe.wait_ge(o_done, g.n)
                    if part == 0:
                        pe.wait_ge(masked, g.n * SB + tile + 1)
                    for h in range(GH):
                        last = pe.matmul(out_ps[32 * h:32 * h + 32, part * HALF:(part + 1) * HALF],
                                         v_aug[g.third][:, tile, h, :], prob[tile % 2][:, h, part * HALF:(part + 1) * HALF],
                                         start=(tile == 0), stop=False, skip_group_check=True)
                    if part == 1:
                        last.then_inc(weighted, 1)

                def weigh_late(g, pair):
                    pe.wait_ge(mask_late, g.n * (SB // 2) + pair + 1)
                    for k in range(2):
                        tile = 2 * pair + k
                        for h in range(GH):
                            last = pe.matmul(out_ps[32 * h:32 * h + 32, tile * P:(tile + 1) * P],
                                             v_aug[g.third][:, tile, h, :], prob_late[pair % 2][:, k, h, :],
                                             start=False, stop=(pair == SB // 2 - 1), skip_group_check=True)
                    last.then_inc(weighted, 1)

                def turn_out(g):
                    pe.wait_ge(o_copied, g.n + 1)
                    for t in range(SB):
                        last = pe.transpose(out_ps[:, t * P:(t + 1) * P], o_t[:, t * P:(t + 1) * P], ident[:, :])
                    last.then_inc(o_turned, 1)

                def body(g, nxt, before, after, begin, early):
                    if g is None:
                        for n in range(NA // 2):
                            wide_row_unit(n)
                        pe.wait_ge(ident_cast, 1)
                        turn_neg(nxt)
                        pe.wait_ge(values_set, 6)
                        return
                    for kind, tile, h in orders[begin, early]:
                        if kind == "row":
                            if nxt is not None:
                                row_unit(nxt, tile)
                        elif kind == "early":
                            row_unit(after, tile)
                        elif kind == "unit":
                            column_unit(g, tile)
                        elif kind == "turn":
                            if not first(g):
                                turn_out(before)
                        elif kind == "neg":
                            if nxt is not None:
                                turn_neg(nxt)
                        elif kind == "weigh":
                            weigh(g, tile, h)
                        else:
                            weigh_late(g, tile)
                run_groups(pe, body)
                turn_out(Group(NG - 1))

        @block.scalar
        def _(act):
            with act.If(act.value_load(mem["clamps"][0:1, 0:1], min_val=0, max_val=1) == 0):
                def finish(g):
                    act.wait_ge(weighted, (g.n + 1) * (SB + SB // 2))
                    if not first(g):
                        act.wait_ge(o_turned, g.n)
                    act.copy(o_t[:, :], out_ps[:, :]).then_inc(o_copied, 1)

                def body(g, nxt, before, after, begin, early):
                    if g is None:
                        return
                    for n, (kind, tile, h) in enumerate(units):
                        if n == 0 and not first(g):
                            finish(before)
                        act.wait_ge(scored, g.n * NU + n + 1)
                        if kind == "tile":
                            if h == 0 and not (first(g) and tile < 2):
                                act.wait_ge(weighted, used_tile(g, tile))
                            act.activation(prob[tile % 2][:, h, :], score[n % 2][:, :], ACT.Exp).then_inc(exped, 1)
                        else:
                            if not (first(g) and tile < 2):
                                act.wait_ge(weighted, used_late(g, tile))
                            act.activation(prob_late[tile % 2][:, :, :, :],
                                           score[n % 2][:, :].rearrange("p (k h c) -> p k h c", k=2, h=GH),
                                           ACT.Exp).then_inc(exped, 1)

                run_groups(act, body)
                finish(Group(NG - 1))

        @block.gpsimd
        def _(pool):
            with pool.If(pool.value_load(mem["clamps"][0:1, 0:1], min_val=0, max_val=1) == 0):
                def stage(g):
                    if not (isinstance(g.n, int) and g.n < 2):
                        pool.wait_ge(weighted, (g.n - 1) * NW)
                    pool.tensor_copy(v_aug[g.third][:, :, :, 0:HD],
                                     v_src[:, g.n, :, :].rearrange("p t (h r) -> p t h r", r=HD)).then_inc(v_staged, 1)

                def body(g, nxt, before, after, begin, early):
                    if g is None:
                        stage(nxt)
                        return
                    if nxt is not None:
                        stage(nxt)
                    for n, (kind, tile, h) in enumerate(units):
                        if kind == "tile" and h == GH - 1:
                            at = tile * P
                            pool.wait_ge(exped, g.n * NU + n + 1)
                            pool.sem_inc(pool_passed, 1)
                            pool.affine_select(out=prob[tile % 2][:, :, at:at + P], in_=prob[tile % 2][:, :, at:at + P],
                                               compare_op=ALU.is_ge, fill=0.0, base=0, pattern=[[0, GH], [1, P]],
                                               channel_multiplier=-1).then_inc(masked, 1)
                        if kind == "late":
                            pool.wait_ge(exped, g.n * NU + n + 1)
                            pool.sem_inc(pool_passed, 1)
                            pool.affine_select(out=prob_late[tile % 2][:, :, :, :], in_=prob_late[tile % 2][:, :, :, :],
                                               compare_op=ALU.is_gt, fill=0.0, base=0, pattern=[[0, 2 * GH], [-1, P]],
                                               channel_multiplier=1).then_inc(mask_late, 1)

                for i in (1, 2):
                    pool.memset(stack[i][64:96, :, 1, :, :].bitcast(F32), TWO_ONES).then_inc(rows_set[i], 1)
                pool.wait_ge(rows_set[2], 1)
                for v in v_aug:
                    pool.memset(v[:, :, :, HD + 1:32], 0.0).then_inc(values_set, 1)
                    pool.memset(v[:, :, :, HD:HD + 1], 1.0).then_inc(values_set, 1)
                pool.tensor_copy(ident_b[:, :], ident[:, :]).then_inc(ident_cast, 1)
                run_groups(pool, body)

        @block.vector
        def _(dve):
            with dve.If(dve.value_load(mem["clamps"][0:1, 0:1], min_val=0, max_val=1) == 0):
                def row_unit(g, n):
                    tile, h, part = n // (2 * GH), n // 2 % GH, n % 2
                    dve.wait_ge(row_ready, g.n * NA + n + 1)
                    at = S - P - tile * P + part * HALF
                    dve.sem_inc(dve_passed, 1)
                    dve.tensor_tensor_reduce(junk[:, n % 2, :], row[:, n % 2, :], rest[:, at:at + HALF], 1.0, LOWEST,
                                             ALU.mult, ALU.max, top[:, 0, h, tile, part:part + 1]).then_inc(row_done, 1)

                def wide_row_unit(n):
                    tile, h = n // GH, n % GH
                    dve.wait_ge(row_ready, 2 * n + 2)
                    dve.tensor_tensor_reduce(prob[n % 2][:, 0, :], score[n % 2][:, :],
                                             rest[:, S - P - tile * P:2 * S - P - tile * P], 1.0, LOWEST,
                                             ALU.mult, ALU.max, top[:, 0, h, tile, 0:1]).then_inc(row_done, 2)

                def negate(g):
                    base = g.n * 6
                    dve.wait_ge(row_done, (g.n + 1) * NA)
                    dve.tensor_reduce(top[:, 1, :, :, 0], top[:, 0, :, :, :], AX, ALU.max).then_inc(neg_chain, 1)
                    dve.wait_ge(neg_chain, base + 1)
                    dve.tensor_scalar(neg[:, :, :], top[:, 1, :, :, 0], -1.0, None, ALU.mult).then_inc(neg_chain, 1)
                    dve.wait_ge(neg_chain, base + 2)
                    if not first(g):
                        dve.wait_ge(neg_turned, g.n)
                    dve.tensor_copy(neg_parts[:, 0, :, :], neg[:, :, :]).then_inc(neg_chain, 1)
                    dve.wait_ge(neg_chain, base + 3)
                    dve.tensor_tensor(neg_left[:, :, :], neg[:, :, :], neg_parts[:, 0, :, :], ALU.subtract).then_inc(neg_chain, 1)
                    dve.wait_ge(neg_chain, base + 4)
                    dve.tensor_copy(neg_parts[:, 1, :, :], neg_left[:, :, :]).then_inc(neg_chain, 1)
                    dve.wait_ge(neg_chain, base + 5)
                    dve.tensor_tensor(neg_parts[:, 2, :, :], neg_left[:, :, :], neg_parts[:, 1, :, :], ALU.subtract).then_inc(neg_chain, 1)
                    dve.wait_ge(neg_turned, g.n + 1)
                    if not first(g):
                        prev = Group(g.k - 1, g.turn)
                        dve.wait_ge(neg_in[prev.third], (prev.round + 1) * NEGS * 16)
                    dve.tensor_copy(neg_rows[:, :], row[0:GH * NPART * SB, 0, 0:P // 2].bitcast(BF16)).then_inc(neg_copied, 1)

                def finish(g):
                    dve.wait_ge(o_turned, g.n + 1)
                    out = out_ps[:, :].rearrange("p (t h r) -> p t h r", t=SB, h=GH)
                    if not first(g):
                        dve.wait_ge(o_done, g.n)
                    dve.reciprocal(recip[:, :, :], out[:, :, :, HD]).then_inc(o_inv, 1)
                    dve.wait_ge(o_inv, g.n + 1)
                    dve.tensor_tensor(o_src[:, g.n, :, :].rearrange("p t (h r) -> p t h r", r=HD), out[:, :, :, 0:HD],
                                      recip[:, :, :].unsqueeze(3).to_broadcast([P, SB, GH, HD]), ALU.mult).then_inc(o_done, 1)

                def body(g, nxt, before, after, begin, early):
                    if g is None:
                        for n in range(NA // 2):
                            wide_row_unit(n)
                        negate(nxt)
                    elif nxt is not None:
                        for n in range(begin, NA):
                            if n == finish_at[begin, early] and g is not None and not first(g):
                                finish(before)
                            row_unit(nxt, n)
                        negate(nxt)
                        for n in range(early):
                            row_unit(after, n)
                    else:
                        finish(before)

                dve.memset(top[:, 0, :, :, :], LOWEST).then_inc(lowest_in, 1)
                dve.wait_ge(lowest_in, 1)
                run_groups(dve, body)
                finish(Group(NG - 1))


def attention_general(nc, mem, dram, io):
    with ExitStack() as ctx:
        sb, ps, sem = tools(nc, ctx)
        queries, keys = sb("queries", [P, S], BF16), sb("keys", [P, S], BF16)
        bound, low, rest = sb("bound", [P, 2 * S - P]), sb("low", [P, 2 * S - P]), mem["rest"]
        raw, clean, number = sb("raw", [P, S]), sb("clean", [P, S]), sb("number", [P, S], I32)
        prob, prob_t = sb("prob", [P, S]), sb("prob_t", [P, S])
        top, neg, denom, inv = (sb(n, [P, 1]) for n in ("top", "neg", "denom", "inv"))
        score, turned_ps, out_ps = ps("score", [P, S]), ps("turned", [P, S]), ps("out", [P, HD])
        loaded, tables, set_up, scored, steps, maxed, exped, turned, t_copied, weighted, done = (
            sem(n) for n in ("loaded", "tables", "set_up", "scored", "steps", "maxed", "exped", "turned", "t_copied",
                             "weighted", "done"))
        ident, v_src, o_src = mem["ident"], mem["v_src"], mem["o_src"]
        passed = sem("passed")
        block = ctx.enter_context(nc.Block())
        STEPS = 9

        def general(eng):
            return eng.If(eng.value_load(mem["clamps"][0:1, 0:1], min_val=0, max_val=1) == 1)

        def head_tiles(eng, body):
            with eng.Fori(0, NG) as g:
                with eng.Fori(0, GH) as h:
                    with eng.Fori(0, SB) as shift:
                        body(g, h, shift, g * (GH * SB) + h * SB + shift)

        def hold(eng, semaphore, value):
            eng.wait_ge(semaphore, value)
            eng.sem_inc(passed, 1)

        parts = dram["parts"]
        v_heads = v_src[:, :, :, :].rearrange("p g t (h r) -> p g h t r", r=HD)
        o_heads = o_src[:, :, :, :].rearrange("p g t (h r) -> p g h t r", r=HD)

        @block.sync
        def _(sp):
            with general(sp):
                sp.dma_start(bound[:, :], io["c_bound"]).then_inc(tables, 16)
                sp.wait_ge(tables, 16)
                with sp.Fori(0, NG) as g:
                  with sp.Fori(0, GH) as h:
                    hold(sp, done, g * (GH * SB) + h * SB + 1)
                    for a in range(NPART):
                        sp.dma_start(queries[a * NPART * HD:(a + 1) * NPART * HD, :],
                                     parts[0, 0, g, a, :, h, :].unsqueeze(0).to_broadcast([NPART, HD, S])).then_inc(loaded, 16)
                    sp.dma_start(keys[0:KR, :], parts[1, 0, g, :, :, h, :].rearrange("k r t -> (k r) t")
                                 .unsqueeze(0).to_broadcast([NPART, NPART * HD, S])).then_inc(loaded, 16)

        @block.tensor
        def _(pe):
            def body(g, h, shift, n):
                hold(pe, loaded, g * (GH * 16 * (NPART + 1)) + h * (16 * (NPART + 1)) + 16 * (NPART + 1))
                hold(pe, done, n + 1)
                for c in range(2):
                    last = pe.matmul(score[:, c * 512:(c + 1) * 512],
                                     queries[0:KR, bass.ds((SB - 1) * P - shift * P, P)],
                                     keys[0:KR, c * 512:(c + 1) * 512], start=True, stop=True)
                last.then_inc(scored, 1)
                hold(pe, exped, n + 1)
                for t in range(SB):
                    last = pe.transpose(turned_ps[:, t * P:(t + 1) * P], prob[:, t * P:(t + 1) * P], ident[:, :])
                last.then_inc(turned, 1)
                hold(pe, t_copied, n + 1)
                for t in range(SB):
                    last = pe.matmul(out_ps[:, :], prob_t[:, t * P:(t + 1) * P], v_heads[:, g, h, t, :],
                                     start=(t == 0), stop=(t == SB - 1))
                last.then_inc(weighted, 1)

            with general(pe):
                pe.wait_ge(tables, 16)
                head_tiles(pe, body)

        @block.scalar
        def _(act):
            def body(g, h, shift, n):
                hold(act, maxed, n + 1)
                act.activation(prob[:, :], clean[:, :], ACT.Exp, bias=neg[:, 0:1], accum_out=denom[:, 0:1]).then_inc(exped, 1)

            with general(act):
                head_tiles(act, body)

        @block.vector
        def _(dve):
            def body(g, h, shift, n):
                base = n * STEPS

                def step(k, ins):
                    ins.then_inc(steps, 1)
                    hold(dve, steps, base + k)

                hold(dve, scored, n + 1)
                dve.tensor_copy(raw[:, :], score[:, :]).then_inc(steps, 1)

                def at(table):
                    return table[:, bass.ds(shift * P, S)]

                dve.tensor_copy(clean[:, :], at(low)).then_inc(steps, 1)
                hold(dve, steps, base + 2)
                step(3, dve.tensor_tensor(number[:, :], raw[:, :], raw[:, :], ALU.is_equal))
                step(4, dve.copy_predicated(clean[:, :], number[:, :], raw[:, :]))
                step(5, dve.tensor_tensor(clean[:, :], clean[:, :], at(bound), ALU.min))
                step(6, dve.tensor_tensor(clean[:, :], clean[:, :], at(low), ALU.max))
                step(7, dve.tensor_tensor(clean[:, :], clean[:, :], at(rest), ALU.mult))
                step(8, dve.tensor_reduce(top[:, :], clean[:, :], AX, ALU.max))
                dve.tensor_scalar(neg[:, :], top[:, :], -1.0, None, ALU.mult).then_inc(maxed, 1)
                hold(dve, exped, n + 1)
                step(9, dve.reciprocal(inv[:, :], denom[:, :]))
                hold(dve, turned, n + 1)
                dve.tensor_copy(prob_t[:, :], turned_ps[:, :]).then_inc(t_copied, 1)
                hold(dve, weighted, n + 1)
                dve.tensor_scalar(o_heads[:, g, h, (SB - 1) - shift, :], out_ps[:, :], inv[:, 0:1], None, ALU.mult).then_inc(done, 1)

            with general(dve):
                dve.wait_ge(tables, 16)
                dve.tensor_scalar(low[:, :], bound[:, :], -1.0, None, ALU.mult).then_inc(set_up, 1)
                dve.wait_ge(set_up, 1)
                dve.sem_inc(done, 1)
                head_tiles(dve, body)


class Steps:

    def __init__(self, eng, semaphore):
        self.eng, self.semaphore, self.done = eng, semaphore, 0

    def __call__(self, *instructions):
        for ins in instructions:
            ins.then_inc(self.semaphore, 1)
        self.done += len(instructions)
        self.eng.wait_ge(self.semaphore, self.done)


def statistics(dve, mem, step, tiles):
    step(*[dve.bn_stats(mem["stats"][:, t, :], mem["y"][:, t, :]) for t in tiles])
    step(*[dve.bn_aggr(mem["mv"][:, t, :], mem["stats"][:, t, :]) for t in tiles])


def attention_output(nc, mem, io):
    with ExitStack() as ctx:
        sb, ps, sem = tools(nc, ctx)
        wo, a_t = sb("wo", [P, D]), sb("a_t", [P, 2, 512])
        o_tok, ordered = sb("o_tok", [P, NT, D]), sem("ordered")
        turned_ps = [ps(f"turned_ps{i}", [P, 512]) for i in range(2)]
        out_ps = [ps(f"attn_ps{i}", [P, 512]) for i in range(2)]
        loaded, turned, copied, projected, added = (sem(n) for n in ("wo_in", "turned", "copied", "projected", "added"))
        stat_steps = sem("stat_steps")
        ident, o_src, x, y = mem["ident"], mem["o_src"], mem["x_tok"], mem["y"]
        block = ctx.enter_context(nc.Block())

        @block.sync
        def _(sp):
            sp.dma_start(wo[:, :], io["L0_attn_Wo"]).then_inc(loaded, 16)
            load_expert_weights(sp, mem, io, 0)
            sp.wait_ge(loaded, 16)

        @block.tensor
        def _(pe):
            pe.wait_ge(loaded, 16)
            for c in range(NT // 4 + 1):
                if c < NT // 4:
                    pe.wait_ge(ordered, c + 1)
                    if c >= 2:
                        pe.wait_ge(copied, c - 1)
                    for k in range(4):
                        last = pe.transpose(turned_ps[c % 2][:, k * P:(k + 1) * P], o_tok[:, 4 * c + k, :], ident[:, :])
                    last.then_inc(turned, 1)
                if c:
                    n = c - 1
                    pe.wait_ge(copied, n + 1)
                    if n >= 2:
                        pe.wait_ge(added, n - 1)
                    for k in range(4):
                        last = pe.matmul(out_ps[n % 2][:, k * P:(k + 1) * P], a_t[:, n % 2, k * P:(k + 1) * P],
                                         wo[:, :], start=True, stop=True)
                    last.then_inc(projected, 1)

        @block.scalar
        def _(act):
            for c in range(NT // 4):
                act.wait_ge(turned, c + 1)
                if c >= 2:
                    act.wait_ge(projected, c - 1)
                act.copy(a_t[:, c % 2, :], turned_ps[c % 2][:, :]).then_inc(copied, 1)

        @block.vector
        def _(dve):
            for c in range(NT // 4):
                b, t = 4 * c // SB, 4 * c % SB
                dve.tensor_copy(o_tok[:, 4 * c:4 * c + 4, :].rearrange("p t (g r) -> p g t r", r=GH * HD),
                                o_src[:, b * (NG // B):(b + 1) * (NG // B), t:t + 4, :]).then_inc(ordered, 1)
            step = Steps(dve, stat_steps)
            for c in range(NT // 4):
                dve.wait_ge(projected, c + 1)
                dve.tensor_tensor(y[:, 4 * c:4 * c + 4, :], x[:, 4 * c:4 * c + 4, :],
                                  out_ps[c % 2][:, :].rearrange("p (t d) -> p t d", d=D), ALU.add).then_inc(added, 1)
                dve.wait_ge(added, c + 1)
                statistics(dve, mem, step, range(4 * c, 4 * c + 4))


def layer_norm(nc, mem, out=None, io=None, weight=None):
    with ExitStack() as ctx:
        sb, ps, sem = tools(nc, ctx)
        mv = mem["mv"]
        var, std, inv = sb("var", [P, NT]), sb("std", [P, NT]), sb("inv", [P, NT])
        bank = [ps(f"norm_ps{i}", [P, 512]) for i in range(4)]
        steps, var_in, std_in, normed = sem("ln_steps"), sem("var_in"), sem("std_in"), sem("normed")
        turned, copied, stored, w_in = sem("ln_turned"), sem("ln_copied"), sem("ln_stored"), sem("ln_w_in")
        x, y, ident = mem["x_tok"], mem["y"], mem["ident"]
        to_turn, target, ready = x, mem["x_t"], normed
        if weight is not None:
            w_row, square = sb("w_row", [P, D]), sb("square", [P, NT])
            mean, std2, inv2 = sb("mean", [P, NT]), sb("std2", [P, NT]), sb("inv2", [P, NT])
            rms_ready = sem("rms_normed")
            to_turn, target, ready = mem["h_tok"], mem["h_t"], rms_ready
        block = ctx.enter_context(nc.Block())

        @block.vector
        def _(dve):
            step = Steps(dve, steps)
            dve.tensor_scalar(var[:, :], mv[:, :, 1], EPS, None, ALU.add).then_inc(var_in, 1)
            dve.wait_ge(std_in, 1)
            step(dve.reciprocal(inv[:, :], std[:, :]))
            if weight is not None:
                step(dve.tensor_tensor(square[:, :], inv[:, :], inv[:, :], ALU.mult))
                step(dve.tensor_tensor(square[:, :], square[:, :], mv[:, :, 1], ALU.mult))
                dve.tensor_scalar(mean[:, :], square[:, :], EPS, None, ALU.add).then_inc(var_in, 1)
            for t in range(NT):
                dve.tensor_scalar(x[:, t, :], y[:, t, :], mv[:, t, 0:1], inv[:, t:t + 1],
                                  ALU.subtract, ALU.mult).then_inc(normed, 1)
            if weight is not None:
                dve.wait_ge(normed, NT)
                dve.wait_ge(std_in, 2)
                step(dve.reciprocal(inv2[:, :], std2[:, :]))
                dve.wait_ge(w_in, 16)
                for t in range(NT):
                    dve.scalar_tensor_tensor(to_turn[:, t, :], x[:, t, :], inv2[:, t:t + 1], w_row[:, :],
                                             ALU.mult, ALU.mult).then_inc(rms_ready, 1)

        @block.scalar
        def _(act):
            act.wait_ge(var_in, 1)
            act.activation(std[:, :], var[:, :], ACT.Sqrt).then_inc(std_in, 1)
            if weight is not None:
                act.wait_ge(var_in, 2)
                act.activation(std2[:, :], mean[:, :], ACT.Sqrt).then_inc(std_in, 1)
            if out is None:
                for c in range(NT // 4):
                    act.wait_ge(turned, c + 1)
                    act.copy(target[:, c * 512:(c + 1) * 512], bank[c][:, :]).then_inc(copied, 1)

        if out is None:
            @block.tensor
            def _(pe):
                for t in range(NT):
                    pe.wait_ge(ready, t + 1)
                    last = pe.transpose(bank[t // 4][:, t % 4 * P:t % 4 * P + P], to_turn[:, t, :], ident[:, :])
                    if t % 4 == 3:
                        last.then_inc(turned, 1)

        if out is not None or weight is not None:
            @block.sync
            def _(sp):
                if weight is not None:
                    sp.dma_start(w_row[:, :], io[weight].rearrange("(a d) -> a d", a=1).to_broadcast([P, D])).then_inc(w_in, 16)
                    sp.wait_ge(w_in, 16)
                    return
                for c in range(4):
                    sp.wait_ge(normed, NT // 4 * (c + 1))
                    sp.dma_start(out.rearrange("b (t p) d -> p (b t) d", p=P)[:, 4 * c:4 * c + 4, :],
                                 x[:, 4 * c:4 * c + 4, :]).then_inc(stored, 16)
                sp.wait_ge(stored, 64)


E = 8
C0 = T // E
C1 = int(1.25 * T / E)
F0 = 512
RW = D + 1


def route(nc, mem, io, layer):
    K = 1 + layer
    cap = (C0, C1)[layer]
    rows = E * cap
    table, far = mem[f"slots{layer}"], float(4 * T)
    with ExitStack() as ctx:
        sb, ps, sem = tools(nc, ctx)

        def cube(name, dt=F32):
            return sb(name, [P, NT, E], dt)

        router = sb("router", [P, E])
        router_e = sb("router_e", [E, D])
        before, ones = sb("before", [P, P], BF16), sb("ones", [P, P], BF16)
        before_f = sb("before_f", [P, P])
        order, number = sb("order", [P, E]), sb("number", [P, E])
        logit, e_x, same, ranked, left = cube("logit"), cube("e_x"), cube("same"), cube("ranked"), cube("left")
        pick = [cube(f"pick{k}") for k in range(K)]
        picked_b = cube("picked_b", BF16)
        total, total2, place, prod = cube("total"), cube("total2"), cube("place"), cube("prod")
        kept = cube("kept")
        mx, mx2, denom, inv, prob1, prob2, tie = (sb(n, [P, NT]) for n in ("mx", "mx2", "denom", "inv", "prob1", "prob2", "tie"))
        slot, own, is_kept, at, out_at = (sb(n, [P, NT]) for n in ("slot", "own", "is_kept", "at", "out_at"))
        out_index = [sb(f"out_index{k}", [P, NT], I32) for k in range(K)]
        gate = mem["gate"]
        token = sb("token", [P, NT], I32)
        rows_x = [sb(f"rows_x{k}", [P, NT, RW]) for k in range(K)]
        empty = sb("empty", [P, 4, RW])
        weight, above = cube("weight"), cube("above", BF16)
        found, cand, added = sb("found", [P, E], I32), sb("cand", [P, 3, E], I32), sb("added", [P, E], I32)
        reach, counts, holds = sb("reach", [P, 3, NT, E], BF16), sb("counts", [P, 3, E], BF16), sb("holds", [P, 3, E])
        count, room, fit = sb("count", [P, E], BF16), sb("room", [P, E]), cube("fit")
        logit_ps = ps("logit_ps", [P, NT, E])
        turn_ps = ps("turn_ps", [P, 512])
        place_ps, total_ps, count_ps = ps("place_ps", [P, NT, E]), ps("total_ps", [P, NT, E]), ps("count_ps", [P, 3, E])
        cleared, numbered = sem("rt_cleared"), sem("rt_numbered")
        loaded, zeroed, set_up, routed, steps, exp_in, exped = (
            sem(n) for n in ("rt_loaded", "rt_zeroed", "rt_set", "rt_routed", "rt_steps", "rt_exp_in", "rt_exped"))
        cum_in, cum_out, count_in, count_out, index_in = (
            sem(n) for n in ("cum_in", "cum_out", "count_in", "count_out", "index_in"))
        sent = mem[f"sent{layer}"]
        turned = sem("rt_turned")
        x, x_t, ident = mem["x_tok"], mem["x_t"], mem["ident"]
        block = ctx.enter_context(nc.Block())

        @block.sync
        def _(sp):
            sp.dma_start(before_f[:, :], io["c_before"]).then_inc(loaded, 16)
            sp.dma_start(order[:, :], io["c_order"]).then_inc(loaded, 16)
            sp.dma_start(number[:, :], io["c_number"]).then_inc(loaded, 16)
            sp.dma_start(token[:, :], io["c_token"]).then_inc(loaded, 16)
            if layer == 0:
                sp.dma_start(router[:, :], io["L0_ffn_router_w"]).then_inc(loaded, 16)
            else:
                sp.dma_start(router_e[:, :], io["L1_ffn_router_w"]).then_inc(loaded, 16)
            sp.wait_ge(set_up, 2)
            for r in range(0, rows, 4 * P):
                sp.dma_start(table[r:r + 4 * P, :].rearrange("(p k) d -> p k d", k=4), empty[:, :, :]).then_inc(zeroed, 16)
            for r in range(0, K * T, 4 * P):
                sp.dma_start(mem[f"results{layer}"][r:r + 4 * P, :].rearrange("(p k) d -> p k d", k=4),
                             empty[:, :, 0:D]).then_inc(cleared, 16)
            sp.wait_ge(zeroed, 16 * (rows // (4 * P)))
            sp.wait_ge(cleared, 16 * (K * T // (4 * P)))

        @block.tensor
        def _(pe):
            pe.wait_ge(loaded, 80)
            if layer == 1:
                pe.transpose(turn_ps[:, 0:E], router_e[:, :], ident[0:E, 0:E]).then_inc(turned, 1)
                pe.wait_ge(steps, 1)
            for t in range(NT):
                last = pe.matmul(logit_ps[:, t, :], x_t[:, t * P:(t + 1) * P], router[:, :], start=True, stop=True)
            last.then_inc(routed, 1)

            def cumulate(n):
                pe.wait_ge(cum_in, n + 1)
                pe.matmul(place_ps[:, :, :], before[:, :], picked_b[:, :, :], start=True, stop=True)
                pe.matmul(total_ps[:, :, :], ones[:, :], picked_b[:, :, :], start=True, stop=True).then_inc(cum_out, 1)

            if layer == 1:
                for n in range(BITS // 2):
                    pe.wait_ge(count_in, n + 1)
                    pe.matmul(count_ps[:, :, :], ones[:, :], counts[:, :, :], start=True, stop=True).then_inc(count_out, 1)
                pe.wait_ge(count_in, BITS // 2 + 1)
                pe.matmul(count_ps[:, 0, :], ones[:, :], count[:, :], start=True, stop=True).then_inc(count_out, 1)
            for n in range(1 + layer):
                cumulate(n)

        @block.scalar
        def _(act):
            act.wait_ge(exp_in, 1)
            act.activation(e_x[:, :, :], left[:, :, :], ACT.Exp).then_inc(exped, 1)
            for k in range(K):
                act.copy(rows_x[k][:, :, 0:D], x[:, :, :]).then_inc(numbered, 1)

        def wide(a):
            return a.unsqueeze(2).to_broadcast([P, NT, E])

        def tiles(a):
            return a.unsqueeze(1).to_broadcast([P, NT, E])

        @block.vector
        def _(dve):
            step = Steps(dve, steps)
            dve.wait_ge(loaded, 80)
            if layer == 1:
                dve.wait_ge(turned, 1)
                step(dve.tensor_copy(router[:, :], turn_ps[:, 0:E]))
            dve.memset(empty[:, :, 0:D], 0.0).then_inc(set_up, 1)
            dve.memset(empty[:, :, D:RW].bitcast(I32), 4 * T).then_inc(set_up, 1)
            step(dve.memset(ones[:, :], 1.0), dve.tensor_copy(before[:, :], before_f[:, :]))
            dve.wait_ge(routed, 1)
            step(dve.tensor_copy(logit[:, :, :], logit_ps[:, :, :]))
            step(dve.tensor_reduce(mx[:, :], logit[:, :, :], AX, ALU.max))
            dve.tensor_tensor(left[:, :, :], logit[:, :, :], wide(mx[:, :]), ALU.subtract).then_inc(exp_in, 1)
            dve.wait_ge(exped, 1)
            step(dve.tensor_reduce(denom[:, :], e_x[:, :, :], AX, ALU.add), dve.tensor_reduce(mx[:, :], e_x[:, :, :], AX, ALU.max))
            step(dve.reciprocal(inv[:, :], denom[:, :]))
            step(dve.tensor_tensor(prob1[:, :], mx[:, :], inv[:, :], ALU.mult))

            def first_of(values, top, to):
                step(dve.tensor_tensor(same[:, :, :], values, wide(top), ALU.is_equal))
                step(dve.tensor_tensor(ranked[:, :, :], same[:, :, :], tiles(order[:, :]), ALU.mult))
                step(dve.tensor_reduce(tie[:, :], ranked[:, :, :], AX, ALU.max))
                step(dve.tensor_tensor(to[:, :, :], ranked[:, :, :], wide(tie[:, :]), ALU.is_equal))

            first_of(e_x[:, :, :], mx[:, :], pick[0])
            if layer == 1:
                step(dve.scalar_tensor_tensor(left[:, :, :], pick[0][:, :, :], -2.0, e_x[:, :, :], ALU.mult, ALU.add))
                step(dve.tensor_reduce(mx2[:, :], left[:, :, :], AX, ALU.max))
                first_of(left[:, :, :], mx2[:, :], pick[1])
                step(dve.tensor_tensor(prob2[:, :], mx2[:, :], inv[:, :], ALU.mult))
                step(dve.tensor_tensor(denom[:, :], prob1[:, :], prob2[:, :], ALU.add))
                step(dve.tensor_scalar(denom[:, :], denom[:, :], 1e-6, None, ALU.add))
                step(dve.reciprocal(inv[:, :], denom[:, :]))
                step(dve.tensor_tensor(prob1[:, :], prob1[:, :], inv[:, :], ALU.mult),
                     dve.tensor_tensor(prob2[:, :], prob2[:, :], inv[:, :], ALU.mult))
                step(dve.tensor_tensor(prod[:, :, :], pick[0][:, :, :], wide(prob1[:, :]), ALU.mult),
                     dve.tensor_tensor(left[:, :, :], pick[1][:, :, :], wide(prob2[:, :]), ALU.mult),
                     dve.tensor_tensor(same[:, :, :], pick[0][:, :, :], pick[1][:, :, :], ALU.add))
                step(dve.tensor_tensor(weight[:, :, :], prod[:, :, :], left[:, :, :], ALU.add))
                step(dve.scalar_tensor_tensor(weight[:, :, :], same[:, :, :], -1.0, weight[:, :, :], ALU.add, ALU.add))
                step(dve.memset(found[:, :], 0))
                for n in range(BITS // 2):
                    low = BITS - 2 - 2 * n
                    step(*[dve.tensor_scalar(cand[:, k, :], found[:, :], (k + 1) << low, None, ALU.bitwise_or)
                           for k in range(3)])
                    step(dve.tensor_tensor(
                        reach[:, :, :, :], weight[:, :, :].unsqueeze(1).to_broadcast([P, 3, NT, E]),
                        cand[:, :, :].bitcast(F32).unsqueeze(2).to_broadcast([P, 3, NT, E]), ALU.is_ge))
                    with nc.allow_low_precision(reason="counts up to NT are exact"):
                        dve.tensor_reduce(counts[:, :, :], reach[:, :, :, :].rearrange("p c t e -> p c e t"),
                                          AX, ALU.add).then_inc(count_in, 1)
                    dve.wait_ge(count_out, n + 1)
                    step(dve.tensor_scalar(holds[:, :, :], count_ps[:, :, :], float(cap), float(1 << low),
                                           ALU.is_ge, ALU.mult))
                    with nc.allow_low_precision(reason="up to three times a power of two is exact"):
                        step(dve.tensor_reduce(added[:, :], holds[:, :, :].rearrange("p c e -> p e c"), AX, ALU.add))
                    step(dve.tensor_tensor(found[:, :], found[:, :], added[:, :], ALU.bitwise_or))
                bound = found[:, :].bitcast(F32)
                step(dve.tensor_tensor(above[:, :, :], weight[:, :, :], tiles(bound), ALU.is_gt),
                     dve.tensor_tensor(picked_b[:, :, :], weight[:, :, :], tiles(bound), ALU.is_equal))
                with nc.allow_low_precision(reason="counts up to NT are exact"):
                    dve.tensor_reduce(count[:, :], above[:, :, :].rearrange("p t e -> p e t"), AX, ALU.add).then_inc(count_in, 1)
                dve.wait_ge(count_out, BITS // 2 + 1)
                step(dve.tensor_scalar(room[:, :], count_ps[:, 0, :], -1.0, float(cap), ALU.mult, ALU.add))
            else:
                step(dve.tensor_copy(picked_b[:, :, :], pick[0][:, :, :]))

            def earlier(n):
                dve.sem_inc(cum_in, 1)
                dve.wait_ge(cum_out, n + 1)
                step(dve.memset(total[:, 0, :], 0.0), dve.tensor_copy(total[:, 1:NT, :], total_ps[:, 0:NT - 1, :]))
                a, b, d = total, total2, 1
                while d < NT:
                    step(dve.tensor_tensor(b[:, d:NT, :], a[:, d:NT, :], a[:, 0:NT - d, :], ALU.add),
                         dve.tensor_copy(b[:, 0:d, :], a[:, 0:d, :]))
                    a, b, d = b, a, 2 * d
                step(dve.tensor_tensor(place[:, :, :], a[:, :, :], place_ps[:, :, :], ALU.add))

            earlier(0)
            if layer == 1:
                step(dve.tensor_tensor(fit[:, :, :], place[:, :, :], tiles(room[:, :]), ALU.is_lt))
                step(dve.tensor_tensor(fit[:, :, :], fit[:, :, :], picked_b[:, :, :], ALU.mult))
                step(dve.tensor_tensor(kept[:, :, :], fit[:, :, :], above[:, :, :], ALU.add))
                step(dve.tensor_copy(picked_b[:, :, :], kept[:, :, :]))
                earlier(1)
            for k in range(K):
                step(dve.tensor_tensor(prod[:, :, :], pick[k][:, :, :], place[:, :, :], ALU.mult))
                step(dve.tensor_reduce(slot[:, :], prod[:, :, :], AX, ALU.add))
                step(dve.tensor_tensor(prod[:, :, :], pick[k][:, :, :], tiles(number[:, :]), ALU.mult))
                step(dve.tensor_reduce(own[:, :], prod[:, :, :], AX, ALU.add))
                if layer == 0:
                    step(dve.tensor_scalar(is_kept[:, :], slot[:, :], float(cap), None, ALU.is_lt))
                else:
                    step(dve.tensor_tensor(prod[:, :, :], pick[k][:, :, :], kept[:, :, :], ALU.mult))
                    step(dve.tensor_reduce(is_kept[:, :], prod[:, :, :], AX, ALU.add))
                step(dve.tensor_scalar(slot[:, :], slot[:, :], float(cap - 1), None, ALU.min))
                step(dve.scalar_tensor_tensor(at[:, :], own[:, :], float(cap), slot[:, :], ALU.mult, ALU.add))
                step(dve.tensor_scalar(out_at[:, :], is_kept[:, :], -far, far, ALU.mult, ALU.add))
                step(dve.tensor_tensor(out_at[:, :], out_at[:, :], at[:, :], ALU.add))
                step(dve.tensor_copy(out_index[k][:, :], out_at[:, :]),
                     dve.tensor_scalar(rows_x[k][:, :, D].bitcast(I32), token[:, :], k * T, None, ALU.add),
                     dve.tensor_tensor(gate[:, k, :], (prob1, prob2)[k][:, :], is_kept[:, :], ALU.mult))
                dve.sem_inc(index_in, 1)

        @block.gpsimd
        def _(pool):
            pool.wait_ge(zeroed, 16 * (rows // (4 * P)))
            for k in range(K):
                pool.wait_ge(index_in, k + 1)
                pool.wait_ge(numbered, k + 1)
                for t in range(NT):
                    pool.indirect_dma_start(table[:, :], bass.IndirectOffsetOnAxis(out_index[k][:, t:t + 1], 0),
                                            rows_x[k][:, t, :], None, bounds_check=rows - 1, oob_is_err=False).then_inc(sent, 16)
            pool.wait_ge(sent, 16 * NT * K)


BITS = 30


def expert_names(layer):
    return (("w1", "w2"), ("wg", "wu", "wd"))[layer]


def load_expert_weights(sp, mem, io, layer):
    names = expert_names(layer)
    up, down, loaded = mem["up_w"], mem["down_w"], mem[f"weights_in{layer}"]
    for j, name in enumerate(names[:-1]):
        sp.dma_start(up[:, j, :, :], io[f"L{layer}_ffn_{name}"].rearrange("e d f -> d e f")).then_inc(loaded, 16)
    sp.dma_start(down[:, :, :], io[f"L{layer}_ffn_{names[-1]}"].rearrange("e (c p) d -> p (e c) d", p=P)).then_inc(loaded, 16)


def experts(nc, mem, io, layer):
    cap = (C0, C1)[layer]
    F, FC = F0, F0 // P
    ups = len(expert_names(layer)) - 1
    tiles = E * cap // P
    chunks = tiles // 4
    K = 1 + layer

    def pieces(e):
        at = e * cap
        while at < (e + 1) * cap:
            end = min((at // P + 1) * P, (e + 1) * cap)
            yield at // P, at % P, at % P + end - at
            at = end

    with ExitStack() as ctx:
        sb, ps, sem = tools(nc, ctx)
        rows_in, rows_t = sb("rows_in", [P, tiles, RW]), sb("rows_t", [P, E * cap])
        hidden = [sb(f"hidden{i}", [P, FC, cap]) for i in range(2)]
        acted = sb("acted", [P, 2, cap])
        rows_out = sb("rows_out", [P, tiles, D])
        turn_ps = [ps(f"xturn_ps{i}", [P, 512]) for i in range(2)]
        up_ps = [[ps(f"up_ps{i}{j}", [P, 512]) for j in range(ups)] for i in range(2)]
        down_ps = [ps(f"down_ps{i}", [P, 3, D]) for i in range(2)]
        r_in = [sem(f"r_in{c}") for c in range(chunks)]
        turned, t_copied, upped, h_in, downed, out_in = (sem(n) for n in ("xturned", "t_copied", "upped", "h_in", "downed", "out_in"))
        acted_in = sem("acted_in")
        ident = mem["ident"]
        w_up, w_down = mem["up_w"], mem["down_w"]
        table, results = mem[f"slots{layer}"], mem[f"results{layer}"]
        block = ctx.enter_context(nc.Block())

        @block.sync
        def _(sp):
            for c in range(chunks):
                sp.dma_start(rows_in[:, 4 * c:4 * c + 4, :],
                             table[4 * c * P:(4 * c + 4) * P, :].rearrange("(k p) d -> p k d", p=P)).then_inc(r_in[c], 16)
            if layer == 0:
                load_linear_weights(sp, mem, io)
            for c in range(chunks):
                sp.wait_ge(r_in[c], 16)

        @block.gpsimd
        def _(pool):
            for t in range(tiles):
                pool.wait_ge(out_in, ((t + 1) * P - 1) // cap + 1)
                pool.wait_ge(r_in[t // 4], 16)
                pool.indirect_dma_start(results[:, :], bass.IndirectOffsetOnAxis(rows_in[:, t, D:RW].bitcast(I32), 0),
                                        rows_out[:, t, :], None, bounds_check=K * T - 1, oob_is_err=False
                                        ).then_inc(mem[f"returned{layer}"], 16)
            pool.wait_ge(mem[f"returned{layer}"], 16 * tiles)

        @block.tensor
        def _(pe):
            def turn(c):
                pe.wait_ge(r_in[c], 16)
                if c >= 2:
                    pe.wait_ge(t_copied, c - 1)
                for k in range(4):
                    last = pe.transpose(turn_ps[c % 2][:, k * P:(k + 1) * P], rows_in[:, 4 * c + k, 0:D], ident[:, :])
                last.then_inc(turned, 1)

            def up(e, c):
                n = e * FC + c
                if c == 0:
                    pe.wait_ge(t_copied, -(-(e + 1) * cap // (4 * P)))
                if n >= 2:
                    pe.wait_ge(h_in, n - 1)
                for j in range(ups):
                    last = pe.matmul(up_ps[n % 2][j][:, 0:cap], w_up[:, j, e, c * P:(c + 1) * P],
                                     rows_t[:, e * cap:(e + 1) * cap], start=True, stop=True)
                last.then_inc(upped, 1)

            def down(e, k):
                found = list(pieces(e))
                if k < len(found):
                    tile, a, b = found[k]
                    at = tile * P + a - e * cap
                    if k == 0:
                        pe.wait_ge(h_in, (e + 1) * FC)
                        if e >= 2:
                            pe.wait_ge(out_in, e - 1)
                    for c in range(FC):
                        last = pe.matmul(down_ps[e % 2][a:b, k, :], hidden[e % 2][:, c, at:at + b - a],
                                         w_down[:, e * FC + c, :], start=(c == 0), stop=(c == FC - 1))
                    if k == len(found) - 1:
                        last.then_inc(downed, 1)

            turns = 0
            for e in range(E + 1):
                while turns < chunks and turns * 4 * P < (e + 2) * cap:
                    turn(turns)
                    turns += 1
                if e == 0:
                    pe.wait_ge(mem[f"weights_in{layer}"], (ups + 1) * 16)
                for c in range(FC):
                    if e < E:
                        up(e, c)
                    if e and c:
                        down(e - 1, c - 1)

        @block.scalar
        def _(act):
            for n in range(E * FC):
                e, c = n // FC, n % FC
                act.wait_ge(upped, n + 1)
                if layer == 0:
                    if c == 0 and e >= 2:
                        act.wait_ge(downed, e - 1)
                    act.activation(hidden[e % 2][:, c, :], up_ps[n % 2][0][:, 0:cap], ACT.Gelu_apprx_tanh).then_inc(h_in, 1)
                else:
                    if n >= 2:
                        act.wait_ge(h_in, n - 1)
                    act.activation(acted[:, n % 2, :], up_ps[n % 2][0][:, 0:cap], ACT.Silu).then_inc(acted_in, 1)

        @block.vector
        def _(dve):
            def rows(c):
                dve.wait_ge(turned, c + 1)
                dve.tensor_copy(rows_t[:, 4 * c * P:(4 * c + 4) * P], turn_ps[c % 2][:, :]).then_inc(t_copied, 1)

            def gates(e):
                for c in range(FC):
                    n = e * FC + c
                    dve.wait_ge(acted_in, n + 1)
                    if c == 0 and e >= 2:
                        dve.wait_ge(downed, e - 1)
                    dve.tensor_tensor(hidden[e % 2][:, c, :], acted[:, n % 2, :], up_ps[n % 2][1][:, 0:cap],
                                      ALU.mult).then_inc(h_in, 1)

            def results_out(e):
                dve.wait_ge(downed, e + 1)
                for k, (tile, a, b) in enumerate(pieces(e)):
                    last = dve.tensor_copy(rows_out[a:b, tile, :], down_ps[e % 2][a:b, k, :])
                last.then_inc(out_in, 1)

            turns = 0
            for e in range(E + 1):
                while turns < chunks and turns * 4 * P < (e + 2) * cap:
                    rows(turns)
                    turns += 1
                if e < E and layer == 1:
                    gates(e)
                if e:
                    results_out(e - 1)


def combine(nc, mem, io, layer):
    K = 1 + layer
    with ExitStack() as ctx:
        sb, ps, sem = tools(nc, ctx)
        got = [sb(f"got{k}", [P, NT, D]) for k in range(K)]
        loaded = [sem(f"got_in{c}") for c in range(NT // 4)]
        summed, stat_steps = sem("summed"), sem("stat_steps")
        x, y, gate = mem["x_tok"], mem["y"], mem["gate"]
        folding = weight_folding(mem, sb, ps, sem) if layer == 0 else None
        block = ctx.enter_context(nc.Block())

        @block.sync
        def _(sp):
            for c in range(NT // 4):
                for k in range(K):
                    rows = mem[f"results{layer}"][k * T + 4 * c * P:k * T + (4 * c + 4) * P, :]
                    sp.dma_start(got[k][:, 4 * c:4 * c + 4, :], rows.rearrange("(t p) d -> p t d", p=P)).then_inc(loaded[c], 16)

        @block.vector
        def _(dve):
            if folding:
                scale_output_weights(dve, mem, folding)
            step = Steps(dve, stat_steps)
            for c in range(NT // 4):
                dve.wait_ge(loaded[c], K * 16)
                for k in range(K):
                    for t in range(4 * c, 4 * c + 4):
                        last = dve.scalar_tensor_tensor(y[:, t, :], got[k][:, t, :], gate[:, k, t:t + 1],
                                                        (x, y)[k][:, t, :], ALU.mult, ALU.add)
                    last.then_inc(summed, 1)
                    dve.wait_ge(summed, K * c + k + 1)
                statistics(dve, mem, step, range(4 * c, 4 * c + 4))

        if folding:
            @block.tensor
            def _(pe):
                fold_weights_products(pe, mem, folding)

            @block.scalar
            def _(act):
                fold_weights_copies(act, mem, folding)


H1 = 8
NC1 = S // P


def rms_norm(nc, mem, io, weight):
    with ExitStack() as ctx:
        sb, ps, sem = tools(nc, ctx)
        w_row = sb("w_row", [P, D])
        square, mean, std, inv = (sb(n, [P, NT]) for n in ("square", "mean", "std", "inv"))
        bank = [ps(f"rms_ps{i}", [P, 512]) for i in range(4)]
        loaded, steps, var_in, std_in, normed, turned, copied = (
            sem(n) for n in ("rms_loaded", "rms_steps", "rms_var", "rms_std", "rms_normed", "rms_turned", "rms_copied"))
        y, h_tok, h_t, ident, mv = mem["y"], mem["h_tok"], mem["h_t"], mem["ident"], mem["mv"]
        block = ctx.enter_context(nc.Block())

        @block.sync
        def _(sp):
            sp.dma_start(w_row[:, :], io[weight].rearrange("(a d) -> a d", a=1).to_broadcast([P, D])).then_inc(loaded, 16)
            sp.wait_ge(loaded, 16)

        @block.vector
        def _(dve):
            step = Steps(dve, steps)
            step(dve.tensor_tensor(square[:, :], mv[:, :, 0], mv[:, :, 0], ALU.mult))
            step(dve.tensor_scalar(square[:, :], square[:, :], EPS, None, ALU.add))
            dve.tensor_tensor(mean[:, :], square[:, :], mv[:, :, 1], ALU.add).then_inc(var_in, 1)
            dve.wait_ge(std_in, 1)
            step(dve.reciprocal(inv[:, :], std[:, :]))
            dve.wait_ge(loaded, 16)
            for t in range(NT):
                dve.scalar_tensor_tensor(h_tok[:, t, :], y[:, t, :], inv[:, t:t + 1], w_row[:, :],
                                         ALU.mult, ALU.mult).then_inc(normed, 1)

        @block.scalar
        def _(act):
            act.wait_ge(var_in, 1)
            act.activation(std[:, :], mean[:, :], ACT.Sqrt).then_inc(std_in, 1)
            for c in range(NT // 4):
                act.wait_ge(turned, c + 1)
                act.copy(h_t[:, c * 512:(c + 1) * 512], bank[c][:, :]).then_inc(copied, 1)

        @block.tensor
        def _(pe):
            for t in range(NT):
                pe.wait_ge(normed, t + 1)
                last = pe.transpose(bank[t // 4][:, t % 4 * P:t % 4 * P + P], h_tok[:, t, :], ident[:, :])
                if t % 4 == 3:
                    last.then_inc(turned, 1)


def load_linear_weights(sp, mem, io):
    loaded = mem["linear_in"]
    for n in "qkv":
        sp.dma_start(mem[f"w_{n}"][:, :, :], io["L1_attn_W" + n].rearrange("d (h e) -> d h e", h=H1)).then_inc(loaded, 16)
    sp.dma_start(mem["w_o"][:, :, :], io["L1_attn_Wo"].rearrange("(h e) d -> e h d", h=H1)).then_inc(loaded, 16)
    sp.dma_start(mem["norm_w"][:, :], io["L1_attn_attn_out_norm_w"].rearrange("(d a) -> d a", a=1)).then_inc(loaded, 16)


def weight_folding(mem, sb, ps, sem):
    fold = {n: sem("lw_" + n) for n in ("scaled", "turned", "t_copied", "folded", "f_copied")}
    fold["turned_w"] = sb("turned_w", [P, 2, 3, P])
    fold["turn_ps"] = [ps(f"wturn_ps{i}", [P, 3, P]) for i in range(2)]
    fold["fold_ps"] = [ps(f"fold_ps{i}", [P, 2, D]) for i in range(2)]
    return fold


def scale_output_weights(dve, mem, fold):
    dve.wait_ge(mem["linear_in"], 80)
    w_o = mem["w_o"]
    dve.tensor_scalar(w_o[:, :, :], w_o[:, :, :], mem["norm_w"][:, 0:1], None, ALU.mult).then_inc(fold["scaled"], 1)


def fold_weights_products(pe, mem, fold):
    turn_ps, fold_ps, turned_w = fold["turn_ps"], fold["fold_ps"], fold["turned_w"]
    pe.wait_ge(mem["linear_in"], 80)
    for h in range(H1 + 1):
        if h < H1:
            if h >= 2:
                pe.wait_ge(fold["t_copied"], h - 1)
            for k, n in enumerate("qkv"):
                last = pe.transpose(turn_ps[h % 2][:, k, :], mem[f"w_{n}"][:, h, :], mem["ident"][:, :])
            last.then_inc(fold["turned"], 1)
        if h:
            g = h - 1
            pe.wait_ge(fold["t_copied"], g + 1)
            pe.wait_ge(fold["scaled"], 1)
            if g >= 2:
                pe.wait_ge(fold["f_copied"], g - 1)
            pe.matmul(fold_ps[g % 2][:, 0, :], turned_w[:, g % 2, 0, :], turned_w[:, g % 2, 1, :], start=True, stop=True)
            pe.matmul(fold_ps[g % 2][:, 1, :], turned_w[:, g % 2, 2, :], mem["w_o"][:, g, :],
                      start=True, stop=True).then_inc(fold["folded"], 1)


def fold_weights_copies(act, mem, fold):
    a_w, vm_w = mem["a_w"], mem["vm_w"]
    for h in range(H1 + 1):
        if h < H1:
            act.wait_ge(fold["turned"], h + 1)
            if h >= 2:
                act.wait_ge(fold["folded"], h - 1)
            act.copy(fold["turned_w"][:, h % 2, :, :], fold["turn_ps"][h % 2][:, :, :]).then_inc(fold["t_copied"], 1)
        if h:
            g = h - 1
            act.wait_ge(fold["folded"], g + 1)
            act.copy(a_w[:, g, :], fold["fold_ps"][g % 2][:, 0, :])
            act.copy(vm_w[:, g, 0:D], mem["w_v"][:, g, :])
            act.copy(vm_w[:, g, D:2 * D], fold["fold_ps"][g % 2][:, 1, :]).then_inc(fold["f_copied"], 1)


def linear_attention(nc, mem, io):
    with ExitStack() as ctx:
        sb, ps, sem = tools(nc, ctx)
        chunk_t = [sb(f"chunk_t{i}", [P, P]) for i in range(2)]
        chunk_k = [sb(f"chunk_k{i}", [P, D]) for i in range(2)]
        sums = [sb(f"sums{i}", [P, D]) for i in range(2)]
        query = sb("query", [P, H1, P])
        scores = sb("scores", [P, H1, P])
        mixed = sb("mixed", [P, H1, P])
        causal = sb("causal", [P, P])
        squares = sb("squares", [P, H1, D])
        mean, std, inv = sb("o_mean", [P, 2, H1]), sb("o_std", [P, 2, H1]), sb("o_inv", [P, 2, H1])
        heads = sb("heads", [P, H1, D])
        total = sb("heads_sum", [P, D])
        work = [ps(f"work{i}", [P, 4, P]) for i in range(4)]
        outs = [ps(f"outs{i}", [P, 2, 2 * D]) for i in range(4)]
        loaded, set_up, staged = sem("la_loaded"), sem("la_set"), sem("staged")
        q_done, q_copied, s_done, s_copied = sem("q_done"), sem("q_copied"), sem("s_done"), sem("s_copied")
        m_done, m_copied, g_done, g_copied = sem("m_done"), sem("m_copied"), sem("g_done"), sem("g_copied")
        o_done, squared, steps, root_in, root_out, scaled, y_in = (
            sem(n) for n in ("la_o", "squared", "la_steps", "root_in", "root_out", "la_scaled", "y_in"))
        x, y, h_t, h_tok, a_w, vm_w = (mem[n] for n in ("x_tok", "y", "h_t", "h_tok", "a_w", "vm_w"))
        block = ctx.enter_context(nc.Block())
        HH = H1 // 2

        STEPS = 6

        def summed_at(n):
            return n * STEPS + 1

        @block.sync
        def _(sp):
            sp.dma_start(causal[:, :], io["c_causal"]).then_inc(loaded, 16)
            sp.dma_start(mem["w_gate"][:, :], io["L1_attn_Wgate"]).then_inc(mem["mlp_in"], 16)
            sp.dma_start(mem["w_up"][:, :], io["L1_attn_Wup"]).then_inc(mem["mlp_in"], 16)
            sp.dma_start(mem["w_down"][:, :, :], io["L1_attn_Wdown"].rearrange("(c p) d -> p c d", p=P)).then_inc(mem["mlp_in"], 16)
            load_expert_weights(sp, mem, io, 1)
            sp.wait_ge(loaded, 16)

        @block.gpsimd
        def _(pool):
            for n in range(NT):
                c = n % 2
                if n >= 2:
                    pool.wait_ge(o_done, n - 1)
                pool.tensor_copy(chunk_t[c][:, :], h_t[:, n * P:(n + 1) * P]).then_inc(staged, 1)
                pool.tensor_copy(chunk_k[c][:, :], h_tok[:, n, :]).then_inc(staged, 1)

        @block.tensor
        def _(pe):
            def queries(n):
                for h in range(H1):
                    if h % HH == 0 and n:
                        pe.wait_ge(m_copied, 2 * (n - 1) + h // HH + 1)
                    last = pe.matmul(work[h // HH][:, h % HH, :], a_w[:, h, :], h_t[:, n * P:(n + 1) * P], start=True, stop=True)
                    if h % HH == HH - 1:
                        last.then_inc(q_done, 1)

            def attend(n):
                c = n % 2
                pe.wait_ge(staged, 2 * n + 2)
                for half in range(2):
                    pe.wait_ge(q_copied, 2 * n + half + 1)
                    if n:
                        pe.wait_ge(g_copied, n)
                    pe.matmul(work[2 + half][:, :, :], chunk_t[c][:, :], query[:, half * HH:(half + 1) * HH, :],
                              start=True, stop=True).then_inc(s_done, 1)

            def mix(n):
                c = n % 2
                for half in range(2):
                    pe.wait_ge(s_copied, 2 * n + half + 1)
                    first = n % NC1 == 0
                    last = pe.matmul(work[half][:, :, :], chunk_k[c][:, :], scores[:, half * HH:(half + 1) * HH, :],
                                     start=True, stop=first)
                    if not first:
                        pe.wait_ge(g_copied, n)
                        last = pe.matmul(work[half][:, :, :], sums[(n - 1) % 2][:, :], query[:, half * HH:(half + 1) * HH, :],
                                         start=False, stop=True)
                    last.then_inc(m_done, 1)

            def gather(n):
                pe.wait_ge(s_copied, 2 * n + 1)
                pe.matmul(work[2][:, 0, :], chunk_k[n % 2][:, :], chunk_k[n % 2][:, :], start=True, stop=True).then_inc(g_done, 1)

            def project(n, half):
                for h in range(half * HH, (half + 1) * HH):
                    if h % HH == 0:
                        pe.wait_ge(m_copied, 2 * n + h // HH + 1)
                        if n and half == 0:
                            pe.wait_ge(scaled, n)
                            pe.wait_ge(squared, n)
                    last = pe.matmul(outs[h // 2][:, h % 2, :], mixed[:, h, :], vm_w[:, h, :], start=True, stop=True)
                if half == 1:
                    last.then_inc(o_done, 1)

            for n in range(NT):
                queries(n)
                if n:
                    project(n - 1, 0)
                attend(n)
                if n:
                    project(n - 1, 1)
                gather(n)
                mix(n)
            project(NT - 1, 0)
            project(NT - 1, 1)

        @block.scalar
        def _(act):
            def root(n):
                act.wait_ge(root_in, n + 1)
                act.activation(std[:, n % 2, :], mean[:, n % 2, :], ACT.Sqrt).then_inc(root_out, 1)

            for n in range(NT):
                for half in range(2):
                    act.wait_ge(q_done, 2 * n + half + 1)
                    if n:
                        act.wait_ge(m_done, 2 * (n - 1) + half + 1)
                    act.copy(query[:, half * HH:(half + 1) * HH, :], work[half][:, :, :]).then_inc(q_copied, 1)
                if n:
                    act.wait_ge(o_done, n)
                    if n > 1:
                        act.wait_ge(steps, summed_at(n - 2))
                    for k in range(4):
                        last = act.activation(squares[:, 2 * k:2 * k + 2, :], outs[k][:, :, 0:D], ACT.Square)
                    last.then_inc(squared, 1)
                for half in range(2):
                    act.wait_ge(m_done, 2 * n + half + 1)
                    if n:
                        act.wait_ge(o_done, n)
                    act.copy(mixed[:, half * HH:(half + 1) * HH, :], work[half][:, :, :]).then_inc(m_copied, 1)
                    if n and half == 0:
                        root(n - 1)
            act.wait_ge(o_done, NT)
            act.wait_ge(steps, summed_at(NT - 2))
            for k in range(4):
                last = act.activation(squares[:, 2 * k:2 * k + 2, :], outs[k][:, :, 0:D], ACT.Square)
            last.then_inc(squared, 1)
            root(NT - 1)

        @block.vector
        def _(dve):
            step = Steps(dve, steps)
            dve.wait_ge(loaded, 16)

            def mask(n):
                for half in range(2):
                    dve.wait_ge(s_done, 2 * n + half + 1)
                    if n:
                        dve.wait_ge(m_done, 2 * (n - 1) + half + 1)
                    dve.tensor_tensor(scores[:, half * HH:(half + 1) * HH, :], work[2 + half][:, :, :],
                                      causal[:, :].unsqueeze(1).to_broadcast([P, HH, P]), ALU.mult).then_inc(s_copied, 1)

            def add_up(n):
                dve.wait_ge(g_done, n + 1)
                if n:
                    dve.wait_ge(m_done, 2 * n)
                if n % NC1 == 0:
                    dve.tensor_copy(sums[n % 2][:, :], work[2][:, 0, :]).then_inc(g_copied, 1)
                else:
                    dve.wait_ge(g_copied, n)
                    dve.tensor_tensor(sums[n % 2][:, :], sums[(n - 1) % 2][:, :], work[2][:, 0, :], ALU.add).then_inc(g_copied, 1)

            def finish(n):
                dve.wait_ge(squared, n + 1)
                step(dve.tensor_reduce(mean[:, n % 2, :], squares[:, :, :], AX, ALU.add))
                dve.tensor_scalar(mean[:, n % 2, :], mean[:, n % 2, :], 1.0 / P, EPS, ALU.mult, ALU.add).then_inc(root_in, 1)
                dve.wait_ge(root_out, n + 1)
                step(dve.reciprocal(inv[:, n % 2, :], std[:, n % 2, :]))
                for k in range(4):
                    last = dve.tensor_tensor(heads[:, 2 * k:2 * k + 2, :], outs[k][:, :, D:2 * D],
                                             inv[:, n % 2, 2 * k:2 * k + 2].unsqueeze(2).to_broadcast([P, 2, D]), ALU.mult)
                last.then_inc(scaled, 1)
                dve.wait_ge(scaled, n + 1)
                step(dve.tensor_reduce(total[:, :], heads[:, :, :].rearrange("p h d -> p d h"), AX, ALU.add))
                step(dve.tensor_tensor(y[:, n, :], total[:, :], x[:, n, :], ALU.add))
                statistics(dve, mem, step, [n])

            for n in range(NT):
                mask(n)
                add_up(n)
                if n:
                    finish(n - 1)
            finish(NT - 1)


def gated_mlp(nc, mem, io):
    FC = F0 // P
    with ExitStack() as ctx:
        sb, ps, sem = tools(nc, ctx)
        w_gate, w_up, w_down = mem["w_gate"], mem["w_up"], mem["w_down"]
        acted, hidden = sb("acted1", [P, 2, 512]), sb("hidden1", [P, 2, FC, 512])
        up_ps = [[ps(f"gu_ps{i}{j}", [P, 512]) for j in range(2)] for i in range(2)]
        down_ps = [ps(f"dn_ps{i}", [P, 4, D]) for i in range(2)]
        upped, acted_in, h_in, downed, added = (sem(n) for n in ("m_upped", "m_acted", "m_h", "m_downed", "m_added"))
        stat_steps = sem("stat_steps")
        x, y, h_t = mem["x_tok"], mem["y"], mem["h_t"]
        around = sem("m_around")
        block = ctx.enter_context(nc.Block())
        NB = T // 512

        @block.tensor
        def _(pe):
            pe.wait_ge(mem["mlp_in"], 48)

            def down(b):
                pe.wait_ge(h_in, (b + 1) * FC)
                if b >= 2:
                    pe.wait_ge(added, b - 1)
                for k in range(4):
                    for c in range(FC):
                        last = pe.matmul(down_ps[b % 2][:, k, :], hidden[:, b % 2, c, k * P:(k + 1) * P], w_down[:, c, :],
                                         start=(c == 0), stop=(c == FC - 1))
                last.then_inc(downed, 1)

            for b in range(NB):
                for c in range(FC):
                    n = b * FC + c
                    if n >= 2:
                        pe.wait_ge(h_in, n - 1)
                    for j, w in enumerate((w_gate, w_up)):
                        last = pe.matmul(up_ps[n % 2][j][:, :], w[:, c * P:(c + 1) * P], h_t[:, b * 512:(b + 1) * 512],
                                         start=True, stop=True)
                    last.then_inc(upped, 1)
                if b:
                    down(b - 1)
            down(NB - 1)

        @block.scalar
        def _(act):
            for n in range(NB * FC):
                act.wait_ge(upped, n + 1)
                if n >= 2:
                    act.wait_ge(h_in, n - 1)
                act.activation(acted[:, n % 2, :], up_ps[n % 2][0][:, :], ACT.Silu).then_inc(acted_in, 1)

        @block.vector
        def _(dve):
            step = Steps(dve, stat_steps)
            dve.tensor_tensor(y[:, :, :], y[:, :, :], x[:, :, :], ALU.add).then_inc(around, 1)
            dve.wait_ge(around, 1)
            for b in range(NB + 1):
                if b < NB:
                    for c in range(FC):
                        n = b * FC + c
                        dve.wait_ge(acted_in, n + 1)
                        if b >= 2:
                            dve.wait_ge(downed, b - 1)
                        dve.tensor_tensor(hidden[:, b % 2, c, :], acted[:, n % 2, :], up_ps[n % 2][1][:, :], ALU.mult).then_inc(h_in, 1)
                if b:
                    dve.wait_ge(downed, b)
                    dve.tensor_tensor(y[:, 4 * b - 4:4 * b, :], y[:, 4 * b - 4:4 * b, :], down_ps[(b - 1) % 2][:, :, :], ALU.add).then_inc(added, 1)
                    dve.wait_ge(added, b)
                    statistics(dve, mem, step, range(4 * b - 4, 4 * b))


def two_layers(nc, io, out):
    with ExitStack() as ctx:
        sb, ps, sem = tools(nc, ctx, last=True)
        mem = {
            "x_tok": sb("x_tok", [P, NT, D]), "x_t": sb("x_t", [P, T]), "ident": sb("ident", [P, P]),
            "y": sb("y", [P, NT, D]), "gate": sb("gate", [P, 2, NT]),
            "clamps": sb("clamps", [1, 1], I32),
            "slots0": nc.dram_tensor("slots0", (E * C0, RW), F32, kind="Internal").ap(),
            "slots1": nc.dram_tensor("slots1", (E * C1, RW), F32, kind="Internal").ap(),
            "results0": nc.dram_tensor("results0", (T, D), F32, kind="Internal").ap(),
            "results1": nc.dram_tensor("results1", (2 * T, D), F32, kind="Internal").ap(),
        }
        for i in range(2):
            mem[f"sent{i}"] = sem(f"sent{i}")
            mem[f"returned{i}"] = sem(f"returned{i}")
        dram = {"parts": nc.dram_tensor("parts_dram", (2, 2, NG, NPART, HD, GH, S), BF16, kind="Internal").ap()}
        for i in range(2):
            mem[f"weights_in{i}"] = sem(f"weights_in{i}")
        mem["linear_in"], mem["mlp_in"] = sem("linear_in"), sem("mlp_in")
        mem.update(stats=sb("stats", [P, NT, 6]), mv=sb("mv", [P, NT, 2]))
        with ExitStack() as layer:
            sb, ps, sem = tools(nc, layer)
            mem.update(v_src=sb("v_src", [P, NG, SB, 32]), o_src=sb("o_src", [P, NG, SB, 32]), rest=sb("rest", [P, 2 * S - P]))
            with ExitStack() as scores:
                sb0, _, _ = tools(nc, scores)
                mem["stack0"] = sb0("stack0", [P, 2, 2, GH, S], BF16)
                attention_setup(nc, mem, dram, io)
                attention_scores(nc, mem, dram)
                attention_general(nc, mem, dram, io)
            mem.update(up_w=sb("up_w", [P, 2, E, F0]), down_w=sb("down_w", [P, E * F0 // P, D]))
            mem.update({f"w_{n}": sb(f"w_{n}", [P, H1, P]) for n in "qkvo"}, norm_w=sb("norm_w", [P, 1]))
            attention_output(nc, mem, io)
            layer_norm(nc, mem)
            route(nc, mem, io, 0)
            experts(nc, mem, io, 0)
            mem.update(a_w=sb("a_w", [P, H1, D]), vm_w=sb("vm_w", [P, H1, 2 * D]))
            combine(nc, mem, io, 0)
            mem.update(h_tok=sb("h_tok", [P, NT, D]), h_t=sb("h_t", [P, T]))
            layer_norm(nc, mem, io=io, weight="L1_attn_attn_norm_w")
            with ExitStack() as linear:
                sb, ps, sem = tools(nc, linear)
                mem.update(w_gate=sb("w_gate", [P, F0]), w_up=sb("w_up", [P, F0]), w_down=sb("w_down", [P, F0 // P, D]))
                linear_attention(nc, mem, io)
                rms_norm(nc, mem, io, "L1_attn_mlp_norm_w")
                gated_mlp(nc, mem, io)
            layer_norm(nc, mem)
            route(nc, mem, io, 1)
            experts(nc, mem, io, 1)
            combine(nc, mem, io, 1)
            layer_norm(nc, mem, out)


def kernel(**inputs):
    import numpy as _np
    import concourse.bacc as _bacc
    from concourse import mybir as _mybir
    from concourse.bass_utils import run_bass_kernel_spmd as _run

    nc = _bacc.Bacc("TRN2", target_bir_lowering=False, num_devices=1)
    arrays, io = {}, {}
    for name, value in {**inputs, **host_constants()}.items():
        a = _np.ascontiguousarray(value)
        arrays[f"in_{name}_dram"] = a
        io[name] = nc.dram_tensor(f"in_{name}_dram", a.shape, _mybir.dt.from_np(a.dtype), kind="ExternalInput").ap()
    out = nc.dram_tensor("out_0_dram", (B, S, D), _mybir.dt.float32, kind="ExternalOutput").ap()
    two_layers(nc, io, out)
    r = _run(nc, [arrays], core_ids=[0])
    return r.results[0]["out_0_dram"]
```
